# Optimizing a Trainium2 kernel written in Bass

```python
import numpy as np
import jax
import jax.numpy as jnp

def _softmax(x, axis=-1):
    return jax.nn.softmax(x, axis=axis)

def _gelu(x):
    return jax.nn.gelu(x, approximate=True)

def _silu(x):
    return jax.nn.silu(x)

def _sigmoid(x):
    return jax.nn.sigmoid(x)

def _layernorm(x, axis=-1, eps=1e-05):
    m = jnp.mean(x, axis=axis, keepdims=True)
    v = jnp.var(x, axis=axis, keepdims=True)
    return (x - m) / jnp.sqrt(v + eps)

def _scatter_add(tgt, idx, src, axis=0):
    return tgt.at[idx].add(src)

def _segment_sum(src, seg, n):
    return jax.ops.segment_sum(src, seg, n)
kernel_name = 'mk_conv_attn_hybrid_d2_conv_nhwc256_r2_bd814d'

def setup_inputs(seed: int=0):
    np.random.seed(seed)
    _w = jnp.asarray

    def _rec_inputs():
        import jax
        import jax.numpy as jnp
        _gk = jax.random.key(seed)
        x = -0.0002928 + 1 * jax.random.normal(jax.random.fold_in(_gk, 1), (4, 32, 32, 128), jnp.float32)
        return x
    x = _rec_inputs()

    def _L0_conv_setup():
        import jax, jax.numpy as jnp
        import numpy as np
        MAX_LR = 0.1

        def _l2norm(x):
            n = jnp.linalg.norm(x, axis=-1, keepdims=True)
            return x / jnp.maximum(n, 1e-12)

        def _mlp(params, h):
            for w1, w2 in params:
                h = h + jax.nn.gelu(h @ w1) @ w2
            return h
        key = jax.random.key(seed)
        ks = jax.random.split(key, 11)
        B, T, C, D, DE = (4, 32, 32, 128, 256)
        s = 0.02
        return {'x': jax.random.normal(ks[0], (B, T, C, D), jnp.float32), 'Wq': jax.random.normal(ks[1], (D, D), jnp.float32) * s, 'Wk': jax.random.normal(ks[2], (D, D), jnp.float32) * s, 'Wv': jax.random.normal(ks[3], (D, D), jnp.float32) * s, 'w_lr': jax.random.normal(ks[4], (D,), jnp.float32) * s, 'w_forget': jax.random.normal(ks[5], (D,), jnp.float32) * s, 'w_eta': jax.random.normal(ks[6], (D,), jnp.float32) * s, 'w1_0': jax.random.normal(ks[7], (D, DE), jnp.float32) * s, 'w2_0': jax.random.normal(ks[8], (DE, D), jnp.float32) * s, 'w1_1': jax.random.normal(ks[9], (D, DE), jnp.float32) * s, 'w2_1': jax.random.normal(ks[10], (DE, D), jnp.float32) * s}
    _L0_conv_all = _L0_conv_setup()
    _L0_conv_in = {k: v for k, v in _L0_conv_all.items() if k in ('Wq', 'Wk', 'Wv', 'w_lr', 'w_forget', 'w_eta', 'w1_0', 'w2_0', 'w1_1', 'w2_1')}
    del _L0_conv_all

    def _L1_attn_setup():
        import jax, jax.numpy as jnp
        import numpy as np
        UNITS = 32
        ATT_WIDTH = 32
        key = jax.random.key(seed)
        ks = jax.random.split(key, 4)
        B, T, F = (4, 512, 128)
        x = jax.random.normal(ks[0], (B, T, F), dtype=jnp.float32)
        Wt = jax.random.normal(ks[1], (F, UNITS), dtype=jnp.float32) * (1.0 / np.sqrt(F))
        Wx = jax.random.normal(ks[2], (F, UNITS), dtype=jnp.float32) * (1.0 / np.sqrt(F))
        bh = jnp.zeros((UNITS,), dtype=jnp.float32)
        Wa = jax.random.normal(ks[3], (UNITS, 1), dtype=jnp.float32) * (1.0 / np.sqrt(UNITS))
        ba = jnp.zeros((1,), dtype=jnp.float32)
        return {'x': x, 'Wt': Wt, 'Wx': Wx, 'bh': bh, 'Wa': Wa, 'ba': ba}
    _L1_attn_all = _L1_attn_setup()
    _L1_attn_in = {k: v for k, v in _L1_attn_all.items() if k in ('Wt', 'Wx', 'bh', 'Wa', 'ba')}
    del _L1_attn_all

    def _L1_ffn_setup():
        import jax, jax.numpy as jnp
        import numpy as np
        TOP_K = 2
        LN_EPS = 1e-05
        key = jax.random.key(seed)
        ks = jax.random.split(key, 8)
        B, S, D, E, H = (16, 512, 128, 8, 512)
        x = jax.random.normal(ks[0], (B, S, D), dtype=jnp.float32)
        Wr = jax.random.normal(ks[1], (D, E), dtype=jnp.float32) * 0.1
        br = jnp.zeros((E,), dtype=jnp.float32)
        ln_g = jnp.ones((E, D), dtype=jnp.float32)
        ln_b = jnp.zeros((E, D), dtype=jnp.float32)
        W1 = jax.random.normal(ks[2], (E, D, H), dtype=jnp.float32) * (1.0 / np.sqrt(D))
        b1 = jnp.zeros((E, H), dtype=jnp.float32)
        W2 = jax.random.normal(ks[3], (E, H, D), dtype=jnp.float32) * (1.0 / np.sqrt(H))
        b2 = jnp.zeros((E, D), dtype=jnp.float32)
        return {'x': x, 'Wr': Wr, 'br': br, 'ln_g': ln_g, 'ln_b': ln_b, 'W1': W1, 'b1': b1, 'W2': W2, 'b2': b2}
    _L1_ffn_all = _L1_ffn_setup()
    _L1_ffn_in = {k: v for k, v in _L1_ffn_all.items() if k in ('Wr', 'br', 'ln_g', 'ln_b', 'W1', 'b1', 'W2', 'b2')}
    del _L1_ffn_all
    return {'x': x, 'L0_conv_Wq': _L0_conv_in['Wq'], 'L0_conv_Wk': _L0_conv_in['Wk'], 'L0_conv_Wv': _L0_conv_in['Wv'], 'L0_conv_w_lr': _L0_conv_in['w_lr'], 'L0_conv_w_forget': _L0_conv_in['w_forget'], 'L0_conv_w_eta': _L0_conv_in['w_eta'], 'L0_conv_w1_0': _L0_conv_in['w1_0'], 'L0_conv_w2_0': _L0_conv_in['w2_0'], 'L0_conv_w1_1': _L0_conv_in['w1_1'], 'L0_conv_w2_1': _L0_conv_in['w2_1'], 'L1_attn_Wt': _L1_attn_in['Wt'], 'L1_attn_Wx': _L1_attn_in['Wx'], 'L1_attn_bh': _L1_attn_in['bh'], 'L1_attn_Wa': _L1_attn_in['Wa'], 'L1_attn_ba': _L1_attn_in['ba'], 'L1_ffn_Wr': _L1_ffn_in['Wr'], 'L1_ffn_br': _L1_ffn_in['br'], 'L1_ffn_ln_g': _L1_ffn_in['ln_g'], 'L1_ffn_ln_b': _L1_ffn_in['ln_b'], 'L1_ffn_W1': _L1_ffn_in['W1'], 'L1_ffn_b1': _L1_ffn_in['b1'], 'L1_ffn_W2': _L1_ffn_in['W2'], 'L1_ffn_b2': _L1_ffn_in['b2']}

def reference(x, L0_conv_Wq, L0_conv_Wk, L0_conv_Wv, L0_conv_w_lr, L0_conv_w_forget, L0_conv_w_eta, L0_conv_w1_0, L0_conv_w2_0, L0_conv_w1_1, L0_conv_w2_1, L1_attn_Wt, L1_attn_Wx, L1_attn_bh, L1_attn_Wa, L1_attn_ba, L1_ffn_Wr, L1_ffn_br, L1_ffn_ln_g, L1_ffn_ln_b, L1_ffn_W1, L1_ffn_b1, L1_ffn_W2, L1_ffn_b2):
    import jax
    import jax.numpy as jnp

    def _L0_conv_ref(x, Wq, Wk, Wv, w_lr, w_forget, w_eta, w1_0, w2_0, w1_1, w2_1):
        import jax, jax.numpy as jnp
        import numpy as np
        MAX_LR = 0.1

        def _l2norm(x):
            n = jnp.linalg.norm(x, axis=-1, keepdims=True)
            return x / jnp.maximum(n, 1e-12)

        def _mlp(params, h):
            for w1, w2 in params:
                h = h + jax.nn.gelu(h @ w1) @ w2
            return h
        B = x.shape[0]
        mem0 = ((w1_0, w2_0), (w1_1, w2_1))
        params0 = jax.tree.map(lambda p: jnp.broadcast_to(p, (B,) + p.shape), mem0)
        mom0 = jax.tree.map(jnp.zeros_like, params0)
        q = _l2norm(jnp.einsum('btcd,de->btce', x, Wq))

        def assoc_loss(p, k, v):
            pred = _mlp(p, k)
            return jnp.mean((pred - v) ** 2)
        grad_fn = jax.vmap(jax.grad(assoc_loss))

        def step(carry, x_t):
            params, mom = carry
            k = _l2norm(x_t @ Wk)
            v = x_t @ Wv
            lr = MAX_LR * jnp.mean(jax.nn.sigmoid(x_t @ w_lr), axis=1)
            forget = jnp.mean(jax.nn.sigmoid(x_t @ w_forget), axis=1)
            eta = jnp.mean(jax.nn.sigmoid(x_t @ w_eta), axis=1)
            g = grad_fn(params, k, v)

            def upd_m(m, gg):
                sh = (B,) + (1,) * (m.ndim - 1)
                return eta.reshape(sh) * m - lr.reshape(sh) * gg
            new_mom = jax.tree.map(upd_m, mom, g)

            def upd_p(p, nm):
                sh = (B,) + (1,) * (p.ndim - 1)
                return p * (1.0 - forget.reshape(sh)) + nm
            new_params = jax.tree.map(upd_p, params, new_mom)
            return ((new_params, new_mom), None)
        (paramsT, momT), _ = jax.lax.scan(step, (params0, mom0), jnp.swapaxes(x, 0, 1))
        final = jax.tree.map(lambda p: jnp.mean(p, axis=0), paramsT)
        return _mlp(final, q)

    def _L1_attn_ref(x, Wt, Wx, bh, Wa, ba):
        import jax, jax.numpy as jnp
        import numpy as np
        UNITS = 32
        ATT_WIDTH = 32
        q = jnp.einsum('btf,fu->btu', x, Wt)[:, :, None, :]
        k = jnp.einsum('bsf,fu->bsu', x, Wx)[:, None, :, :]
        h = jnp.tanh(q + k + bh)
        e = jnp.einsum('btsu,uo->bts', h, Wa) + ba[0]
        T = x.shape[1]
        idx = jnp.arange(T)
        lower = idx - ATT_WIDTH // 2
        band = (lower[:, None] <= idx[None, :]) & (idx[None, :] < lower[:, None] + ATT_WIDTH)
        e = e - 10000.0 * (1.0 - band.astype(e.dtype))
        a = jax.nn.softmax(e, axis=-1)
        v = jnp.einsum('bts,bsf->btf', a, x)
        return v

    def _L1_ffn_ref(x, Wr, br, ln_g, ln_b, W1, b1, W2, b2):
        import jax, jax.numpy as jnp
        import numpy as np
        TOP_K = 2
        LN_EPS = 1e-05
        B, S, D = x.shape
        N = B * S
        xt = x.reshape(N, D)
        logits = xt @ Wr + br
        probs = jax.nn.softmax(logits, axis=-1)
        top_p, top_idx = jax.lax.top_k(probs, TOP_K)
        weights = top_p / top_p.sum(axis=-1, keepdims=True)
        mu = xt.mean(axis=-1, keepdims=True)
        var = ((xt - mu) ** 2).mean(axis=-1, keepdims=True)
        xn = (xt - mu) * jax.lax.rsqrt(var + LN_EPS)
        xe = xn[None, :, :] * ln_g[:, None, :] + ln_b[:, None, :]
        h = jax.nn.gelu(jnp.einsum('end,edh->enh', xe, W1) + b1[:, None, :], approximate=False)
        y = jnp.einsum('enh,ehd->end', h, W2) + b2[:, None, :]
        y_tok = jnp.transpose(y, (1, 0, 2))
        sel = jnp.take_along_axis(y_tok, top_idx[:, :, None], axis=1)
        out = (weights[:, :, None] * sel).sum(axis=1)
        return out.reshape(B, S, D)

    def _gn(v, G=32, eps=1e-05):
        B_, H_, W_, C_ = v.shape
        g = v.reshape(B_, H_, W_, G, C_ // G)
        m = jnp.mean(g, axis=(1, 2, 4), keepdims=True)
        s = jnp.var(g, axis=(1, 2, 4), keepdims=True)
        return ((g - m) / jnp.sqrt(s + eps)).reshape(v.shape)

    def _ln_c(v, eps=1e-06):
        m = jnp.mean(v, axis=-1, keepdims=True)
        s = jnp.var(v, axis=-1, keepdims=True)
        return (v - m) / jnp.sqrt(s + eps)

    def _ln_t(v, eps=1e-05):
        m = jnp.mean(v, axis=-1, keepdims=True)
        s = jnp.var(v, axis=-1, keepdims=True)
        return (v - m) / jnp.sqrt(s + eps)

    def _to_tokens(v):
        B_, H_, W_, C_ = v.shape
        return v.reshape(B_, H_ * W_, C_)

    def _from_tokens(t, like):
        return t.reshape(like.shape)
    x = x + _L0_conv_ref(_gn(x), L0_conv_Wq, L0_conv_Wk, L0_conv_Wv, L0_conv_w_lr, L0_conv_w_forget, L0_conv_w_eta, L0_conv_w1_0, L0_conv_w2_0, L0_conv_w1_1, L0_conv_w2_1)
    t = _to_tokens(x)
    t = t + _L1_attn_ref(_ln_t(t), L1_attn_Wt, L1_attn_Wx, L1_attn_bh, L1_attn_Wa, L1_attn_ba)
    t = t + _L1_ffn_ref(_ln_t(t), L1_ffn_Wr, L1_ffn_br, L1_ffn_ln_g, L1_ffn_ln_b, L1_ffn_W1, L1_ffn_b1, L1_ffn_W2, L1_ffn_b2)
    x = _from_tokens(t, x)
    return x

_drawn_inputs = setup_inputs


def setup_inputs(seed=0):
    import zlib

    import numpy as np

    out = dict(_drawn_inputs(seed))
    spreads = {'L1_attn_bh': (0.0, 0.298),
     'L1_ffn_br': (0.0, 0.1),
     'L1_ffn_ln_g': (1.0, 0.2),
     'L1_ffn_ln_b': (0.0, 0.1),
     'L1_ffn_b1': (0.0, 0.1),
     'L1_ffn_b2': (0.0, 0.1)}
    factors = {}
    for name, (base, spread) in spreads.items():
        noise = np.random.default_rng([zlib.crc32(name.encode()), seed]).standard_normal(out[name].shape)
        drawn = base * np.exp(spread * noise) if base else spread * noise
        out[name] = jnp.asarray(drawn.astype(out[name].dtype))
    for name, factor in factors.items():
        out[name] = (out[name] * factor).astype(out[name].dtype)
    return out
```

```python
from contextlib import ExitStack

import concourse.bass as bass
from concourse import mybir

F32 = mybir.dt.float32
ALU = mybir.AluOpType
ACT = mybir.ActivationFunctionType
AX = mybir.AxisListType

B, T, C, D = 4, 32, 32, 128
S = T * C
NT = B * S // 128
DE = 256
NC_E = DE // 128
U = 32
WIN = 32
E = 8
H = 512
MAX_LR = 0.1
GELU_C = 0.7978845608028654
GELU_A = 0.044715
C_ID, C_MEAN, C_GRP, C_BAND, C_EDGE, C_RANK, C_SEL = 0, 128, 256, 384, 544, 800, 808
C_ALL = C_SEL + 512


PARAMS = ("21", "11", "10", "20")


def prepare(nc, st, sb, inp, consts):
    sem = lambda name: st.enter_context(nc.semaphore(name))
    with ExitStack() as ctx:
        xs = ctx.enter_context(nc.sbuf_tensor("xs", [128, T, 128], F32))
        xf = ctx.enter_context(nc.sbuf_tensor("xf", [128, T, B, C], F32))
        xg = ctx.enter_context(nc.sbuf_tensor("xg", [128, T, B, C], F32))
        proj = ctx.enter_context(nc.sbuf_tensor("proj", [128, T, 259], F32))
        wcat = ctx.enter_context(nc.sbuf_tensor("wcat", [128, 259], F32))
        wv = ctx.enter_context(nc.sbuf_tensor("wv", [128, 128], F32))
        bst = ctx.enter_context(nc.sbuf_tensor("bst", [128, B, 2, 6], F32))
        mv = ctx.enter_context(nc.sbuf_tensor("mv", [128, B, 2], F32))
        me = ctx.enter_context(nc.sbuf_tensor("me", [128, B, 2], F32))
        ge = ctx.enter_context(nc.sbuf_tensor("ge", [128, B, 2], F32))
        gvar = ctx.enter_context(nc.sbuf_tensor("gvar", [128, B], F32))
        gsd = ctx.enter_context(nc.sbuf_tensor("gsd", [128, B], F32))
        grs = ctx.enter_context(nc.sbuf_tensor("grs", [128, B], F32))
        gneg = ctx.enter_context(nc.sbuf_tensor("gneg", [128, B], F32))
        ss = ctx.enter_context(nc.sbuf_tensor("ss", [128, T, 2], F32))
        sn = ctx.enter_context(nc.sbuf_tensor("sn", [128, T, 2], F32))
        sig = ctx.enter_context(nc.sbuf_tensor("sig", [128, 3, T], F32))
        ps = [ctx.enter_context(nc.psum_tensor(f"pp{i}", [128, 512], F32)) for i in range(8)]

        load_x, load_c, load_w, load_p = sem("load_x"), sem("load_c"), sem("load_w"), sem("load_p")
        xt_done, xf_ready = sem("xt_done"), sem("xf_ready")
        gn_chain, gn_sum, gn_sqrt = sem("gn_chain"), sem("gn_sum"), sem("gn_sqrt")
        xg_ready, proj_done, proj_ready = sem("xg_ready"), sem("proj_done"), sem("proj_ready")
        v_done, v_ready = sem("v_done"), sem("v_ready")
        sq_ready, nrm_chain, nrm_sqrt = sem("sq_ready"), sem("nrm_chain"), sem("nrm_sqrt")
        qk_normed, qk_turned, qk_ready = sem("qk_normed"), sem("qk_turned"), sem("qk_ready")
        sig_ready, gate_done = sem("sig_ready"), sem("gate_done")
        zeroed, gn_step, q_copied = sem("mom_zeroed"), sem("gn_step"), sem("q_copied")

        with nc.Block() as block:
            @block.sync
            def _(sp):
                xv = inp["x"].rearrange("b t c d -> b c t d")
                for b in range(B):
                    sp.dma_start(xs[32 * b:32 * b + 32, :, :], xv[b]).then_inc(load_x, 16)
                sp.dma_start(sb["cst"][:, :], consts).then_inc(load_c, 16)
                sp.dma_start(sb["x1"][:, :, :], inp["x"].rearrange("b t c d -> (b t c) d").rearrange("(n p) d -> p n d", p=128)).then_inc(sb["load_xb"], 16)

            @block.gpsimd
            def _(pool):
                for k in ("w10", "w20", "w11", "w21"):
                    nc.gpsimd.memset(sb["m" + k[1:]][:, :, :], 0.0).then_inc(zeroed, 1)

            @block.scalar
            def _(act):
                for a, k in ((0, "L0_conv_Wq"), (128, "L0_conv_Wk")):
                    act.dma_start(wcat[:, a:a + 128], inp[k]).then_inc(load_w, 16)
                for i, k in enumerate(("L0_conv_w_lr", "L0_conv_w_forget", "L0_conv_w_eta")):
                    act.dma_start(wcat[:, 256 + i:257 + i], inp[k].rearrange("(d a) -> d a", a=1)).then_inc(load_w, 16)
                act.dma_start(wv[:, :], inp["L0_conv_Wv"]).then_inc(load_w, 16)
                for b in range(B):
                    for k, src in (("w10", "L0_conv_w1_0"), ("w11", "L0_conv_w1_1")):
                        act.dma_start(sb[k][:, b, :], inp[src]).then_inc(load_p, 16)
                    for k, src in (("w20", "L0_conv_w2_0"), ("w21", "L0_conv_w2_1")):
                        act.dma_start(sb[k][:, b, :].rearrange("p (h d) -> p h d", h=2),
                                      inp[src].rearrange("(h p) d -> p h d", p=128)).then_inc(load_p, 16)
                for g in range(T // 4):
                    act.wait_ge(xt_done, g + 1)
                    nc.scalar.copy(xf[:, 4 * g:4 * g + 4, :, :].rearrange("p t b c -> p (t b c)"), ps[g % 4][:, :]).then_inc(xf_ready, 1)
                act.wait_ge(gn_chain, 5)
                nc.scalar.activation(gsd[:, :], gvar[:, :], ACT.Sqrt).then_inc(gn_sqrt, 1)
                for t in range(T):
                    act.wait_ge(proj_done, t + 1)
                    nc.scalar.copy(proj[:, t, :], ps[t % 4][:, 0:259]).then_inc(proj_ready, 1)
                for g in range(T // 4):
                    act.wait_ge(v_done, g + 1)
                    nc.scalar.copy(sb["vf"][:, 4 * g:4 * g + 4, :].rearrange("p t n -> p (t n)"), ps[4 + g % 4][:, :]).then_inc(v_ready, 1)
                act.wait_ge(proj_ready, T)
                nc.scalar.activation(xs[:, :, :], proj[:, :, 0:128], ACT.Square).then_inc(sq_ready, 1)
                act.wait_ge(xg_ready, B)
                nc.scalar.activation(xf[:, :, :, :].rearrange("p t b c -> p t (b c)"), proj[:, :, 128:256], ACT.Square).then_inc(sq_ready, 1)
                act.wait_ge(nrm_chain, 1)
                nc.scalar.activation(sn[:, :, :], ss[:, :, :], ACT.Sqrt).then_inc(nrm_sqrt, 1)
                nc.scalar.activation(sig[:, :, :], proj[:, :, 256:259].rearrange("p t g -> p g t"), ACT.Sigmoid).then_inc(sig_ready, 1)
                for g in range(T // 4):
                    act.wait_ge(qk_turned, 2 * g + 2)
                    nc.scalar.copy(sb["kf"][:, 4 * g:4 * g + 4, :].rearrange("p t n -> p (t n)"), ps[4 + g % 2][:, :]).then_inc(qk_ready, 1)
                act.wait_ge(zeroed, 4)
                act.wait_ge(load_p, 16 * 16)

            @block.tensor
            def _(pe):
                cst = sb["cst"]
                ident = cst[:, C_ID:C_ID + 128]
                pe.wait_ge(load_c, 16)
                pe.wait_ge(load_x, 64)
                for t in range(T):
                    if t % 4 == 0 and t >= 16:
                        pe.wait_ge(xf_ready, t // 4 - 3)
                    i = nc.tensor.transpose(ps[(t // 4) % 4][:, 128 * (t % 4):128 * (t % 4) + 128], xs[:, t, :], ident)
                    if t % 4 == 3:
                        i.then_inc(xt_done, 1)
                pe.wait_ge(gn_chain, 3)
                pe.wait_ge(xf_ready, T // 4)
                nc.tensor.matmul(ps[7][:, 0:2 * B], cst[:, C_GRP:C_GRP + 128],
                                 me[:, :, :].rearrange("p b s -> p (b s)"), start=True, stop=True).then_inc(gn_sum, 1)
                pe.wait_ge(xg_ready, B)
                pe.wait_ge(load_w, 16 * 6)
                for t in range(T):
                    if t >= 4:
                        pe.wait_ge(proj_ready, t - 3)
                    nc.tensor.matmul(ps[t % 4][:, 0:259], xg[:, t, :, :].rearrange("p b c -> p (b c)"), wcat[:, :],
                                     start=True, stop=True).then_inc(proj_done, 1)
                for g in range(T // 4):
                    if g >= 4:
                        pe.wait_ge(v_ready, g - 3)
                    nc.tensor.matmul(ps[4 + g % 4][:, :], wv[:, :], xg[:, 4 * g:4 * g + 4, :, :].rearrange("p t b c -> p (t b c)"),
                                     start=True, stop=True).then_inc(v_done, 1)
                pe.wait_ge(sig_ready, 1)
                pe.wait_ge(v_ready, T // 4)
                for b in range(B):
                    nc.tensor.matmul(ps[6][:, 64 * b:64 * b + 64], cst[:, C_SEL + 128 * b:C_SEL + 128 * b + 128],
                                     sig[:, 1:3, :].rearrange("p g t -> p (g t)"), start=True, stop=True)
                nc.tensor.matmul(ps[6][:, 256:256 + T], cst[:, C_MEAN:C_MEAN + 128], sig[:, 0, :],
                                 start=True, stop=True).then_inc(gate_done, 1)
                pe.wait_ge(qk_normed, 1)
                for g in range(T // 4):
                    if g >= 2:
                        pe.wait_ge(qk_ready, g - 1)
                    for j in range(2):
                        if g >= 2:
                            pe.wait_ge(q_copied, g - 1)
                        for i in range(4):
                            t = 4 * g + i
                            src = proj[:, t, 0:128] if j == 0 else sb["ktok"][:, t, :]
                            m = nc.tensor.transpose(ps[(0 if j == 0 else 4) + g % 2][:, 128 * i:128 * i + 128], src, ident)
                        m.then_inc(qk_turned, 1)

            @block.vector
            def _(dve):
                dve.wait_ge(load_c, 16)
                dve.wait_ge(xf_ready, T // 4)
                for b in range(B):
                    for h in range(2):
                        i = nc.vector.bn_stats(bst[:, b, h, :], xf[:, 16 * h:16 * h + 16, b, :])
                i.then_inc(gn_chain, 1)
                dve.wait_ge(gn_chain, 1)
                for b in range(B):
                    i = nc.vector.bn_aggr(mv[:, b, :], bst[:, b, :, :].rearrange("p h s -> p (h s)"))
                i.then_inc(gn_chain, 1)
                dve.wait_ge(gn_chain, 2)
                nc.vector.tensor_copy(me[:, :, 0], mv[:, :, 0])
                for b in range(B):
                    i = nc.vector.scalar_tensor_tensor(out=me[:, b, 1:2], in0=mv[:, b, 0:1], scalar=mv[:, b, 0:1],
                                                       in1=mv[:, b, 1:2], op0=ALU.mult, op1=ALU.add)
                i.then_inc(gn_chain, 1)
                dve.wait_ge(gn_sum, 1)
                nc.vector.tensor_copy(ge[:, :, :].rearrange("p b s -> p (b s)"), ps[7][:, 0:2 * B]).then_inc(gn_chain, 1)
                dve.wait_ge(gn_chain, 4)
                for b in range(B):
                    i = nc.vector.tensor_scalar(gvar[:, b:b + 1], ge[:, b, 0:1], ge[:, b, 0:1], -1.0, ALU.mult, ALU.mult)
                i.then_inc(gn_step, 1)
                dve.wait_ge(gn_step, 1)
                nc.vector.scalar_tensor_tensor(out=gvar[:, :], in0=gvar[:, :], scalar=1e-5, in1=ge[:, :, 1],
                                               op0=ALU.add, op1=ALU.add).then_inc(gn_chain, 1)
                dve.wait_ge(gn_sqrt, 1)
                nc.vector.reciprocal(grs[:, :], gsd[:, :]).then_inc(gn_step, 1)
                dve.wait_ge(gn_step, 2)
                nc.vector.scalar_tensor_tensor(out=gneg[:, :], in0=ge[:, :, 0], scalar=-1.0, in1=grs[:, :],
                                               op0=ALU.mult, op1=ALU.mult).then_inc(gn_step, 1)
                dve.wait_ge(gn_step, 3)
                for b in range(B):
                    nc.vector.tensor_scalar(xg[:, :, b, :], xf[:, :, b, :], grs[:, b:b + 1], gneg[:, b:b + 1],
                                            ALU.mult, ALU.add).then_inc(xg_ready, 1)
                dve.wait_ge(sq_ready, 2)
                nc.vector.tensor_reduce(ss[:, :, 0:1], xs[:, :, :], AX.X, ALU.add)
                nc.vector.tensor_reduce(ss[:, :, 1:2], xf[:, :, :, :].rearrange("p t b c -> p t (b c)"), AX.X, ALU.add).then_inc(nrm_chain, 1)
                dve.wait_ge(nrm_sqrt, 1)
                nc.vector.tensor_scalar(sn[:, :, :], sn[:, :, :], 1e-12, None, ALU.max).then_inc(nrm_chain, 1)
                dve.wait_ge(nrm_chain, 2)
                nc.vector.reciprocal(sn[:, :, :], sn[:, :, :]).then_inc(nrm_chain, 1)
                dve.wait_ge(nrm_chain, 3)
                rn = sn[:, :, :]
                nc.vector.tensor_tensor(proj[:, :, 0:128], proj[:, :, 0:128], rn[:, :, 0:1].to_broadcast([128, T, 128]), ALU.mult)
                nc.vector.tensor_tensor(sb["ktok"][:, :, :], proj[:, :, 128:256], rn[:, :, 1:2].to_broadcast([128, T, 128]), ALU.mult).then_inc(qk_normed, 1)
                dve.wait_ge(gate_done, 1)
                gates = ps[6][:, 0:256].rearrange("p (b g t) -> p b g t", b=B, g=2)
                for b in range(B):
                    nc.vector.tensor_copy(sb["coef"][:, :, b], gates[:, b, 1, :])
                    nc.vector.tensor_scalar(sb["coef"][:, :, 4 + b], gates[:, b, 0, :], -1.0, 1.0, ALU.mult, ALU.add)
                nc.vector.tensor_scalar(sb["coef"][:, :, 8], ps[6][:, 256:256 + T], -MAX_LR * 2.0 / (C * D), None, ALU.mult).then_inc(nrm_chain, 1)
                for g in range(T // 4):
                    dve.wait_ge(qk_turned, 2 * g + 1)
                    nc.vector.tensor_copy(sb["qf"][:, :, 4 * g:4 * g + 4, :].rearrange("p b t c -> p t b c"),
                                          ps[g % 2][:, :].rearrange("p (t b c) -> p t b c", t=4, b=B)).then_inc(q_copied, 1)


def learn(nc, st, sb):
    sem = lambda name: st.enter_context(nc.semaphore(name))
    with ExitStack() as ctx:
        def buf(name, shape):
            return ctx.enter_context(nc.sbuf_tensor("l_" + name, shape, F32))

        W, M = {k: sb["w" + k] for k in PARAMS}, {k: sb["m" + k] for k in PARAMS}
        WT = {k: buf("wt" + k, [128, B, 256]) for k in ("21", "11", "20")}
        kt, vt, ktok = buf("kt", [128, 128]), buf("vt", [128, 128]), buf("ktok", [128, 128])
        cf = buf("cf", [128, 9])
        g = [buf("g0", [128, 256]), buf("g1", [128, 256])]
        h1, hv, dp, dh1 = (buf(n, [128, 128]) for n in ("h1", "hv", "dp", "dh1"))
        da = [buf("da0", [128, 256]), buf("da1", [128, 256])]
        a = [buf("a0", [128, 256]), buf("a1", [128, 256])]
        asq = [buf("asq0", [128, 256]), buf("asq1", [128, 256])]
        u = [buf("u0", [128, 256]), buf("u1", [128, 256])]
        th = [buf("th0", [128, 256]), buf("th1", [128, 256])]
        th2 = [buf("ths0", [128, 256]), buf("ths1", [128, 256])]
        dd = [buf("dd0", [128, 256]), buf("dd1", [128, 256])]
        gp = [buf("gp0", [128, 256]), buf("gp1", [128, 256])]
        g_tok = [buf("gt0", [128, 256]), buf("gt1", [128, 256])]
        h1_tok, dp_tok, dh1_tok = (buf(n, [128, 128]) for n in ("h1t", "dpt", "dh1t"))
        da_tok = [buf("dat0", [128, 256]), buf("dat1", [128, 256])]

        def bank(name, n=1):
            return ctx.enter_context(nc.psum_tensor("lp_" + name, [128, 512 * n], F32))

        ps_a, ps_b, ps_h, ps_t = bank("a"), bank("b"), bank("h"), bank("t")
        ps_g = [bank("g0", 2), bank("g1", 2)]

        mm_done = sem("l_mm")
        turned, turned_read = sem("l_turned"), sem("l_turned_read")
        grad_done = sem("l_grad")
        wt_done, wt_ready = sem("l_wt"), sem("l_wt_ready")
        gelu_ready, pre_ready = sem("l_gelu"), sem("l_pre")
        tanh_ready, u_ready = [sem("l_tanh0"), sem("l_tanh1")], [sem("l_u0"), sem("l_u1")]
        poly_ready, gp_ready = [sem("l_poly0"), sem("l_poly1")], [sem("l_gp0"), sem("l_gp1")]
        step_in, cf_in = sem("l_step_in"), sem("l_cf_in")
        chain = sem("l_chain")
        mom_ready = sem("l_mom")
        w_ready = {k: sem("l_w" + k) for k in PARAMS}
        A0, H1, A1, Y, DG1, DH1, DG0 = range(1, 8)
        TG0, TH1, TG1, TDP, TDA1, TDH1, TDA0 = range(1, 8)
        G21, G11, G10, G20 = range(1, 5)
        X21, X11, X20 = range(1, 4)
        K_H1, K_HV, K_DP, K_DA1, K_DH1, K_DA0 = range(1, 7)

        def grad_bank(b):
            return ps_g[b // 2][:, 512 * (b % 2):512 * (b % 2) + 256]

        def rows(b):
            return slice(32 * b, 32 * b + 32)

        def gelu_slope(ns, eng, t, l):
            eng.wait_ge(pre_ready, t * 4 + 2 * l + 2)
            ns.tensor_scalar(u[l][:, :], asq[l][:, :], GELU_A, 1.0, ALU.mult, ALU.add).then_inc(poly_ready[l], 1)
            eng.wait_ge(poly_ready[l], t * 5 + 1)
            ns.tensor_tensor(u[l][:, :], u[l][:, :], a[l][:, :], ALU.mult).then_inc(u_ready[l], 1)
            ns.tensor_scalar(dd[l][:, :], asq[l][:, :], 1.5 * GELU_C * GELU_A, 0.5 * GELU_C, ALU.mult, ALU.add).then_inc(poly_ready[l], 1)
            eng.wait_ge(poly_ready[l], t * 5 + 2)
            ns.tensor_tensor(dd[l][:, :], dd[l][:, :], a[l][:, :], ALU.mult).then_inc(poly_ready[l], 1)
            eng.wait_ge(tanh_ready[l], t * 2 + 2)
            eng.wait_ge(poly_ready[l], t * 5 + 3)
            ns.tensor_scalar(th2[l][:, :], th2[l][:, :], -1.0, 1.0, ALU.mult, ALU.add).then_inc(poly_ready[l], 1)
            eng.wait_ge(poly_ready[l], t * 5 + 4)
            ns.tensor_tensor(dd[l][:, :], dd[l][:, :], th2[l][:, :], ALU.mult)
            ns.tensor_scalar(th[l][:, :], th[l][:, :], 0.5, None, ALU.mult).then_inc(poly_ready[l], 1)
            eng.wait_ge(poly_ready[l], t * 5 + 5)
            ns.tensor_tensor(gp[l][:, :], dd[l][:, :], th[l][:, :], ALU.add).then_inc(gp_ready[l], 1)

        with nc.Block() as block:
            @block.gpsimd
            def _(pool):
                with pool.Fori(0, T) as t:
                    pool.wait_ge(chain, t * 6)
                    nc.gpsimd.tensor_copy(kt[:, :], sb["kf"][:, bass.ds(t, 1), :].rearrange("p a n -> p (a n)")).then_inc(step_in, 1)
                    nc.gpsimd.tensor_copy(vt[:, :], sb["vf"][:, bass.ds(t, 1), :].rearrange("p a n -> p (a n)")).then_inc(step_in, 1)
                    pool.wait_ge(grad_done, t * 16)
                    nc.gpsimd.tensor_copy(ktok[:, :], sb["ktok"][:, bass.ds(t, 1), :].rearrange("p a n -> p (a n)")).then_inc(step_in, 1)

            @block.scalar
            def _(act):
                def hidden(t, l, p):
                    act.wait_ge(mm_done, t * 7 + (A0, A1)[l])
                    nc.scalar.activation(g[l][:, :], p[:, 0:256], ACT.Gelu_apprx_tanh).then_inc(gelu_ready, 1)
                    nc.scalar.copy(a[l][:, :], p[:, 0:256]).then_inc(pre_ready, 1)
                    nc.scalar.activation(asq[l][:, :], p[:, 0:256], ACT.Square).then_inc(pre_ready, 1)

                def slope(t, l):
                    act.wait_ge(u_ready[l], t + 1)
                    nc.scalar.activation(th[l][:, :], u[l][:, :], ACT.Tanh, scale=GELU_C).then_inc(tanh_ready[l], 1)
                    act.wait_ge(tanh_ready[l], t * 2 + 1)
                    nc.scalar.activation(th2[l][:, :], th[l][:, :], ACT.Square).then_inc(tanh_ready[l], 1)

                def tok(t, n, dst, width, scaled):
                    act.wait_ge(turned, t * 7 + n)
                    if scaled:
                        nc.scalar.mul(dst, ps_t[:, 0:width], cf[:, 8:9]).then_inc(turned_read, 1)
                    else:
                        nc.scalar.copy(dst, ps_t[:, 0:width]).then_inc(turned_read, 1)

                def wt(t, n, k):
                    act.wait_ge(wt_done, t * 3 + n)
                    nc.scalar.copy(WT[k][:, :, :].rearrange("p b n -> p (b n)"), ps_g[(n + 1) % 2][:, :]).then_inc(wt_ready, 1)

                with act.Fori(0, T) as t:
                    hidden(t, 0, ps_a)
                    wt(t, X21, "21")
                    tok(t, TG0, g_tok[0][:, :], 256, False)
                    slope(t, 0)
                    hidden(t, 1, ps_b)
                    act.wait_ge(w_ready["20"], t * 4)
                    nc.scalar.copy(cf[:, :], sb["coef"][:, bass.ds(t, 1), :].rearrange("p a n -> p (a n)")).then_inc(cf_in, 1)
                    act.wait_ge(cf_in, t + 1)
                    wt(t, X11, "11")
                    slope(t, 1)
                    tok(t, TH1, h1_tok[:, :], 128, False)
                    wt(t, X20, "20")
                    tok(t, TG1, g_tok[1][:, :], 256, False)
                    tok(t, TDP, dp_tok[:, :], 128, True)
                    tok(t, TDA1, da_tok[1][:, :], 256, True)
                    tok(t, TDH1, dh1_tok[:, :], 128, True)
                    tok(t, TDA0, da_tok[0][:, :], 256, True)

            @block.vector
            def _(dve):
                def update(t, k, n):
                    for b in range(B):
                        dve.wait_ge(grad_done, t * 16 + 4 * (n - 1) + b + 1)
                        nc.vector.scalar_tensor_tensor(out=M[k][:, b, :], in0=M[k][:, b, :], scalar=cf[:, b:b + 1],
                                                           in1=grad_bank(b),
                                                           op0=ALU.mult, op1=ALU.add).then_inc(mom_ready, 1)
                    for b in range(B):
                        dve.wait_ge(mom_ready, t * 16 + 4 * (n - 1) + b + 1)
                        nc.vector.scalar_tensor_tensor(out=W[k][:, b, :], in0=W[k][:, b, :], scalar=cf[:, 4 + b:5 + b],
                                                       in1=M[k][:, b, :], op0=ALU.mult, op1=ALU.add).then_inc(w_ready[k], 1)

                def slope_times(t, l, p, n, kc):
                    dve.wait_ge(mm_done, t * 7 + n)
                    dve.wait_ge(gp_ready[l], t + 1)
                    nc.vector.scalar_tensor_tensor(out=da[l][:, :], in0=gp[l][:, :], scalar=0.5, in1=p[:, 0:256],
                                                   op0=ALU.add, op1=ALU.mult).then_inc(chain, 1)

                with dve.Fori(0, T) as t:
                    gelu_slope(nc.vector, dve, t, 0)
                    dve.wait_ge(mm_done, t * 7 + H1)
                    dve.wait_ge(step_in, t * 3 + 2)
                    nc.vector.tensor_tensor(h1[:, :], ps_h[:, 0:128], kt[:, :], ALU.add).then_inc(chain, 1)
                    dve.wait_ge(chain, t * 6 + K_H1)
                    nc.vector.tensor_tensor(hv[:, :], h1[:, :], vt[:, :], ALU.subtract).then_inc(chain, 1)
                    gelu_slope(nc.vector, dve, t, 1)
                    dve.wait_ge(mm_done, t * 7 + Y)
                    dve.wait_ge(chain, t * 6 + K_HV)
                    nc.vector.tensor_tensor(dp[:, :], ps_h[:, 0:128], hv[:, :], ALU.add).then_inc(chain, 1)
                    slope_times(t, 1, ps_a, DG1, K_DA1)
                    dve.wait_ge(mm_done, t * 7 + DH1)
                    dve.wait_ge(chain, t * 6 + K_DP)
                    nc.vector.tensor_tensor(dh1[:, :], ps_h[:, 0:128], dp[:, :], ALU.add).then_inc(chain, 1)
                    slope_times(t, 0, ps_b, DG0, K_DA0)
                    dve.wait_ge(cf_in, t + 1)
                    update(t, "21", G21)
                    update(t, "11", G11)
                    update(t, "10", G10)
                    update(t, "20", G20)

            @block.tensor
            def _(pe):
                ident = sb["cst"][:, C_ID:C_ID + 128]

                def up(p, w, x, n):
                    for b in range(B):
                        for h in range(2):
                            i = nc.tensor.matmul(p[:, 128 * h + 32 * b:128 * h + 32 * b + 32], w[:, b, 128 * h:128 * h + 128],
                                                 x[:, rows(b)], start=True, stop=True)
                    i.then_inc(mm_done, 1)

                def down(p, w, x, n):
                    for b in range(B):
                        for h in range(2):
                            i = nc.tensor.matmul(p[:, rows(b)], w[:, b, 128 * h:128 * h + 128],
                                                 x[:, 128 * h + 32 * b:128 * h + 32 * b + 32], start=h == 0, stop=h == 1)
                    i.then_inc(mm_done, 1)

                def turn(t, n, x, width):
                    pe.wait_ge(turned_read, t * 7 + n - 1)
                    for h in range(width // 128):
                        i = nc.tensor.transpose(ps_t[:, 128 * h:128 * h + 128], x[:, 128 * h:128 * h + 128], ident)
                    i.then_inc(turned, 1)

                def turn_w(t, n, k, before):
                    pe.wait_ge(w_ready[k], t * 4)
                    before()
                    for b in range(B):
                        for h in range(2):
                            i = nc.tensor.transpose(ps_g[(n + 1) % 2][:, 256 * b + 128 * h:256 * b + 128 * h + 128],
                                                    W[k][:, b, 128 * h:128 * h + 128], ident)
                    i.then_inc(wt_done, 1)

                def grad(t, n, x_tok, y_tok, chunks, tok_read):
                    pe.wait_ge(turned_read, t * 7 + tok_read)
                    for b in range(B):
                        if n > 1:
                            pe.wait_ge(mom_ready, t * 16 + 4 * (n - 2) + b + 1)
                        if chunks == 1:
                            i = nc.tensor.matmul(grad_bank(b), x_tok[rows(b), :], y_tok[rows(b), :], start=True, stop=True)
                        else:
                            for h in range(2):
                                i = nc.tensor.matmul(grad_bank(b)[:, 128 * h:128 * h + 128],
                                                     x_tok[rows(b), 128 * h:128 * h + 128], y_tok[rows(b), :], start=True, stop=True)
                        i.then_inc(grad_done, 1)

                with pe.Fori(0, T) as t:
                    pe.wait_ge(w_ready["10"], t * 4)
                    pe.wait_ge(step_in, t * 3 + 1)
                    up(ps_a, W["10"], kt, A0)
                    turn_w(t, X21, "21", lambda: pe.wait_ge(mom_ready, t * 16))
                    pe.wait_ge(w_ready["20"], t * 4)
                    pe.wait_ge(gelu_ready, t * 2 + 1)
                    down(ps_h, W["20"], g[0], H1)
                    turn(t, TG0, g[0], 256)
                    turn_w(t, X11, "11", lambda: pe.wait_ge(mom_ready, t * 16))
                    pe.wait_ge(chain, t * 6 + K_H1)
                    up(ps_b, W["11"], h1, A1)
                    turn(t, TH1, h1, 128)
                    turn_w(t, X20, "20", lambda: pe.wait_ge(wt_ready, t * 3 + X21))
                    pe.wait_ge(gelu_ready, t * 2 + 2)
                    down(ps_h, W["21"], g[1], Y)
                    turn(t, TG1, g[1], 256)
                    pe.wait_ge(chain, t * 6 + K_DP)
                    pe.wait_ge(pre_ready, t * 4 + 2)
                    pe.wait_ge(wt_ready, t * 3 + X21)
                    up(ps_a, WT["21"], dp, DG1)
                    turn(t, TDP, dp, 128)
                    pe.wait_ge(chain, t * 6 + K_DA1)
                    pe.wait_ge(wt_ready, t * 3 + X11)
                    down(ps_h, WT["11"], da[1], DH1)
                    turn(t, TDA1, da[1], 256)
                    pe.wait_ge(wt_ready, t * 3 + X20)
                    grad(t, G21, g_tok[1], dp_tok, 2, TDP)
                    pe.wait_ge(chain, t * 6 + K_DH1)
                    pe.wait_ge(pre_ready, t * 4 + 4)
                    up(ps_b, WT["20"], dh1, DG0)
                    turn(t, TDH1, dh1, 128)
                    grad(t, G11, h1_tok, da_tok[1], 1, TDA1)
                    pe.wait_ge(chain, t * 6 + K_DA0)
                    turn(t, TDA0, da[0], 256)
                    pe.wait_ge(step_in, t * 3 + 3)
                    grad(t, G10, ktok, da_tok[0], 1, TDA0)
                    grad(t, G20, g_tok[0], dh1_tok, 2, TDH1)


def read_out(nc, st, sb, inp):
    sem = lambda name: st.enter_context(nc.semaphore(name))
    with ExitStack() as ctx:
        def buf(name, shape):
            return ctx.enter_context(nc.sbuf_tensor("r_" + name, shape, F32))

        wf = {k: buf("wf" + k, [128, 256]) for k in PARAMS}
        g0, g1 = ([buf(f"g{l}{i}", [128, 1024]) for i in range(2)] for l in range(2))
        h1 = [buf(f"h1{i}", [128, 512]) for i in range(4)]
        z = [buf(f"z{i}", [128, 512]) for i in range(2)]
        bst = buf("bst", [128, NT, 6])
        ps_a0, ps_a1 = (ctx.enter_context(nc.psum_tensor("rp_a" + n, [128, 1024], F32)) for n in "01")
        ps_h, ps_z, ps_x = (ctx.enter_context(nc.psum_tensor("rp_" + n, [128, 512], F32)) for n in "hzx")
        wf_sum, wf_ready = sem("r_wfsum"), sem("r_wf")
        a0_done, h_done, a1_done, z_done, x_done = (sem("r_" + n) for n in ("a0", "h", "a1", "z", "x"))
        g0_ready, g1_ready, h_ready, z_ready = (sem("r_" + n) for n in ("g0r", "g1r", "hr", "zr"))
        x1_ready, st_ready, mv_ready = sem("r_x1"), sem("r_st"), sem("r_mv")
        N = B * S // 512
        order = ("10", "20", "11", "21")

        def q(n):
            return sb["qf"][:, n // 2, 16 * (n % 2):16 * (n % 2) + 16, :].rearrange("p t c -> p (t c)")

        with nc.Block() as block:
            @block.scalar
            def _(act):
                for k in range(N + 2):
                    if k < N:
                        act.wait_ge(a0_done, k + 1)
                        if k >= 2:
                            act.wait_ge(h_done, k - 1)
                        nc.scalar.activation(g0[k % 2][:, :], ps_a0[:, :], ACT.Gelu_apprx_tanh).then_inc(g0_ready, 1)
                    if k >= 2:
                        n = k - 2
                        act.wait_ge(a1_done, n + 1)
                        if n >= 2:
                            act.wait_ge(z_done, n - 1)
                        nc.scalar.activation(g1[n % 2][:, :], ps_a1[:, :], ACT.Gelu_apprx_tanh).then_inc(g1_ready, 1)

            @block.tensor
            def _(pe):
                ident = sb["cst"][:, C_ID:C_ID + 128]
                for k in range(N + 4):
                    if k < N:
                        pe.wait_ge(wf_ready, 1)
                        if k >= 1:
                            pe.wait_ge(g0_ready, k)
                        for h in range(2):
                            i = nc.tensor.matmul(ps_a0[:, 512 * h:512 * h + 512], wf["10"][:, 128 * h:128 * h + 128], q(k),
                                                 start=True, stop=True)
                        i.then_inc(a0_done, 1)
                    if 1 <= k <= N:
                        n = k - 1
                        pe.wait_ge(wf_ready, 2)
                        pe.wait_ge(g0_ready, n + 1)
                        if n >= 1:
                            pe.wait_ge(h_ready, n)
                        for h in range(2):
                            i = nc.tensor.matmul(ps_h[:, :], wf["20"][:, 128 * h:128 * h + 128], g0[n % 2][:, 512 * h:512 * h + 512],
                                                 start=h == 0, stop=h == 1)
                        i.then_inc(h_done, 1)
                    if 2 <= k <= N + 1:
                        n = k - 2
                        pe.wait_ge(wf_ready, 3)
                        pe.wait_ge(h_ready, n + 1)
                        if n >= 1:
                            pe.wait_ge(g1_ready, n)
                        for h in range(2):
                            i = nc.tensor.matmul(ps_a1[:, 512 * h:512 * h + 512], wf["11"][:, 128 * h:128 * h + 128], h1[n % 4][:, :],
                                                 start=True, stop=True)
                        i.then_inc(a1_done, 1)
                    if 3 <= k <= N + 2:
                        n = k - 3
                        pe.wait_ge(wf_ready, 4)
                        pe.wait_ge(g1_ready, n + 1)
                        if n >= 1:
                            pe.wait_ge(z_ready, n)
                        for h in range(2):
                            i = nc.tensor.matmul(ps_z[:, :], wf["21"][:, 128 * h:128 * h + 128], g1[n % 2][:, 512 * h:512 * h + 512],
                                                 start=h == 0, stop=h == 1)
                        i.then_inc(z_done, 1)
                    if 4 <= k:
                        n = k - 4
                        pe.wait_ge(z_ready, n + 1)
                        if n >= 1:
                            pe.wait_ge(x1_ready, n)
                        for i in range(4):
                            m = nc.tensor.transpose(ps_x[:, 128 * i:128 * i + 128], z[n % 2][:, 128 * i:128 * i + 128], ident)
                        m.then_inc(x_done, 1)

            @block.vector
            def _(dve):
                for i, k in enumerate(order):
                    nc.vector.tensor_reduce(wf[k][:, :], sb["w" + k][:, :, :].rearrange("p b n -> p n b"), AX.X, ALU.add).then_inc(wf_sum, 1)
                    dve.wait_ge(wf_sum, i + 1)
                    nc.vector.tensor_scalar(wf[k][:, :], wf[k][:, :], 1.0 / B, None, ALU.mult).then_inc(wf_ready, 1)
                for k in range(1, N + 5):
                    if k <= N:
                        n = k - 1
                        dve.wait_ge(h_done, n + 1)
                        if n >= 4:
                            dve.wait_ge(a1_done, n - 3)
                            dve.wait_ge(z_ready, n - 3)
                        nc.vector.tensor_tensor(h1[n % 4][:, :], ps_h[:, :], q(n), ALU.add).then_inc(h_ready, 1)
                    if 3 <= k <= N + 2:
                        n = k - 3
                        dve.wait_ge(z_done, n + 1)
                        dve.wait_ge(h_ready, n + 1)
                        if n >= 2:
                            dve.wait_ge(x_done, n - 1)
                        nc.vector.tensor_tensor(z[n % 2][:, :], ps_z[:, :], h1[n % 4][:, :], ALU.add).then_inc(z_ready, 1)
                    if 4 <= k <= N + 3:
                        n = k - 4
                        dve.wait_ge(x_done, n + 1)
                        dve.wait_ge(sb["load_xb"], 16)
                        x1 = sb["x1"][:, 4 * n:4 * n + 4, :].rearrange("p t f -> p (t f)")
                        nc.vector.tensor_tensor(x1, ps_x[:, :], x1, ALU.add).then_inc(x1_ready, 1)
                    if 5 <= k:
                        n = k - 5
                        dve.wait_ge(x1_ready, n + 1)
                        for i in range(4):
                            m = nc.vector.bn_stats(bst[:, 4 * n + i, :], sb["x1"][:, 4 * n + i, :])
                        m.then_inc(st_ready, 1)
                        dve.wait_ge(st_ready, n + 1)
                        for i in range(4):
                            m = nc.vector.bn_aggr(sb["mv"][:, 4 * n + i, :], bst[:, 4 * n + i, :])
                        m.then_inc(mv_ready, 1)


def attend(nc, st, sb, inp):
    sem = lambda name: st.enter_context(nc.semaphore(name))
    HALF = WIN // 2
    QL, QN = WIN - 1, (WIN - 1) + S + WIN
    R = 6
    SPAN = S + WIN
    NTB = S // 128
    with ExitStack() as ctx:
        def buf(name, shape):
            return ctx.enter_context(nc.sbuf_tensor("t_" + name, shape, F32))

        xl = buf("xl", [128, NT, 128])
        xlf = buf("xlf", [128, NT * 128])
        xsh = buf("xsh", [128, B, NTB + 1, 128])
        wt, wx = buf("wt", [128, U]), buf("wx", [128, U])
        wa, bh, ba = buf("wa", [128, B]), buf("bh", [128, 1]), buf("ba", [128, 1])
        qp, kp = buf("qp", [128, QN]), buf("kp", [128, SPAN])
        hs = [buf(f"h{i}", [128, SPAN]) for i in range(R)]
        e = buf("e", [128, NTB, B, WIN])
        mx = buf("mx", [128, NTB * B])
        am = [buf(f"am{i}", [128, B, 160]) for i in range(2)]
        at1 = [buf(f"at1{i}", [128, 512]) for i in range(2)]
        at2 = [buf(f"at2{i}", [32, 512]) for i in range(2)]
        std, rstd = buf("std", [128, NT]), buf("rstd", [128, NT])
        bst = buf("bst", [128, NT, 6])
        ps = [ctx.enter_context(nc.psum_tensor(f"tp{i}", [128, 512], F32)) for i in range(6)]
        ps_e = ctx.enter_context(nc.psum_tensor("tp_e", [128, 1024], F32))

        load, load_wa, shifted = sem("t_load"), sem("t_loadwa"), sem("t_shift")
        cleared, wa_clear = sem("t_cleared"), sem("t_waclear")
        ve, std_ready, rstd_ready, xl_ready = sem("t_ve"), sem("t_std"), sem("t_rstd"), sem("t_xl")
        xl_turned, xlf_ready = sem("t_turn"), sem("t_xlf")
        qk_done, qk_ready = sem("t_qk"), sem("t_qkr")
        sum_ready = [sem("t_sumv"), sem("t_sump")]
        tanh_ready, e_done = sem("t_tanh"), sem("t_edone")
        soft, exp_ready = sem("t_soft"), sem("t_exp")
        am_ready, at_done, at_ready, v_done = sem("t_am"), sem("t_at"), sem("t_atr"), sem("t_v")
        x2_ready, st_ready, mv_ready = sem("t_x2"), sem("t_st"), sem("t_mv")

        def starts(j):
            s0 = j if j < HALF else j - WIN
            return s0, s0 - (HALF - 1)

        def on_pool(j):
            return j % 3 == 2

        def nth(j):
            return sum(on_pool(i) == on_pool(j) for i in range(j + 1))

        def add(ns, eng, j):
            if j >= R:
                eng.wait_ge(e_done, j - R + 1)
            s0, t0 = starts(j)
            nc_out = hs[j % R][:, :].rearrange("p (g i) -> p g i", i=WIN)
            qv = qp[:, QL + t0:QL + t0 + SPAN].rearrange("p (g i) -> p g i", i=WIN)
            k0 = HALF + s0
            kv = kp[:, k0:k0 + SPAN - WIN + 1:WIN].rearrange("p (g a) -> p g a", a=1).to_broadcast([128, SPAN // WIN, WIN])
            ns.tensor_tensor(nc_out, qv, kv, ALU.add).then_inc(sum_ready[on_pool(j)], 1)

        with nc.Block() as block:
            @block.sync
            def _(sp):
                sp.dma_start(wt[:, :], inp["L1_attn_Wt"]).then_inc(load, 16)
                sp.dma_start(wx[:, :], inp["L1_attn_Wx"]).then_inc(load, 16)
                for b in range(B):
                    sp.dma_start(bh[32 * b:32 * b + 32, :], inp["L1_attn_bh"].rearrange("(u a) -> u a", a=1)).then_inc(load, 16)
                sp.dma_start(ba[:, :], inp["L1_attn_ba"].partition_broadcast(128)).then_inc(load, 16)
                sp.wait_ge(wa_clear, 1)
                for b in range(B):
                    sp.dma_start(wa[32 * b:32 * b + 32, b:b + 1], inp["L1_attn_Wa"]).then_inc(load_wa, 16)
                sp.wait_ge(cleared, 2)
                for b in range(B):
                    sp.wait_ge(xl_ready, 8 * b + 8)
                    sp.dma_start(xsh[HALF:128, b, 0:NTB, :], xl[0:128 - HALF, 8 * b:8 * b + 8, :]).then_inc(shifted, 16)
                    sp.dma_start(xsh[0:HALF, b, 1:NTB + 1, :], xl[128 - HALF:128, 8 * b:8 * b + 8, :]).then_inc(shifted, 16)

            @block.gpsimd
            def _(pool):
                nc.gpsimd.memset(wa[:, :], 0.0).then_inc(wa_clear, 1)
                nc.gpsimd.memset(xsh[:, :, 0, :], 0.0).then_inc(cleared, 1)
                nc.gpsimd.memset(xsh[:, :, NTB, :], 0.0).then_inc(cleared, 1)
                nc.gpsimd.memset(qp[:, :], 0.0).then_inc(cleared, 1)
                nc.gpsimd.memset(kp[:, :], 0.0).then_inc(cleared, 1)
                pool.wait_ge(qk_ready, 2)
                for j in range(WIN):
                    if on_pool(j):
                        add(nc.gpsimd, pool, j)

            @block.scalar
            def _(act):
                act.wait_ge(ve, 1)
                nc.scalar.activation(std[:, :], std[:, :], ACT.Sqrt).then_inc(std_ready, 1)
                for g in range(NT // 4):
                    act.wait_ge(xl_turned, g + 1)
                    nc.scalar.copy(xlf[:, 512 * g:512 * g + 512], ps[g % 2][:, :]).then_inc(xlf_ready, 1)
                act.wait_ge(cleared, 4)
                act.wait_ge(load, 16 * 7)
                for h in range(2):
                    act.wait_ge(qk_done, 2 * h + 1)
                    nc.scalar.activation(qp[:, QL + 512 * h:QL + 512 * h + 512], ps[2 + h][:, :], ACT.Identity, bias=bh[:, 0:1])
                    act.wait_ge(qk_done, 2 * h + 2)
                    nc.scalar.copy(kp[:, HALF + 512 * h:HALF + 512 * h + 512], ps[4 + h][:, :]).then_inc(qk_ready, 1)
                for j in range(WIN):
                    act.wait_ge(sum_ready[on_pool(j)], nth(j))
                    t0 = -starts(j)[1]
                    nc.scalar.activation(hs[j % R][:, t0:t0 + S], hs[j % R][:, t0:t0 + S], ACT.Tanh).then_inc(tanh_ready, 1)
                act.wait_ge(soft, 3)
                nc.scalar.activation(e[:, :, :, :], e[:, :, :, :], ACT.Exp).then_inc(exp_ready, 1)
                for n in range(NTB):
                    act.wait_ge(at_done, n + 1)
                    if n >= 2:
                        act.wait_ge(v_done, n - 1)
                    nc.scalar.copy(at1[n % 2][:, :], ps[n % 2][:, :])
                    nc.scalar.copy(at2[n % 2][:, :], ps[2 + n % 2][0:32, :]).then_inc(at_ready, 1)

            @block.tensor
            def _(pe):
                ident = sb["cst"][:, C_ID:C_ID + 128]
                for g in range(NT // 4):
                    pe.wait_ge(xl_ready, 4 * g + 4)
                    if g >= 2:
                        pe.wait_ge(xlf_ready, g - 1)
                    for i in range(4):
                        m = nc.tensor.transpose(ps[g % 2][:, 128 * i:128 * i + 128], xl[:, 4 * g + i, :], ident)
                    m.then_inc(xl_turned, 1)
                pe.wait_ge(load, 16 * 7)
                pe.wait_ge(xlf_ready, NT // 4)
                for h in range(2):
                    for w, o in ((wt, 2), (wx, 4)):
                        for b in range(B):
                            m = nc.tensor.matmul(ps[o + h][32 * b:32 * b + 32, :], w[:, :], xlf[:, 1024 * b + 512 * h:1024 * b + 512 * h + 512],
                                                 start=True, stop=True)
                        m.then_inc(qk_done, 1)
                pe.wait_ge(load_wa, 16 * B)
                for j in range(WIN):
                    pe.wait_ge(tanh_ready, j + 1)
                    t0 = -starts(j)[1]
                    jj = (j + HALF) % WIN
                    for n in range(NTB):
                        m = nc.tensor.matmul(ps_e[:, 128 * n + jj:128 * n + jj + 3 * WIN + 1:WIN], hs[j % R][:, t0 + 128 * n:t0 + 128 * n + 128],
                                             wa[:, :], start=True, stop=True)
                    m.then_inc(e_done, 1)
                pe.wait_ge(shifted, 16 * 2 * B)
                pe.wait_ge(qk_ready, 2)
                for k in range(NTB + 1):
                    if k < NTB:
                        n = k
                        pe.wait_ge(am_ready, n + 1)
                        if n >= 2:
                            pe.wait_ge(at_ready, n - 1)
                        for b in range(B):
                            nc.tensor.transpose(ps[n % 2][:, 128 * b:128 * b + 128], am[n % 2][:, b, 0:128], ident)
                        for b in range(B):
                            m = nc.tensor.transpose(ps[2 + n % 2][0:32, 128 * b:128 * b + 128], am[n % 2][:, b, 128:160], ident)
                        m.then_inc(at_done, 1)
                    if k >= 1:
                        n = k - 1
                        pe.wait_ge(at_ready, n + 1)
                        if n >= 2:
                            pe.wait_ge(x2_ready, n - 1)
                        for b in range(B):
                            nc.tensor.matmul(ps[4 + n % 2][:, 128 * b:128 * b + 128], at1[n % 2][:, 128 * b:128 * b + 128],
                                             xsh[:, b, n, :], start=True, stop=False)
                            m = nc.tensor.matmul(ps[4 + n % 2][:, 128 * b:128 * b + 128], at2[n % 2][:, 128 * b:128 * b + 128],
                                                 xsh[0:32, b, n + 1, :], start=False, stop=True)
                        m.then_inc(v_done, 1)

            @block.vector
            def _(dve):
                mv = sb["mv"]
                nc.vector.tensor_scalar(std[:, :], mv[:, :, 1], 1e-5, None, ALU.add).then_inc(ve, 1)
                dve.wait_ge(std_ready, 1)
                nc.vector.reciprocal(rstd[:, :], std[:, :]).then_inc(rstd_ready, 1)
                dve.wait_ge(rstd_ready, 1)
                for n in range(NT):
                    nc.vector.tensor_scalar(xl[:, n, :], sb["x1"][:, n, :], mv[:, n, 0:1], rstd[:, n:n + 1],
                                            ALU.subtract, ALU.mult).then_inc(xl_ready, 1)
                dve.wait_ge(qk_ready, 2)
                for j in range(WIN):
                    if not on_pool(j):
                        add(nc.vector, dve, j)
                dve.wait_ge(e_done, WIN)
                edge = sb["cst"][:, C_EDGE:C_EDGE + NTB * WIN].rearrange("p (n j) -> p n j", j=WIN)
                pe_ = ps_e[:, :].rearrange("p (n b j) -> p n b j", n=NTB, b=B)
                for b in range(B):
                    m = nc.vector.scalar_tensor_tensor(out=e[:, :, b, :], in0=pe_[:, :, b, :], scalar=ba[:, 0:1], in1=edge,
                                                       op0=ALU.add, op1=ALU.add)
                m.then_inc(soft, 1)
                dve.wait_ge(soft, 1)
                er = e[:, :, :, :].rearrange("p n b j -> p (n b) j")
                bc = mx[:, :].rearrange("p (n a) -> p n a", a=1).to_broadcast([128, NTB * B, WIN])
                nc.vector.tensor_reduce(mx[:, :], er, AX.X, ALU.max).then_inc(soft, 1)
                dve.wait_ge(soft, 2)
                nc.vector.tensor_tensor(er, er, bc, ALU.subtract).then_inc(soft, 1)
                dve.wait_ge(exp_ready, 1)
                nc.vector.tensor_reduce(mx[:, :], er, AX.X, ALU.add).then_inc(soft, 1)
                dve.wait_ge(soft, 4)
                nc.vector.reciprocal(mx[:, :], mx[:, :]).then_inc(soft, 1)
                dve.wait_ge(soft, 5)
                nc.vector.tensor_tensor(er, er, bc, ALU.mult).then_inc(soft, 1)
                dve.wait_ge(soft, 6)
                band = sb["cst"][:, C_BAND:C_BAND + 160].rearrange("p (r j) -> p r j", j=WIN)
                x1v = sb["x1"][:, :, :].rearrange("p (b n) f -> p b n f", b=B)
                for k in range(NTB + 2):
                    if k < NTB:
                        if k >= 2:
                            dve.wait_ge(at_done, k - 1)
                        for b in range(B):
                            m = nc.vector.tensor_tensor(am[k % 2][:, b, :].rearrange("p (r j) -> p r j", j=WIN),
                                                        e[:, k, b:b + 1, :].to_broadcast([128, 5, WIN]), band, ALU.mult)
                        m.then_inc(am_ready, 1)
                    if k >= 2:
                        n = k - 2
                        dve.wait_ge(v_done, n + 1)
                        nc.vector.tensor_tensor(x1v[:, :, n, :], ps[4 + n % 2][:, :].rearrange("p (b f) -> p b f", b=B),
                                                x1v[:, :, n, :], ALU.add).then_inc(x2_ready, 1)
                dve.wait_ge(x2_ready, NTB)
                for n in range(NT):
                    m = nc.vector.bn_stats(bst[:, n, :], sb["x1"][:, n, :])
                m.then_inc(st_ready, 1)
                dve.wait_ge(st_ready, 1)
                for n in range(NT):
                    m = nc.vector.bn_aggr(mv[:, n, :], bst[:, n, :])
                m.then_inc(mv_ready, 1)


def experts(nc, st, sb, inp, out):
    sem = lambda name: st.enter_context(nc.semaphore(name))
    NH = H // 128
    with ExitStack() as ctx:
        def buf(name, shape):
            return ctx.enter_context(nc.sbuf_tensor("f_" + name, shape, F32))

        std, r1, v2, s2, r12 = (buf(n, [128, NT]) for n in ("std", "r1", "v2", "s2", "r12"))
        xn = buf("xn", [128, 4, 128])
        xnf = buf("xnf", [128, NT * 128])
        wr, br = buf("wr", [128, E]), buf("br", [128, E])
        lg, key, sel, ex, lg2 = (buf(n, [128, NT, E]) for n in ("lg", "key", "sel", "ex", "lg2"))
        m1, mk = buf("m1", [128, NT]), buf("mk", [128, NT])
        wt8 = buf("wt8", [E, NT * 128])
        b2 = buf("b2", [E, 128])
        NROW = 2 * E + E * NH
        rowp, colp = buf("rowp", [NROW, 128]), buf("colp", [128, NROW])
        lng, lnb, b1t = colp[:, 0:E], colp[:, E:2 * E], colp[:, 2 * E:NROW].rearrange("p (e h) -> p e h", h=NH)
        w1 = [buf(f"w1{i}", [128, H]) for i in range(2)]
        w1g = [buf(f"w1g{i}", [128, H]) for i in range(2)]
        w2 = [buf(f"w2{i}", [128, NH, 128]) for i in range(2)]
        hb = [buf(f"hb{i}", [128, NH]) for i in range(2)]
        hh = [buf(f"hh{i}", [128, NH, 512]) for i in range(2)]
        ps_h = [ctx.enter_context(nc.psum_tensor(f"fp_h{i}", [128, 512], F32)) for i in range(4)]
        ps_y = [ctx.enter_context(nc.psum_tensor(f"fp_y{i}", [128, 512], F32)) for i in range(2)]
        ps_r, ps_b = (ctx.enter_context(nc.psum_tensor("fp_" + n, [128, 512], F32)) for n in "rb")
        load, load_w, stored = sem("f_load"), [sem("f_lw0"), sem("f_lw1")], sem("f_out")
        nrm, sq1 = sem("f_nrm"), sem("f_sq")
        xn_ready, xn_turned, xnf_ready = sem("f_xn"), sem("f_turn"), sem("f_xnf")
        lg_done, rt, ex_ready = sem("f_lg"), sem("f_rt"), sem("f_ex")
        wt_done, wt_ready, bt_done, bt_used = sem("f_wt"), sem("f_wtr"), sem("f_bt"), sem("f_btu")
        w_ready, hb_done, hb_ready = sem("f_w"), sem("f_hbd"), sem("f_hb")
        h_done, h_ready, y_done, y_used = sem("f_h"), sem("f_hr"), sem("f_y"), sem("f_yu")
        col_done, col_ready = sem("f_cold"), sem("f_col")
        NCH = S * B // 512
        NN = E * NCH

        with nc.Block() as block:
            @block.sync
            def _(sp):
                sp.dma_start(wr[:, :], inp["L1_ffn_Wr"]).then_inc(load, 16)
                sp.dma_start(br[:, :], inp["L1_ffn_br"].partition_broadcast(128)).then_inc(load, 16)
                sp.dma_start(b2[:, :], inp["L1_ffn_b2"]).then_inc(load, 16)
                sp.dma_start(rowp[0:E, :], inp["L1_ffn_ln_g"]).then_inc(load, 16)
                sp.dma_start(rowp[E:2 * E, :], inp["L1_ffn_ln_b"]).then_inc(load, 16)
                sp.dma_start(rowp[2 * E:NROW, :], inp["L1_ffn_b1"].rearrange("e (h p) -> (e h) p", p=128)).then_inc(load, 16)
                for e in range(E):
                    if e >= 2:
                        sp.wait_ge(y_done, NCH * (e - 1))
                    sp.dma_start(w1[e % 2][:, :], inp["L1_ffn_W1"][e]).then_inc(load_w[e % 2], 16)
                    sp.dma_start(w2[e % 2][:, :, :], inp["L1_ffn_W2"][e].rearrange("(h p) d -> p h d", p=128)).then_inc(load_w[e % 2], 16)
                ov = out.rearrange("b t c d -> (b t c) d").rearrange("(n p) d -> p n d", p=128)
                for n in range(NCH):
                    sp.wait_ge(y_used, 4 * (NN - NCH + n + 1))
                    sp.dma_start(ov[:, 4 * n:4 * n + 4, :], sb["x1"][:, 4 * n:4 * n + 4, :]).then_inc(stored, 16)
                sp.wait_ge(stored, 16 * NCH)

            @block.scalar
            def _(act):
                act.wait_ge(nrm, 1)
                nc.scalar.activation(std[:, :], std[:, :], ACT.Sqrt).then_inc(sq1, 1)
                act.wait_ge(nrm, 5)
                nc.scalar.activation(s2[:, :], v2[:, :], ACT.Sqrt).then_inc(sq1, 1)
                for g in range(NT // 4):
                    act.wait_ge(xn_turned, g + 1)
                    nc.scalar.copy(xnf[:, 512 * g:512 * g + 512], ps_y[g % 2][:, :]).then_inc(xnf_ready, 1)
                act.wait_ge(rt, 12)
                nc.scalar.activation(ex[:, :, :], ex[:, :, :], ACT.Exp).then_inc(ex_ready, 1)
                for g in range(NT // 4):
                    act.wait_ge(wt_done, g + 1)
                    nc.scalar.copy(wt8[:, 512 * g:512 * g + 512], ps_y[g % 2][0:E, :]).then_inc(wt_ready, 1)
                for n in range(NN):
                    e = n // NCH
                    act.wait_ge(hb_ready, e + 1)
                    if n >= 2:
                        act.wait_ge(y_done, n - 1)
                    for h in range(NH):
                        act.wait_ge(h_done, NH * n + h + 1)
                        nc.scalar.activation(hh[n % 2][:, h, :], ps_h[h][:, :], ACT.Gelu, bias=hb[e % 2][:, h:h + 1]).then_inc(h_ready, 1)

            @block.tensor
            def _(pe):
                ident = sb["cst"][:, C_ID:C_ID + 128]
                pe.wait_ge(load, 96)
                nc.tensor.transpose(ps_b[:, 0:NROW], rowp[:, :], ident[0:NROW, 0:NROW]).then_inc(col_done, 1)
                for g in range(NT // 4):
                    if g >= 2:
                        pe.wait_ge(xnf_ready, g - 1)
                    for i in range(4):
                        pe.wait_ge(xn_ready, 4 * g + i + 1)
                        m = nc.tensor.transpose(ps_y[g % 2][:, 128 * i:128 * i + 128], xn[:, i, :], ident)
                        m.then_inc(sb["xn_used"], 1) if i < 3 else m.then_inc(xn_turned, 1)
                pe.wait_ge(xnf_ready, NT // 4)
                pe.wait_ge(load, 96)
                for n in range(NT):
                    m = nc.tensor.matmul(ps_r[:, E * n:E * n + E], xnf[:, 128 * n:128 * n + 128], wr[:, :], start=True, stop=True)
                m.then_inc(lg_done, 1)
                pe.wait_ge(rt, 16)
                for g in range(NT // 4):
                    if g >= 2:
                        pe.wait_ge(wt_ready, g - 1)
                    for i in range(4):
                        m = nc.tensor.transpose(ps_y[g % 2][0:E, 128 * i:128 * i + 128], sel[:, 4 * g + i, :], ident)
                    m.then_inc(wt_done, 1)
                for g in range(NT // 4):
                    pe.wait_ge(wt_ready, g + 1)
                    if g >= 1:
                        pe.wait_ge(bt_used, g)
                    for i in range(4):
                        n = 4 * g + i
                        m = nc.tensor.matmul(ps_b[:, 128 * i:128 * i + 128], wt8[:, 128 * n:128 * n + 128], b2[:, :], start=True, stop=True)
                    m.then_inc(bt_done, 1)
                pe.wait_ge(bt_used, NT // 4)
                for k in range(NN + 1):
                    if k < NN:
                        n, e = k, k // NCH
                        pe.wait_ge(w_ready, e + 1)
                        if n % NCH == 0:
                            pe.wait_ge(col_ready, 1)
                            for h in range(NH):
                                m = nc.tensor.matmul(ps_r[:, h:h + 1], w1[e % 2][:, 128 * h:128 * h + 128], lnb[:, e:e + 1], start=True, stop=True)
                            m.then_inc(hb_done, 1)
                        for h in range(NH):
                            if n >= 1:
                                pe.wait_ge(h_ready, NH * (n - 1) + h + 1)
                            nc.tensor.matmul(ps_h[h][:, :], w1g[e % 2][:, 128 * h:128 * h + 128],
                                             xnf[:, 512 * (n % NCH):512 * (n % NCH) + 512], start=True, stop=True).then_inc(h_done, 1)
                    if k >= 1:
                        n, e = k - 1, (k - 1) // NCH
                        pe.wait_ge(h_ready, NH * (n + 1))
                        if n >= 2:
                            pe.wait_ge(y_used, 4 * (n - 1))
                        for i in range(4):
                            for h in range(NH):
                                m = nc.tensor.matmul(ps_y[n % 2][:, 128 * i:128 * i + 128], hh[n % 2][:, h, 128 * i:128 * i + 128],
                                                     w2[e % 2][:, h, :], start=h == 0, stop=h == NH - 1)
                        m.then_inc(y_done, 1)

            @block.vector
            def _(dve):
                mv = sb["mv"]
                nc.vector.tensor_scalar(std[:, :], mv[:, :, 1], 1e-5, None, ALU.add).then_inc(nrm, 1)
                dve.wait_ge(sq1, 1)
                nc.vector.reciprocal(r1[:, :], std[:, :]).then_inc(nrm, 1)
                dve.wait_ge(nrm, 2)
                nc.vector.tensor_tensor(v2[:, :], r1[:, :], r1[:, :], ALU.mult).then_inc(nrm, 1)
                dve.wait_ge(nrm, 3)
                nc.vector.tensor_tensor(v2[:, :], v2[:, :], mv[:, :, 1], ALU.mult).then_inc(nrm, 1)
                dve.wait_ge(nrm, 4)
                nc.vector.tensor_scalar(v2[:, :], v2[:, :], 1e-5, None, ALU.add).then_inc(nrm, 1)
                dve.wait_ge(sq1, 2)
                nc.vector.reciprocal(r12[:, :], s2[:, :]).then_inc(nrm, 1)
                dve.wait_ge(nrm, 6)
                nc.vector.tensor_tensor(r12[:, :], r12[:, :], r1[:, :], ALU.mult).then_inc(nrm, 1)
                dve.wait_ge(nrm, 7)
                for n in range(NT):
                    if n >= 4:
                        g, i = (n - 4) // 4, (n - 4) % 4
                        if i < 3:
                            dve.wait_ge(sb["xn_used"], 3 * g + i + 1)
                        else:
                            dve.wait_ge(xn_turned, g + 1)
                    nc.vector.tensor_scalar(xn[:, n % 4, :], sb["x1"][:, n, :], mv[:, n, 0:1], r12[:, n:n + 1],
                                            ALU.subtract, ALU.mult).then_inc(xn_ready, 1)
                dve.wait_ge(col_done, 1)
                nc.vector.tensor_copy(colp[:, :], ps_b[:, 0:NROW]).then_inc(col_ready, 1)
                dve.wait_ge(col_ready, 1)
                step = [0]

                def link(i):
                    step[0] += 1
                    i.then_inc(rt, 1)
                    dve.wait_ge(rt, step[0])

                def per_tile(v):
                    return v.rearrange("p (n a) -> p n a", a=1).to_broadcast([128, NT, E])

                def per_expert(v):
                    return v.rearrange("p (a e) -> p a e", a=1).to_broadcast([128, NT, E])

                rank = per_expert(sb["cst"][:, C_RANK:C_RANK + E])
                dve.wait_ge(lg_done, 1)
                link(nc.vector.tensor_tensor(lg[:, :, :], ps_r[:, 0:NT * E].rearrange("p (n e) -> p n e", e=E), per_tile(s2[:, :]), ALU.mult))
                link(nc.vector.tensor_tensor(lg[:, :, :], lg[:, :, :], per_expert(br[:, :]), ALU.add))
                link(nc.vector.tensor_reduce(m1[:, :], lg[:, :, :], AX.X, ALU.max))
                link(nc.vector.tensor_tensor(key[:, :, :], lg[:, :, :], per_tile(m1[:, :]), ALU.is_ge))
                link(nc.vector.tensor_tensor(key[:, :, :], key[:, :, :], rank, ALU.mult))
                link(nc.vector.tensor_reduce(mk[:, :], key[:, :, :], AX.X, ALU.max))
                link(nc.vector.tensor_tensor(sel[:, :, :], key[:, :, :], per_tile(mk[:, :]), ALU.is_ge))
                link(nc.vector.scalar_tensor_tensor(out=lg2[:, :, :], in0=sel[:, :, :], scalar=-3.0e38, in1=lg[:, :, :],
                                                    op0=ALU.mult, op1=ALU.add))
                link(nc.vector.tensor_reduce(mk[:, :], lg2[:, :, :], AX.X, ALU.max))
                link(nc.vector.tensor_tensor(key[:, :, :], lg2[:, :, :], per_tile(mk[:, :]), ALU.is_ge))
                link(nc.vector.tensor_tensor(key[:, :, :], key[:, :, :], rank, ALU.mult))
                link(nc.vector.tensor_tensor(ex[:, :, :], lg[:, :, :], per_tile(m1[:, :]), ALU.subtract))
                link(nc.vector.tensor_reduce(mk[:, :], key[:, :, :], AX.X, ALU.max))
                link(nc.vector.tensor_tensor(key[:, :, :], key[:, :, :], per_tile(mk[:, :]), ALU.is_ge))
                link(nc.vector.tensor_tensor(sel[:, :, :], sel[:, :, :], key[:, :, :], ALU.add))
                dve.wait_ge(ex_ready, 1)
                step2 = [0]
                def link2(i):
                    step2[0] += 1
                    i.then_inc(sb["f_w2"], 1)
                    dve.wait_ge(sb["f_w2"], step2[0])
                link2(nc.vector.tensor_tensor(ex[:, :, :], ex[:, :, :], sel[:, :, :], ALU.mult))
                link2(nc.vector.tensor_reduce(m1[:, :], ex[:, :, :], AX.X, ALU.add))
                link2(nc.vector.reciprocal(m1[:, :], m1[:, :]))
                nc.vector.tensor_tensor(sel[:, :, :], ex[:, :, :], per_tile(m1[:, :]), ALU.mult).then_inc(rt, 1)
                dve.wait_ge(load, 96)
                for g in range(NT // 4):
                    dve.wait_ge(bt_done, g + 1)
                    x = sb["x1"][:, 4 * g:4 * g + 4, :].rearrange("p n f -> p (n f)")
                    nc.vector.tensor_tensor(x, ps_b[:, :], x, ALU.add).then_inc(bt_used, 1)

                def prepare_w(e):
                    if e >= 2:
                        dve.wait_ge(y_done, NCH * (e - 1))
                    dve.wait_ge(load_w[e % 2], 32 * (e // 2 + 1))
                    nc.vector.tensor_scalar(w1g[e % 2][:, :], w1[e % 2][:, :], lng[:, e:e + 1], None, ALU.mult).then_inc(w_ready, 1)

                def prepare_b(e):
                    dve.wait_ge(hb_done, e + 1)
                    nc.vector.tensor_tensor(hb[e % 2][:, :], ps_r[:, 0:NH], b1t[:, e, :], ALU.add).then_inc(hb_ready, 1)

                prepare_w(0)
                prepare_b(0)
                for n in range(NN):
                    e = n // NCH
                    if n % NCH == 1 and e + 1 < E:
                        prepare_w(e + 1)
                    dve.wait_ge(y_done, n + 1)
                    if n >= NCH:
                        dve.wait_ge(y_used, 4 * (n - NCH + 1))
                    for i in range(4):
                        j = 4 * (n % NCH) + i
                        nc.vector.scalar_tensor_tensor(out=sb["x1"][:, j, :], in0=ps_y[n % 2][:, 128 * i:128 * i + 128],
                                                       scalar=sel[:, j, e:e + 1], in1=sb["x1"][:, j, :],
                                                       op0=ALU.mult, op1=ALU.add).then_inc(y_used, 1)
                    if n % NCH == NCH - 1 and e + 1 < E:
                        prepare_b(e + 1)


def build(nc, inp, consts, out, stop=None, dbg=None):
    with ExitStack() as st:
        sb = {}

        def alloc(name, shape, dt=F32, stack=st):
            sb[name] = stack.enter_context(nc.sbuf_tensor("s_" + name, shape, dt))

        alloc("cst", [128, C_ALL])
        alloc("x1", [128, NT, 128])
        alloc("mv", [128, NT, 2])
        sb["load_xb"] = st.enter_context(nc.semaphore("load_xb"))
        mem = st.enter_context(ExitStack())
        alloc("qf", [128, B, T, C], stack=mem)
        for k in ("10", "20", "11", "21"):
            alloc("w" + k, [128, B, 256], stack=mem)
        steps = mem.enter_context(ExitStack())
        for k in ("10", "20", "11", "21"):
            alloc("m" + k, [128, B, 256], stack=steps)
        alloc("kf", [128, T, 128], stack=steps)
        alloc("vf", [128, T, 128], stack=steps)
        alloc("ktok", [128, T, 128], stack=steps)
        alloc("coef", [128, T, 9], stack=steps)
        prepare(nc, st, sb, inp, consts)
        if stop == 0:
            dump(nc, st, sb, dbg)
            return
        learn(nc, st, sb)
        if stop == 1:
            dump(nc, st, sb, dbg)
            return
        steps.close()
        read_out(nc, st, sb, inp)
        mem.close()
        if stop == 2:
            dump(nc, st, sb, dbg)
            return
        attend(nc, st, sb, inp)
        if stop == 3:
            dump(nc, st, sb, dbg)
            return
        sb["xn_used"] = st.enter_context(nc.semaphore("f_xnu"))
        sb["f_w2"] = st.enter_context(nc.semaphore("f_wsum"))
        experts(nc, st, sb, inp, out)


_INS = ['x', 'L0_conv_Wq', 'L0_conv_Wk', 'L0_conv_Wv', 'L0_conv_w_lr', 'L0_conv_w_forget', 'L0_conv_w_eta',
        'L0_conv_w1_0', 'L0_conv_w2_0', 'L0_conv_w1_1', 'L0_conv_w2_1', 'L1_attn_Wt', 'L1_attn_Wx', 'L1_attn_bh',
        'L1_attn_Wa', 'L1_attn_ba', 'L1_ffn_Wr', 'L1_ffn_br', 'L1_ffn_ln_g', 'L1_ffn_ln_b', 'L1_ffn_W1', 'L1_ffn_b1',
        'L1_ffn_W2', 'L1_ffn_b2']


def shape_constants():
    import numpy as np
    c = np.zeros((128, C_ALL), np.float32)
    p = np.arange(128)
    c[:, C_ID:C_ID + 128] = np.eye(128)
    c[:, C_MEAN:C_MEAN + 128] = (p[:, None] // C == p[None] // C) / C
    c[:, C_GRP:C_GRP + 128] = (p[:, None] // 4 == p[None] // 4) / 4
    w = np.arange(128 + WIN)
    c[:, C_BAND:C_BAND + 128 + WIN] = (w[None] >= p[:, None]) & (w[None] < p[:, None] + WIN)
    for n in range(S // 128):
        for j in range(WIN):
            key = 128 * n - WIN // 2 + p + (j - p) % WIN
            c[:, C_EDGE + WIN * n + j] = np.where((key < 0) | (key >= S), -10000.0, 0.0)
    c[:, C_RANK:C_RANK + E] = E - np.arange(E)
    for b in range(B):
        c[:, C_SEL + 128 * b:C_SEL + 128 * b + 128] = (p[:, None] // C == b) / C
    return c


def kernel(**inputs):
    import numpy as _np
    import concourse.bacc as _bacc
    from concourse import mybir as _mybir
    from concourse.bass_utils import run_bass_kernel_spmd as _run

    nc = _bacc.Bacc("TRN2", target_bir_lowering=False, num_devices=1)
    arrays, aps = {}, {}
    for name in _INS:
        a = _np.ascontiguousarray(inputs[name])
        arrays[f"in_{name}_dram"] = a
        aps[name] = nc.dram_tensor(f"in_{name}_dram", a.shape, _mybir.dt.from_np(a.dtype), kind="ExternalInput").ap()
    c = shape_constants()
    arrays["in_constants_dram"] = c
    consts = nc.dram_tensor("in_constants_dram", c.shape, _mybir.dt.float32, kind="ExternalInput").ap()
    out = nc.dram_tensor("out_0_dram", (B, T, C, D), _mybir.dt.float32, kind="ExternalOutput").ap()
    build(nc, aps, consts, out)
    r = _run(nc, [arrays], core_ids=[0])
    return r.results[0]["out_0_dram"]
```

```python
from contextlib import ExitStack

import concourse.bass as bass
from concourse import mybir

F32 = mybir.dt.float32
BF16 = mybir.dt.bfloat16
ALU = mybir.AluOpType
ACT = mybir.ActivationFunctionType
AX = mybir.AxisListType

B, T, C, D = 4, 32, 32, 128
S = T * C
NT = B * S // 128
DE = 256
NC_E = DE // 128
U = 32
WIN = 32
E = 8
H = 512
MAX_LR = 0.1
GELU_C = 0.7978845608028654
GELU_A = 0.044715
C_ID, C_MEAN, C_GRP, C_BAND, C_EDGE, C_RANK, C_SEL = 0, 128, 256, 384, 544, 800, 808
C_ALL = C_SEL + 512


PARAMS = ("21", "11", "10", "20")


def prepare(nc, st, sb, inp, consts):
    sem = lambda name: st.enter_context(nc.semaphore(name))
    NP = 3 * D + 3
    with ExitStack() as ctx:
        xs = ctx.enter_context(nc.sbuf_tensor("xs", [128, T, 128], F32))
        xf = ctx.enter_context(nc.sbuf_tensor("xf", [128, T, B, C], F32))
        xg = ctx.enter_context(nc.sbuf_tensor("xg", [128, T, B, C], F32))
        proj = ctx.enter_context(nc.sbuf_tensor("proj", [128, T, NP], F32))
        wcat = ctx.enter_context(nc.sbuf_tensor("wcat", [128, NP], F32))
        bst = ctx.enter_context(nc.sbuf_tensor("bst", [128, B, 2, 6], F32))
        mv = ctx.enter_context(nc.sbuf_tensor("mv", [128, B, 2], F32))
        me = ctx.enter_context(nc.sbuf_tensor("me", [128, B, 2], F32))
        ge = ctx.enter_context(nc.sbuf_tensor("ge", [128, B, 2], F32))
        gvar = ctx.enter_context(nc.sbuf_tensor("gvar", [128, B], F32))
        gsd = ctx.enter_context(nc.sbuf_tensor("gsd", [128, B], F32))
        grs = ctx.enter_context(nc.sbuf_tensor("grs", [128, B], F32))
        gneg = ctx.enter_context(nc.sbuf_tensor("gneg", [128, B], F32))
        ss = ctx.enter_context(nc.sbuf_tensor("ss", [128, T, 2], F32))
        sn = ctx.enter_context(nc.sbuf_tensor("sn", [128, T, 2], F32))
        sig = ctx.enter_context(nc.sbuf_tensor("sig", [128, 3, T], F32))
        ps = [ctx.enter_context(nc.psum_tensor(f"pp{i}", [128, 512], F32)) for i in range(8)]

        load_x, load_c, load_w, load_p = sem("load_x"), sem("load_c"), sem("load_w"), sem("load_p")
        xt_done, xf_ready = sem("xt_done"), sem("xf_ready")
        gn_chain, gn_sum, gn_sqrt = sem("gn_chain"), sem("gn_sum"), sem("gn_sqrt")
        xg_ready, proj_done, proj_ready = sem("xg_ready"), sem("proj_done"), sem("proj_ready")
        sq_ready, nrm_chain, nrm_sqrt = sem("sq_ready"), sem("nrm_chain"), sem("nrm_sqrt")
        qk_normed, qk_turned, qk_ready = sem("qk_normed"), sem("qk_turned"), sem("qk_ready")
        sig_ready, gate_done = sem("sig_ready"), sem("gate_done")
        gn_step, q_copied, coef_ready = sem("gn_step"), sem("q_copied"), sem("coef_ready")

        with nc.Block() as block:
            @block.sync
            def _(sp):
                xv = inp["x"].rearrange("b t c d -> b c t d")
                for b in range(B):
                    sp.dma_start(xs[32 * b:32 * b + 32, :, :], xv[b]).then_inc(load_x, 16)
                sp.dma_start(sb["cst"][:, :], consts).then_inc(load_c, 16)
                sp.dma_start(sb["x1"][:, :, :], inp["x"].rearrange("b t c d -> (b t c) d").rearrange("(n p) d -> p n d", p=128)).then_inc(sb["load_xb"], 16)

            @block.scalar
            def _(act):
                for a, k in ((0, "L0_conv_Wq"), (128, "L0_conv_Wk"), (256, "L0_conv_Wv")):
                    act.dma_start(wcat[:, a:a + 128], inp[k]).then_inc(load_w, 16)
                for i, k in enumerate(("L0_conv_w_lr", "L0_conv_w_forget", "L0_conv_w_eta")):
                    act.dma_start(wcat[:, 384 + i:385 + i], inp[k].rearrange("(d a) -> d a", a=1)).then_inc(load_w, 16)
                for k, src in (("10", "L0_conv_w1_0"), ("11", "L0_conv_w1_1")):
                    act.dma_start(sb["first" + k][:, :], inp[src]).then_inc(load_p, 16)
                for k, src in (("20", "L0_conv_w2_0"), ("21", "L0_conv_w2_1")):
                    act.dma_start(sb["first" + k][:, :].rearrange("p (h d) -> p h d", h=2),
                                  inp[src].rearrange("(h p) d -> p h d", p=128)).then_inc(load_p, 16)
                for g in range(T // 4):
                    act.wait_ge(xt_done, g + 1)
                    nc.scalar.copy(xf[:, 4 * g:4 * g + 4, :, :].rearrange("p t b c -> p (t b c)"), ps[g % 4][:, :]).then_inc(xf_ready, 1)
                act.wait_ge(gn_chain, 5)
                nc.scalar.activation(gsd[:, :], gvar[:, :], ACT.Sqrt).then_inc(gn_sqrt, 1)
                for t in range(T):
                    act.wait_ge(proj_done, t + 1)
                    nc.scalar.copy(proj[:, t, :], ps[t % 4][:, 0:NP]).then_inc(proj_ready, 1)
                act.wait_ge(proj_ready, T)
                nc.scalar.activation(xs[:, :, :], proj[:, :, 0:128], ACT.Square).then_inc(sq_ready, 1)
                act.wait_ge(xg_ready, B)
                nc.scalar.activation(xf[:, :, :, :].rearrange("p t b c -> p t (b c)"), proj[:, :, 128:256], ACT.Square).then_inc(sq_ready, 1)
                act.wait_ge(nrm_chain, 1)
                nc.scalar.activation(sn[:, :, :], ss[:, :, :], ACT.Sqrt).then_inc(nrm_sqrt, 1)
                nc.scalar.activation(sig[:, :, :], proj[:, :, 384:387].rearrange("p t g -> p g t"), ACT.Sigmoid).then_inc(sig_ready, 1)
                for g in range(T // 4):
                    act.wait_ge(qk_turned, 2 * g + 2)
                    nc.scalar.copy(sb["kf"][:, 4 * g:4 * g + 4, :].rearrange("p t n -> p (t n)"), ps[4 + g % 2][:, :]).then_inc(qk_ready, 1)
                act.wait_ge(load_p, 16 * 4)

            @block.tensor
            def _(pe):
                cst = sb["cst"]
                ident = cst[:, C_ID:C_ID + 128]
                pe.wait_ge(load_c, 16)
                pe.wait_ge(load_x, 64)
                for t in range(T):
                    if t % 4 == 0 and t >= 16:
                        pe.wait_ge(xf_ready, t // 4 - 3)
                    i = nc.tensor.transpose(ps[(t // 4) % 4][:, 128 * (t % 4):128 * (t % 4) + 128], xs[:, t, :], ident)
                    if t % 4 == 3:
                        i.then_inc(xt_done, 1)
                pe.wait_ge(gn_chain, 3)
                pe.wait_ge(xf_ready, T // 4)
                nc.tensor.matmul(ps[7][:, 0:2 * B], cst[:, C_GRP:C_GRP + 128],
                                 me[:, :, :].rearrange("p b s -> p (b s)"), start=True, stop=True).then_inc(gn_sum, 1)
                pe.wait_ge(xg_ready, B)
                pe.wait_ge(load_w, 16 * 6)
                for t in range(T):
                    if t >= 4:
                        pe.wait_ge(proj_ready, t - 3)
                    nc.tensor.matmul(ps[t % 4][:, 0:NP], xg[:, t, :, :].rearrange("p b c -> p (b c)"), wcat[:, :],
                                     start=True, stop=True).then_inc(proj_done, 1)
                pe.wait_ge(sig_ready, 1)
                for b in range(B):
                    nc.tensor.matmul(ps[6][:, 64 * b:64 * b + 64], cst[:, C_SEL + 128 * b:C_SEL + 128 * b + 128],
                                     sig[:, 1:3, :].rearrange("p g t -> p (g t)"), start=True, stop=True)
                nc.tensor.matmul(ps[6][:, 256:256 + T], cst[:, C_MEAN:C_MEAN + 128], sig[:, 0, :],
                                 start=True, stop=True).then_inc(gate_done, 1)
                pe.wait_ge(qk_normed, 1)
                for g in range(T // 4):
                    if g >= 2:
                        pe.wait_ge(qk_ready, g - 1)
                    for j in range(2):
                        if g >= 2:
                            pe.wait_ge(q_copied, g - 1)
                        for i in range(4):
                            t = 4 * g + i
                            src = proj[:, t, 0:128] if j == 0 else sb["ktok"][:, t, :]
                            m = nc.tensor.transpose(ps[(0 if j == 0 else 4) + g % 2][:, 128 * i:128 * i + 128], src, ident)
                        m.then_inc(qk_turned, 1)

            @block.vector
            def _(dve):
                nc.vector.memset(sb["kf"][:, T, :], 0.0)
                dve.wait_ge(load_c, 16)
                dve.wait_ge(xf_ready, T // 4)
                for b in range(B):
                    for h in range(2):
                        i = nc.vector.bn_stats(bst[:, b, h, :], xf[:, 16 * h:16 * h + 16, b, :])
                i.then_inc(gn_chain, 1)
                dve.wait_ge(gn_chain, 1)
                for b in range(B):
                    i = nc.vector.bn_aggr(mv[:, b, :], bst[:, b, :, :].rearrange("p h s -> p (h s)"))
                i.then_inc(gn_chain, 1)
                dve.wait_ge(gn_chain, 2)
                nc.vector.tensor_copy(me[:, :, 0], mv[:, :, 0])
                for b in range(B):
                    i = nc.vector.scalar_tensor_tensor(out=me[:, b, 1:2], in0=mv[:, b, 0:1], scalar=mv[:, b, 0:1],
                                                       in1=mv[:, b, 1:2], op0=ALU.mult, op1=ALU.add)
                i.then_inc(gn_chain, 1)
                dve.wait_ge(gn_sum, 1)
                nc.vector.tensor_copy(ge[:, :, :].rearrange("p b s -> p (b s)"), ps[7][:, 0:2 * B]).then_inc(gn_chain, 1)
                dve.wait_ge(gn_chain, 4)
                for b in range(B):
                    i = nc.vector.tensor_scalar(gvar[:, b:b + 1], ge[:, b, 0:1], ge[:, b, 0:1], -1.0, ALU.mult, ALU.mult)
                i.then_inc(gn_step, 1)
                dve.wait_ge(gn_step, 1)
                nc.vector.scalar_tensor_tensor(out=gvar[:, :], in0=gvar[:, :], scalar=1e-5, in1=ge[:, :, 1],
                                               op0=ALU.add, op1=ALU.add).then_inc(gn_chain, 1)
                dve.wait_ge(gn_sqrt, 1)
                nc.vector.reciprocal(grs[:, :], gsd[:, :]).then_inc(gn_step, 1)
                dve.wait_ge(gn_step, 2)
                nc.vector.scalar_tensor_tensor(out=gneg[:, :], in0=ge[:, :, 0], scalar=-1.0, in1=grs[:, :],
                                               op0=ALU.mult, op1=ALU.mult).then_inc(gn_step, 1)
                dve.wait_ge(gn_step, 3)
                for b in range(B):
                    nc.vector.tensor_scalar(xg[:, :, b, :], xf[:, :, b, :], grs[:, b:b + 1], gneg[:, b:b + 1],
                                            ALU.mult, ALU.add).then_inc(xg_ready, 1)
                dve.wait_ge(sq_ready, 2)
                nc.vector.tensor_reduce(ss[:, :, 0:1], xs[:, :, :], AX.X, ALU.add)
                nc.vector.tensor_reduce(ss[:, :, 1:2], xf[:, :, :, :].rearrange("p t b c -> p t (b c)"), AX.X, ALU.add).then_inc(nrm_chain, 1)
                dve.wait_ge(nrm_sqrt, 1)
                nc.vector.tensor_scalar(sn[:, :, :], sn[:, :, :], 1e-12, None, ALU.max).then_inc(nrm_chain, 1)
                dve.wait_ge(nrm_chain, 2)
                nc.vector.reciprocal(sn[:, :, :], sn[:, :, :]).then_inc(nrm_chain, 1)
                dve.wait_ge(nrm_chain, 3)
                rn = sn[:, :, :]
                nc.vector.tensor_tensor(proj[:, :, 0:128], proj[:, :, 0:128], rn[:, :, 0:1].to_broadcast([128, T, 128]), ALU.mult)
                nc.vector.tensor_tensor(sb["ktok"][:, :, :], proj[:, :, 128:256], rn[:, :, 1:2].to_broadcast([128, T, 128]), ALU.mult).then_inc(qk_normed, 1)
                dve.wait_ge(gate_done, 1)
                gates = ps[6][:, 0:256].rearrange("p (b g t) -> p b g t", b=B, g=2)
                for b in range(B):
                    nc.vector.tensor_copy(sb["coef"][:, :, b], gates[:, b, 1, :])
                    nc.vector.tensor_scalar(sb["coef"][:, :, 4 + b], gates[:, b, 0, :], -1.0, 1.0, ALU.mult, ALU.add)
                nc.vector.tensor_scalar(sb["coef"][:, :, 8], ps[6][:, 256:256 + T], -MAX_LR * 2.0 / (C * D), None, ALU.mult).then_inc(coef_ready, 1)
                dve.wait_ge(coef_ready, 1)
                nc.vector.tensor_tensor(sb["vs"][:, :, :], proj[:, :, 256:384], sb["coef"][:, :, 8:9].to_broadcast([128, T, 128]), ALU.mult)
                for g in range(T // 4):
                    dve.wait_ge(qk_turned, 2 * g + 1)
                    nc.vector.tensor_copy(sb["qf"][:, :, 4 * g:4 * g + 4, :].rearrange("p b t c -> p t b c"),
                                          ps[g % 2][:, :].rearrange("p (t b c) -> p t b c", t=4, b=B)).then_inc(q_copied, 1)


def learn(nc, st, sb):
    sem = lambda name: st.enter_context(nc.semaphore(name))
    with ExitStack() as ctx:
        def buf(name, shape):
            return ctx.enter_context(nc.sbuf_tensor("l_" + name, shape, F32))

        W = {k: sb["w" + k] for k in PARAMS}
        M = {k: buf("m" + k, [128, B, 256]) for k in PARAMS}
        WT = {k: buf("wt" + k, [128, B, 256]) for k in ("21", "11", "20")}
        Q = {k: buf("q" + k, [128, B, 256]) for k in ("21", "11", "20")}
        kt = buf("kt", [128, 128])
        cf = buf("cf", [128, 9])
        km, h1m, dpm, dh1m = (buf(n, [128, B, 128]) for n in ("km", "h1m", "dpm", "dh1m"))
        g = [buf("g0", [128, 256]), buf("g1", [128, 256])]
        h1, hv, dp, dh1 = (buf(n, [128, 128]) for n in ("h1", "hv", "dp", "dh1"))
        da = [buf("da0", [128, 256]), buf("da1", [128, 256])]
        gf, daf = [buf("gf0", [128, 256]), buf("gf1", [128, 256])], buf("daf", [128, 256])
        h1f, dpf, dh1f = (buf(n, [128, 128]) for n in ("h1f", "dpf", "dh1f"))
        ca, aq, u, th, tq, dd, gp = ([buf(f"{n}{l}", [128, 256]) for l in range(2)] for n in ("ca", "aq", "u", "th", "tq", "dd", "gp"))

        def bank(name, n=1):
            return ctx.enter_context(nc.psum_tensor("lp_" + name, [128, 512 * n], F32))

        ps_a, ps_b, ps_h, ps_t = bank("a"), bank("b"), bank("h"), bank("t")
        ps_g = [bank("g0", 2), bank("g1", 2)]

        first_turned, mom_clear = sem("l_first"), sem("l_mclear")
        mm_done = sem("l_mm")
        turned, gf_ready = sem("l_turned"), sem("l_f")
        grad_done = sem("l_grad")
        wt_done, wt_ready = sem("l_wt"), sem("l_wt_ready")
        gelu_ready, pre_ready = sem("l_gelu"), sem("l_pre")
        u_ready, tanh_ready, slope_ready = ([sem(f"l_{n}{l}") for l in range(2)] for n in ("u", "tanh", "slope"))
        kt_in, cf_in = sem("l_kt_in"), sem("l_cf_in")
        zeroed, km_ready, h1m_ready, dpm_ready, dh1m_ready = (sem("l_" + n) for n in ("zeroed", "kmr", "h1mr", "dpmr", "dh1mr"))
        kept = sem("l_kept")
        chain = sem("l_chain")
        mom_ready = sem("l_mom")
        w_ready = {k: sem("l_w" + k) for k in PARAMS}
        table_loaded = sem("l_table")
        A0, H1, A1, Y, DG1, DH1, DG0 = range(1, 8)
        TG0, TH1, TG1, TDP, TDA1, TDH1 = range(1, 7)
        G21, G11, G20, G10 = range(1, 5)
        X20, X21, X11 = 2, 3, 4
        K_H1, K_HV, K_DP, K_DA1, K_DH1, K_DA0 = range(1, 7)

        def grad_bank(b):
            return ps_g[b // 2][:, 512 * (b % 2):512 * (b % 2) + 256]

        def rows(b):
            return slice(32 * b, 32 * b + 32)

        def step_of(t, k):
            return sb[k][:, bass.ds(t, 1), :].rearrange("p a n -> p (a n)")

        with nc.Block() as block:
            @block.gpsimd
            def _(pool):
                def update(t, k, n, q):
                    for h in range(2):
                        pool.wait_ge(mom_ready, t * 16 + 16 + 4 * (n - 1) + 2 * h + 2)
                        pool.wait_ge(kept, t * 3 + q)
                        b = slice(2 * h, 2 * h + 2)
                        nc.gpsimd.tensor_tensor(W[k][:, b, :], Q[k][:, b, :], M[k][:, b, :], ALU.add).then_inc(w_ready[k], 1)

                nc.gpsimd.tensor_copy(kt[:, :], sb["kf"][:, 0, :]).then_inc(kt_in, 1)
                with pool.Fori(0, T) as t:
                    pool.wait_ge(mm_done, t * 7 + A0)
                    nc.gpsimd.tensor_copy(kt[:, :], sb["kf"][:, bass.ds(t + 1, 1), :].rearrange("p a n -> p (a n)")).then_inc(kt_in, 1)
                    update(t, "21", G21, 1)
                    update(t, "11", G11, 2)
                    update(t, "20", G20, 3)

            @block.scalar
            def _(act):
                def hidden(t, l, p):
                    act.wait_ge(mm_done, t * 7 + (A0, A1)[l])
                    nc.scalar.activation(g[l][:, :], p[:, 0:256], ACT.Gelu_apprx_tanh).then_inc(gelu_ready, 1)

                def before_slope(t, l, p):
                    nc.scalar.mul(ca[l][:, :], p[:, 0:256], -1.5 * GELU_C).then_inc(pre_ready, 1)
                    nc.scalar.activation(aq[l][:, :], p[:, 0:256], ACT.Square, scale=GELU_A ** 0.5).then_inc(pre_ready, 1)

                def tanh(t, l):
                    act.wait_ge(u_ready[l], t * 2 + 1)
                    nc.scalar.activation(th[l][:, :], u[l][:, :], ACT.Tanh, scale=-1.0 / 1.5).then_inc(tanh_ready[l], 1)
                    act.wait_ge(tanh_ready[l], t * 2 + 1)
                    nc.scalar.activation(tq[l][:, :], th[l][:, :], ACT.Square).then_inc(tanh_ready[l], 1)

                def feature(t, n, dst, width):
                    act.wait_ge(turned, t * 6 + n)
                    nc.scalar.copy(dst[:, :], ps_t[:, 0:width]).then_inc(gf_ready, 1)

                def wt(t, n, k):
                    act.wait_ge(wt_done, t * 4 + n)
                    nc.scalar.copy(WT[k][:, :, :].rearrange("p b n -> p (b n)"), ps_g[n % 2][:, :]).then_inc(wt_ready, 1)

                def masked(dst, src, ready):
                    for b in range(B):
                        i = nc.scalar.copy(dst[rows(b), b, :], src[rows(b), :])
                    i.then_inc(ready, 1)

                def keep(t, k):
                    act.wait_ge(w_ready[k], t * 2 + 4)
                    for b in range(B):
                        i = nc.scalar.mul(Q[k][:, b, :], W[k][:, b, :], cf[:, 4 + b:5 + b])
                    i.then_inc(kept, 1)

                nc.scalar.activation(g[0][:, :], sb["first10"][:, :], ACT.Gelu_apprx_tanh).then_inc(table_loaded, 1)
                act.wait_ge(table_loaded, 1)
                act.wait_ge(zeroed, 4)
                with act.Fori(0, T) as t:
                    for h, p in ((0, ps_h), (1, ps_t)):
                        act.wait_ge(wt_done, t * 4 + 1 + h)
                        nc.scalar.copy(WT["20"][:, 2 * h:2 * h + 2, :].rearrange("p b n -> p (b n)"), p[:, :]).then_inc(wt_ready, 1)
                    act.wait_ge(w_ready["10"], t * 4 + 4)
                    nc.scalar.copy(cf[:, :], sb["coef"][:, bass.ds(t, 1), :].rearrange("p a n -> p (a n)")).then_inc(cf_in, 1)
                    hidden(t, 0, ps_a)
                    feature(t, TG0, gf[0], 256)
                    before_slope(t, 0, ps_a)
                    wt(t, X21, "21")
                    feature(t, TH1, h1f, 128)
                    tanh(t, 0)
                    hidden(t, 1, ps_b)
                    masked(h1m, h1, h1m_ready)
                    feature(t, TG1, gf[1], 256)
                    before_slope(t, 1, ps_b)
                    wt(t, X11, "11")
                    tanh(t, 1)
                    feature(t, TDP, dpf, 128)
                    masked(dpm, dp, dpm_ready)
                    feature(t, TDA1, daf, 256)
                    act.wait_ge(cf_in, t + 1)
                    keep(t, "21")
                    feature(t, TDH1, dh1f, 128)
                    masked(dh1m, dh1, dh1m_ready)
                    keep(t, "11")
                    for b in range(B):
                        i = nc.scalar.copy(km[rows(b), b, :], sb["ktok"][rows(b), bass.ds(t, 1), :].rearrange("p a n -> p (a n)"))
                    i.then_inc(km_ready, 1)
                    keep(t, "20")

            @block.vector
            def _(dve):
                def momentum(t, k, n, b):
                    dve.wait_ge(grad_done, t * 16 + 16 + 4 * (n - 1) + b + 1)
                    nc.vector.scalar_tensor_tensor(out=M[k][:, b, :], in0=M[k][:, b, :], scalar=cf[:, b:b + 1], in1=grad_bank(b),
                                                   op0=ALU.mult, op1=ALU.add).then_inc(mom_ready, 1)

                def update(t, k, n, b):
                    dve.wait_ge(mom_ready, t * 16 + 16 + 4 * (n - 1) + b + 1)
                    nc.vector.scalar_tensor_tensor(out=W[k][:, b, :], in0=W[k][:, b, :], scalar=cf[:, 4 + b:5 + b],
                                                   in1=M[k][:, b, :], op0=ALU.mult, op1=ALU.add).then_inc(w_ready[k], 1)

                def slope_in(t, l):
                    dve.wait_ge(pre_ready, t * 4 + 2 * l + 2)
                    nc.vector.scalar_tensor_tensor(out=u[l][:, :], in0=aq[l][:, :], scalar=1.0, in1=ca[l][:, :],
                                                   op0=ALU.add, op1=ALU.mult).then_inc(u_ready[l], 1)
                    nc.vector.scalar_tensor_tensor(out=dd[l][:, :], in0=aq[l][:, :], scalar=1.0 / 3.0, in1=ca[l][:, :],
                                                   op0=ALU.add, op1=ALU.mult).then_inc(u_ready[l], 1)

                def slope_out(t, l):
                    dve.wait_ge(tanh_ready[l], t * 2 + 2)
                    dve.wait_ge(u_ready[l], t * 2 + 2)
                    nc.vector.scalar_tensor_tensor(out=dd[l][:, :], in0=tq[l][:, :], scalar=-1.0, in1=dd[l][:, :],
                                                   op0=ALU.add, op1=ALU.mult).then_inc(slope_ready[l], 1)
                    dve.wait_ge(slope_ready[l], t * 2 + 1)
                    nc.vector.scalar_tensor_tensor(out=gp[l][:, :], in0=th[l][:, :], scalar=0.5, in1=dd[l][:, :],
                                                   op0=ALU.mult, op1=ALU.add).then_inc(slope_ready[l], 1)

                def slope_times(t, l, p, n):
                    dve.wait_ge(slope_ready[l], t * 2 + 2)
                    dve.wait_ge(mm_done, t * 7 + n)
                    nc.vector.scalar_tensor_tensor(out=da[l][:, :], in0=gp[l][:, :], scalar=0.5, in1=p[:, 0:256],
                                                   op0=ALU.add, op1=ALU.mult).then_inc(chain, 1)

                for m in (dpm, h1m, dh1m, km):
                    nc.vector.memset(m[:, :, :], 0.0).then_inc(zeroed, 1)
                for k in PARAMS:
                    for b in range(B):
                        nc.vector.memset(M[k][:, b, :], 0.0).then_inc(mom_ready, 1)
                for k in ("10", "11"):
                    for b in range(B):
                        nc.vector.tensor_copy(W[k][:, b, :], sb["first" + k][:, :]).then_inc(w_ready[k], 1)
                dve.wait_ge(first_turned, 1)
                for k, p in (("20", ps_a), ("21", ps_b)):
                    for b in range(B):
                        nc.vector.tensor_copy(W[k][:, b, :], p[:, 0:256]).then_inc(w_ready[k], 1)
                dve.sem_inc(chain, 6)
                dve.sem_inc(grad_done, 16)
                with dve.Fori(0, T) as t:
                    dve.wait_ge(mm_done, t * 7 + H1)
                    nc.vector.tensor_tensor(h1[:, :], ps_h[:, 0:128], step_of(t, "ktok"), ALU.add).then_inc(chain, 1)
                    dve.wait_ge(chain, t * 6 + 6 + K_H1)
                    dve.wait_ge(cf_in, t + 1)
                    nc.vector.scalar_tensor_tensor(out=hv[:, :], in0=h1[:, :], scalar=cf[:, 8:9], in1=step_of(t, "vs"),
                                                   op0=ALU.mult, op1=ALU.subtract).then_inc(chain, 1)
                    slope_in(t, 0)
                    slope_out(t, 0)
                    slope_in(t, 1)
                    dve.wait_ge(mm_done, t * 7 + Y)
                    dve.wait_ge(chain, t * 6 + 6 + K_HV)
                    nc.vector.scalar_tensor_tensor(out=dp[:, :], in0=ps_h[:, 0:128], scalar=cf[:, 8:9], in1=hv[:, :],
                                                   op0=ALU.mult, op1=ALU.add).then_inc(chain, 1)
                    slope_out(t, 1)
                    slope_times(t, 1, ps_a, DG1)
                    momentum(t, "21", G21, 0)
                    momentum(t, "21", G21, 1)
                    dve.wait_ge(mm_done, t * 7 + DH1)
                    dve.wait_ge(chain, t * 6 + 6 + K_DP)
                    nc.vector.tensor_tensor(dh1[:, :], ps_h[:, 0:128], dp[:, :], ALU.add).then_inc(chain, 1)
                    momentum(t, "21", G21, 2)
                    momentum(t, "21", G21, 3)
                    slope_times(t, 0, ps_b, DG0)
                    for k, n in (("11", G11), ("20", G20), ("10", G10)):
                        for b in range(B):
                            momentum(t, k, n, b)
                    for b in range(B):
                        update(t, "10", G10, b)

            @block.tensor
            def _(pe):
                ident = sb["cst"][:, C_ID:C_ID + 128]

                def up(p, x, w, w_wait=None):
                    for b in range(B):
                        if w_wait:
                            w_wait(b)
                        i = nc.tensor.matmul(p[rows(b), 0:256], x[:, rows(b)], w[:, b, :], start=True, stop=True)
                    i.then_inc(mm_done, 1)

                def down(p, x, w):
                    for h in range(2):
                        for b in range(B):
                            i = nc.tensor.matmul(p[rows(b), 0:128], x[:, 128 * h + 32 * b:128 * h + 32 * b + 32],
                                                 w[:, b, 128 * h:128 * h + 128], start=h == 0, stop=h == 1)
                    i.then_inc(mm_done, 1)

                def turn(x, width):
                    for h in range(width // 128):
                        i = nc.tensor.transpose(ps_t[:, 128 * h:128 * h + 128], x[:, 128 * h:128 * h + 128], ident)
                    i.then_inc(turned, 1)

                def turn_w(k, n, first, last):
                    for j in range(first, last):
                        i = nc.tensor.transpose(ps_g[n % 2][:, 128 * j:128 * j + 128],
                                                W[k][:, j // 2, 128 * (j % 2):128 * (j % 2) + 128], ident)
                    if last == 2 * B:
                        i.then_inc(wt_done, 1)

                def grad(t, n, b, x, y):
                    pe.wait_ge(mom_ready, t * 16 + 12 + 4 * (n - 1) + b + 1)
                    nc.tensor.matmul(grad_bank(b), x[:, b, :], y[:, :], start=True, stop=True).then_inc(grad_done, 1)

                for k, p in (("20", ps_a), ("21", ps_b)):
                    for h in range(2):
                        i = nc.tensor.transpose(p[:, 128 * h:128 * h + 128], sb["first" + k][:, 128 * h:128 * h + 128], ident)
                i.then_inc(first_turned, 1)
                pe.wait_ge(w_ready["21"], 4)
                with pe.Fori(0, T) as t:
                    for h, p in ((0, ps_h), (1, ps_t)):
                        pe.wait_ge(w_ready["20"], t * 2 + 3 + h)
                        for j in range(4):
                            i = nc.tensor.transpose(p[:, 128 * j:128 * j + 128],
                                                    W["20"][:, 2 * h + j // 2, 128 * (j % 2):128 * (j % 2) + 128], ident)
                        i.then_inc(wt_done, 1)
                    pe.wait_ge(kt_in, t + 1)
                    up(ps_a, kt, W["10"], lambda b: pe.wait_ge(w_ready["10"], t * 4 + b + 1))
                    pe.wait_ge(w_ready["21"], t * 2 + 4)
                    turn_w("21", X21, 0, 4)
                    pe.wait_ge(wt_ready, t * 4 + X20)
                    pe.wait_ge(gelu_ready, t * 2 + 1)
                    turn(g[0], 256)
                    turn_w("21", X21, 4, 6)
                    pe.wait_ge(gf_ready, t * 6 + TG0)
                    down(ps_h, gf[0], WT["20"])
                    turn_w("21", X21, 6, 8)
                    pe.wait_ge(chain, t * 6 + 6 + K_H1)
                    turn(h1, 128)
                    pe.wait_ge(w_ready["11"], t * 2 + 4)
                    pe.wait_ge(gf_ready, t * 6 + TH1)
                    up(ps_b, h1f, W["11"])
                    turn_w("11", X11, 0, 5)
                    pe.wait_ge(gelu_ready, t * 2 + 2)
                    turn(g[1], 256)
                    turn_w("11", X11, 5, 8)
                    pe.wait_ge(wt_ready, t * 4 + X21)
                    pe.wait_ge(gf_ready, t * 6 + TG1)
                    down(ps_h, gf[1], WT["21"])
                    pe.wait_ge(chain, t * 6 + 6 + K_DP)
                    turn(dp, 128)
                    pe.wait_ge(pre_ready, t * 4 + 2)
                    pe.wait_ge(gf_ready, t * 6 + TDP)
                    up(ps_a, dpf, W["21"])
                    pe.wait_ge(wt_ready, t * 4 + X11)
                    pe.wait_ge(dpm_ready, t + 1)
                    grad(t, G21, 0, dpm, g[1])
                    pe.wait_ge(chain, t * 6 + 6 + K_DA1)
                    turn(da[1], 256)
                    grad(t, G21, 1, dpm, g[1])
                    pe.wait_ge(gf_ready, t * 6 + TDA1)
                    down(ps_h, daf, WT["11"])
                    grad(t, G21, 2, dpm, g[1])
                    pe.wait_ge(chain, t * 6 + 6 + K_DH1)
                    turn(dh1, 128)
                    grad(t, G21, 3, dpm, g[1])
                    pe.wait_ge(pre_ready, t * 4 + 4)
                    pe.wait_ge(gf_ready, t * 6 + TDH1)
                    up(ps_b, dh1f, W["20"])
                    pe.wait_ge(h1m_ready, t + 1)
                    for b in range(B):
                        grad(t, G11, b, h1m, da[1])
                    pe.wait_ge(dh1m_ready, t + 1)
                    for b in range(B):
                        grad(t, G20, b, dh1m, g[0])
                    pe.wait_ge(km_ready, t + 1)
                    pe.wait_ge(chain, t * 6 + 6 + K_DA0)
                    for b in range(B):
                        grad(t, G10, b, km, da[0])


def read_out(nc, st, sb, inp):
    sem = lambda name: st.enter_context(nc.semaphore(name))
    with ExitStack() as ctx:
        def buf(name, shape):
            return ctx.enter_context(nc.sbuf_tensor("r_" + name, shape, F32))

        wf = {k: buf("wf" + k, [128, 256]) for k in PARAMS}
        g0, g1 = ([buf(f"g{l}{i}", [128, 1024]) for i in range(2)] for l in range(2))
        h1 = [buf(f"h1{i}", [128, 512]) for i in range(4)]
        z = [buf(f"z{i}", [128, 512]) for i in range(2)]
        bst = buf("bst", [128, NT, 6])
        ps_a0, ps_a1 = (ctx.enter_context(nc.psum_tensor("rp_a" + n, [128, 1024], F32)) for n in "01")
        ps_h, ps_z, ps_x = (ctx.enter_context(nc.psum_tensor("rp_" + n, [128, 512], F32)) for n in "hzx")
        wm = {k: buf("wm" + k, [128, 256]) for k in ("20", "21")}
        wm_turned, wt_copied = sem("r_wmt"), sem("r_wtc")
        wf_sum, wf_ready = sem("r_wfsum"), sem("r_wf")
        a0_done, h_done, a1_done, z_done, x_done = (sem("r_" + n) for n in ("a0", "h", "a1", "z", "x"))
        g0_ready, g1_ready, h_ready, z_ready = (sem("r_" + n) for n in ("g0r", "g1r", "hr", "zr"))
        x1_ready, st_ready, mv_ready = sem("r_x1"), sem("r_st"), sem("r_mv")
        N = B * S // 512
        order = ("10", "20", "11", "21")

        def q(n):
            return sb["qf"][:, n // 2, 16 * (n % 2):16 * (n % 2) + 16, :].rearrange("p t c -> p (t c)")

        with nc.Block() as block:
            @block.scalar
            def _(act):
                for k in range(N + 2):
                    if k < N:
                        act.wait_ge(a0_done, k + 1)
                        if k >= 2:
                            act.wait_ge(h_done, k - 1)
                        nc.scalar.activation(g0[k % 2][:, :], ps_a0[:, :], ACT.Gelu_apprx_tanh).then_inc(g0_ready, 1)
                    if k >= 2:
                        n = k - 2
                        act.wait_ge(a1_done, n + 1)
                        if n >= 2:
                            act.wait_ge(z_done, n - 1)
                        nc.scalar.activation(g1[n % 2][:, :], ps_a1[:, :], ACT.Gelu_apprx_tanh).then_inc(g1_ready, 1)

            @block.tensor
            def _(pe):
                ident = sb["cst"][:, C_ID:C_ID + 128]
                for i, k, p in ((2, "20", ps_z), (4, "21", ps_x)):
                    pe.wait_ge(wf_ready, i)
                    for h in range(2):
                        m = nc.tensor.transpose(p[:, 128 * h:128 * h + 128], wm[k][:, 128 * h:128 * h + 128], ident)
                    m.then_inc(wm_turned, 1)
                for k in range(N + 4):
                    if k < N:
                        pe.wait_ge(wf_ready, 1)
                        if k >= 1:
                            pe.wait_ge(g0_ready, k)
                        for h in range(2):
                            i = nc.tensor.matmul(ps_a0[:, 512 * h:512 * h + 512], wf["10"][:, 128 * h:128 * h + 128], q(k),
                                                 start=True, stop=True)
                        i.then_inc(a0_done, 1)
                    if 1 <= k <= N:
                        n = k - 1
                        pe.wait_ge(wt_copied, 1)
                        pe.wait_ge(g0_ready, n + 1)
                        if n >= 1:
                            pe.wait_ge(h_ready, n)
                        for h in range(2):
                            i = nc.tensor.matmul(ps_h[:, :], wf["20"][:, 128 * h:128 * h + 128], g0[n % 2][:, 512 * h:512 * h + 512],
                                                 start=h == 0, stop=h == 1)
                        i.then_inc(h_done, 1)
                    if 2 <= k <= N + 1:
                        n = k - 2
                        pe.wait_ge(wf_ready, 3)
                        pe.wait_ge(h_ready, n + 1)
                        if n >= 1:
                            pe.wait_ge(g1_ready, n)
                        for h in range(2):
                            i = nc.tensor.matmul(ps_a1[:, 512 * h:512 * h + 512], wf["11"][:, 128 * h:128 * h + 128], h1[n % 4][:, :],
                                                 start=True, stop=True)
                        i.then_inc(a1_done, 1)
                    if 3 <= k <= N + 2:
                        n = k - 3
                        pe.wait_ge(wt_copied, 2)
                        pe.wait_ge(g1_ready, n + 1)
                        if n >= 1:
                            pe.wait_ge(z_ready, n)
                        for h in range(2):
                            i = nc.tensor.matmul(ps_z[:, :], wf["21"][:, 128 * h:128 * h + 128], g1[n % 2][:, 512 * h:512 * h + 512],
                                                 start=h == 0, stop=h == 1)
                        i.then_inc(z_done, 1)
                    if 4 <= k:
                        n = k - 4
                        pe.wait_ge(z_ready, n + 1)
                        if n >= 1:
                            pe.wait_ge(x1_ready, n)
                        for i in range(4):
                            m = nc.tensor.transpose(ps_x[:, 128 * i:128 * i + 128], z[n % 2][:, 128 * i:128 * i + 128], ident)
                        m.then_inc(x_done, 1)

            @block.vector
            def _(dve):
                for i, k in enumerate(order):
                    w = wm.get(k, wf[k])
                    nc.vector.tensor_reduce(w[:, :], sb["w" + k][:, :, :].rearrange("p b n -> p n b"), AX.X, ALU.add).then_inc(wf_sum, 1)
                    dve.wait_ge(wf_sum, i + 1)
                    nc.vector.tensor_scalar(w[:, :], w[:, :], 1.0 / B, None, ALU.mult).then_inc(wf_ready, 1)
                    if k in wm:
                        dve.wait_ge(wm_turned, 1 if k == "20" else 2)
                        nc.vector.tensor_copy(wf[k][:, :], ps_z[:, 0:256] if k == "20" else ps_x[:, 0:256]).then_inc(wt_copied, 1)
                for k in range(1, N + 5):
                    if k <= N:
                        n = k - 1
                        dve.wait_ge(h_done, n + 1)
                        if n >= 4:
                            dve.wait_ge(a1_done, n - 3)
                            dve.wait_ge(z_ready, n - 3)
                        nc.vector.tensor_tensor(h1[n % 4][:, :], ps_h[:, :], q(n), ALU.add).then_inc(h_ready, 1)
                    if 3 <= k <= N + 2:
                        n = k - 3
                        dve.wait_ge(z_done, n + 1)
                        dve.wait_ge(h_ready, n + 1)
                        if n >= 2:
                            dve.wait_ge(x_done, n - 1)
                        nc.vector.tensor_tensor(z[n % 2][:, :], ps_z[:, :], h1[n % 4][:, :], ALU.add).then_inc(z_ready, 1)
                    if 4 <= k <= N + 3:
                        n = k - 4
                        dve.wait_ge(x_done, n + 1)
                        dve.wait_ge(sb["load_xb"], 16)
                        x1 = sb["x1"][:, 4 * n:4 * n + 4, :].rearrange("p t f -> p (t f)")
                        nc.vector.tensor_tensor(x1, ps_x[:, :], x1, ALU.add).then_inc(x1_ready, 1)
                    if 5 <= k:
                        n = k - 5
                        dve.wait_ge(x1_ready, n + 1)
                        for i in range(4):
                            m = nc.vector.bn_stats(bst[:, 4 * n + i, :], sb["x1"][:, 4 * n + i, :])
                        m.then_inc(st_ready, 1)
                        dve.wait_ge(st_ready, n + 1)
                        for i in range(4):
                            m = nc.vector.bn_aggr(sb["mv"][:, 4 * n + i, :], bst[:, 4 * n + i, :])
                        m.then_inc(mv_ready, 1)


def attend(nc, st, sb, inp):
    sem = lambda name: st.enter_context(nc.semaphore(name))
    HALF = WIN // 2
    QL, QN = WIN - 1, (WIN - 1) + S + WIN
    R = 6
    SPAN = S + WIN
    NTB = S // 128
    with ExitStack() as ctx:
        def buf(name, shape):
            return ctx.enter_context(nc.sbuf_tensor("t_" + name, shape, F32))

        xl = buf("xl", [128, NT, 128])
        xlf = buf("xlf", [128, NT * 128])
        xsh = buf("xsh", [128, B, NTB + 1, 128])
        wt, wx = buf("wt", [128, U]), buf("wx", [128, U])
        wa, bh, ba = buf("wa", [128, B]), buf("bh", [128, 1]), buf("ba", [128, 1])
        qp, kp = buf("qp", [128, QN]), buf("kp", [128, SPAN])
        hs = [buf(f"h{i}", [128, SPAN]) for i in range(R)]
        e = buf("e", [128, NTB, B, WIN])
        mx = buf("mx", [128, NTB * B])
        am = [buf(f"am{i}", [128, B, 160]) for i in range(2)]
        at1 = [buf(f"at1{i}", [128, 512]) for i in range(2)]
        at2 = [buf(f"at2{i}", [32, 512]) for i in range(2)]
        std, rstd = buf("std", [128, NT]), buf("rstd", [128, NT])
        bst = buf("bst", [128, NT, 6])
        ps = [ctx.enter_context(nc.psum_tensor(f"tp{i}", [128, 512], F32)) for i in range(6)]
        ps_e = ctx.enter_context(nc.psum_tensor("tp_e", [128, 1024], F32))

        load, load_wa, shifted = sem("t_load"), sem("t_loadwa"), sem("t_shift")
        cleared, wa_clear = sem("t_cleared"), sem("t_waclear")
        ve, std_ready, rstd_ready, xl_ready = sem("t_ve"), sem("t_std"), sem("t_rstd"), sem("t_xl")
        xl_turned, xlf_ready = sem("t_turn"), sem("t_xlf")
        qk_done, qk_ready = sem("t_qk"), sem("t_qkr")
        sum_ready = [sem("t_sumv"), sem("t_sump")]
        tanh_ready, e_done = sem("t_tanh"), sem("t_edone")
        soft, exp_ready = sem("t_soft"), sem("t_exp")
        am_ready, at_done, at_ready, v_done = sem("t_am"), sem("t_at"), sem("t_atr"), sem("t_v")
        x2_ready, st_ready, mv_ready = sem("t_x2"), sem("t_st"), sem("t_mv")

        def starts(j):
            s0 = j if j < HALF else j - WIN
            return s0, s0 - (HALF - 1)

        def on_pool(j):
            return j % 3 == 2

        def nth(j):
            return sum(on_pool(i) == on_pool(j) for i in range(j + 1))

        def add(ns, eng, j):
            if j >= R:
                eng.wait_ge(e_done, j - R + 1)
            s0, t0 = starts(j)
            nc_out = hs[j % R][:, :].rearrange("p (g i) -> p g i", i=WIN)
            qv = qp[:, QL + t0:QL + t0 + SPAN].rearrange("p (g i) -> p g i", i=WIN)
            k0 = HALF + s0
            kv = kp[:, k0:k0 + SPAN - WIN + 1:WIN].rearrange("p (g a) -> p g a", a=1).to_broadcast([128, SPAN // WIN, WIN])
            ns.tensor_tensor(nc_out, qv, kv, ALU.add).then_inc(sum_ready[on_pool(j)], 1)

        with nc.Block() as block:
            @block.sync
            def _(sp):
                sp.dma_start(wt[:, :], inp["L1_attn_Wt"]).then_inc(load, 16)
                sp.dma_start(wx[:, :], inp["L1_attn_Wx"]).then_inc(load, 16)
                for b in range(B):
                    sp.dma_start(bh[32 * b:32 * b + 32, :], inp["L1_attn_bh"].rearrange("(u a) -> u a", a=1)).then_inc(load, 16)
                sp.dma_start(ba[:, :], inp["L1_attn_ba"].partition_broadcast(128)).then_inc(load, 16)
                sp.wait_ge(wa_clear, 1)
                for b in range(B):
                    sp.dma_start(wa[32 * b:32 * b + 32, b:b + 1], inp["L1_attn_Wa"]).then_inc(load_wa, 16)
                sp.wait_ge(cleared, 2)
                for b in range(B):
                    sp.wait_ge(xl_ready, 8 * b + 8)
                    sp.dma_start(xsh[HALF:128, b, 0:NTB, :], xl[0:128 - HALF, 8 * b:8 * b + 8, :]).then_inc(shifted, 16)
                    sp.dma_start(xsh[0:HALF, b, 1:NTB + 1, :], xl[128 - HALF:128, 8 * b:8 * b + 8, :]).then_inc(shifted, 16)

            @block.gpsimd
            def _(pool):
                nc.gpsimd.memset(wa[:, :], 0.0).then_inc(wa_clear, 1)
                nc.gpsimd.memset(xsh[:, :, 0, :], 0.0).then_inc(cleared, 1)
                nc.gpsimd.memset(xsh[:, :, NTB, :], 0.0).then_inc(cleared, 1)
                nc.gpsimd.memset(qp[:, :], 0.0).then_inc(cleared, 1)
                nc.gpsimd.memset(kp[:, :], 0.0).then_inc(cleared, 1)
                pool.wait_ge(qk_ready, 2)
                for j in range(WIN):
                    if on_pool(j):
                        add(nc.gpsimd, pool, j)

            @block.scalar
            def _(act):
                act.wait_ge(ve, 1)
                nc.scalar.activation(std[:, :], std[:, :], ACT.Sqrt).then_inc(std_ready, 1)
                for g in range(NT // 4):
                    act.wait_ge(xl_turned, g + 1)
                    nc.scalar.copy(xlf[:, 512 * g:512 * g + 512], ps[g % 2][:, :]).then_inc(xlf_ready, 1)
                act.wait_ge(cleared, 4)
                act.wait_ge(load, 16 * 7)
                for h in range(2):
                    act.wait_ge(qk_done, 2 * h + 1)
                    nc.scalar.activation(qp[:, QL + 512 * h:QL + 512 * h + 512], ps[2 + h][:, :], ACT.Identity, bias=bh[:, 0:1])
                    act.wait_ge(qk_done, 2 * h + 2)
                    nc.scalar.copy(kp[:, HALF + 512 * h:HALF + 512 * h + 512], ps[4 + h][:, :]).then_inc(qk_ready, 1)
                for j in range(WIN):
                    act.wait_ge(sum_ready[on_pool(j)], nth(j))
                    t0 = -starts(j)[1]
                    nc.scalar.activation(hs[j % R][:, t0:t0 + S], hs[j % R][:, t0:t0 + S], ACT.Tanh).then_inc(tanh_ready, 1)
                act.wait_ge(soft, 3)
                nc.scalar.activation(e[:, :, :, :], e[:, :, :, :], ACT.Exp).then_inc(exp_ready, 1)
                for n in range(NTB):
                    act.wait_ge(at_done, n + 1)
                    if n >= 2:
                        act.wait_ge(v_done, n - 1)
                    nc.scalar.copy(at1[n % 2][:, :], ps[n % 2][:, :])
                    nc.scalar.copy(at2[n % 2][:, :], ps[2 + n % 2][0:32, :]).then_inc(at_ready, 1)

            @block.tensor
            def _(pe):
                ident = sb["cst"][:, C_ID:C_ID + 128]
                for g in range(NT // 4):
                    pe.wait_ge(xl_ready, 4 * g + 4)
                    if g >= 2:
                        pe.wait_ge(xlf_ready, g - 1)
                    for i in range(4):
                        m = nc.tensor.transpose(ps[g % 2][:, 128 * i:128 * i + 128], xl[:, 4 * g + i, :], ident)
                    m.then_inc(xl_turned, 1)
                pe.wait_ge(load, 16 * 7)
                pe.wait_ge(xlf_ready, NT // 4)
                for h in range(2):
                    for w, o in ((wt, 2), (wx, 4)):
                        for b in range(B):
                            m = nc.tensor.matmul(ps[o + h][32 * b:32 * b + 32, :], w[:, :], xlf[:, 1024 * b + 512 * h:1024 * b + 512 * h + 512],
                                                 start=True, stop=True)
                        m.then_inc(qk_done, 1)
                pe.wait_ge(load_wa, 16 * B)
                for j in range(WIN):
                    pe.wait_ge(tanh_ready, j + 1)
                    t0 = -starts(j)[1]
                    jj = (j + HALF) % WIN
                    for n in range(NTB):
                        m = nc.tensor.matmul(ps_e[:, 128 * n + jj:128 * n + jj + 3 * WIN + 1:WIN], hs[j % R][:, t0 + 128 * n:t0 + 128 * n + 128],
                                             wa[:, :], start=True, stop=True)
                    m.then_inc(e_done, 1)
                pe.wait_ge(shifted, 16 * 2 * B)
                pe.wait_ge(qk_ready, 2)
                for k in range(NTB + 1):
                    if k < NTB:
                        n = k
                        pe.wait_ge(am_ready, n + 1)
                        if n >= 2:
                            pe.wait_ge(at_ready, n - 1)
                        for b in range(B):
                            nc.tensor.transpose(ps[n % 2][:, 128 * b:128 * b + 128], am[n % 2][:, b, 0:128], ident)
                        for b in range(B):
                            m = nc.tensor.transpose(ps[2 + n % 2][0:32, 128 * b:128 * b + 128], am[n % 2][:, b, 128:160], ident)
                        m.then_inc(at_done, 1)
                    if k >= 1:
                        n = k - 1
                        pe.wait_ge(at_ready, n + 1)
                        if n >= 2:
                            pe.wait_ge(x2_ready, n - 1)
                        for b in range(B):
                            nc.tensor.matmul(ps[4 + n % 2][:, 128 * b:128 * b + 128], at1[n % 2][:, 128 * b:128 * b + 128],
                                             xsh[:, b, n, :], start=True, stop=False)
                            m = nc.tensor.matmul(ps[4 + n % 2][:, 128 * b:128 * b + 128], at2[n % 2][:, 128 * b:128 * b + 128],
                                                 xsh[0:32, b, n + 1, :], start=False, stop=True)
                        m.then_inc(v_done, 1)

            @block.vector
            def _(dve):
                mv = sb["mv"]
                nc.vector.tensor_scalar(std[:, :], mv[:, :, 1], 1e-5, None, ALU.add).then_inc(ve, 1)
                dve.wait_ge(std_ready, 1)
                nc.vector.reciprocal(rstd[:, :], std[:, :]).then_inc(rstd_ready, 1)
                dve.wait_ge(rstd_ready, 1)
                for n in range(NT):
                    nc.vector.tensor_scalar(xl[:, n, :], sb["x1"][:, n, :], mv[:, n, 0:1], rstd[:, n:n + 1],
                                            ALU.subtract, ALU.mult).then_inc(xl_ready, 1)
                dve.wait_ge(qk_ready, 2)
                for j in range(WIN):
                    if not on_pool(j):
                        add(nc.vector, dve, j)
                dve.wait_ge(e_done, WIN)
                edge = sb["cst"][:, C_EDGE:C_EDGE + NTB * WIN].rearrange("p (n j) -> p n j", j=WIN)
                pe_ = ps_e[:, :].rearrange("p (n b j) -> p n b j", n=NTB, b=B)
                for b in range(B):
                    m = nc.vector.scalar_tensor_tensor(out=e[:, :, b, :], in0=pe_[:, :, b, :], scalar=ba[:, 0:1], in1=edge,
                                                       op0=ALU.add, op1=ALU.add)
                m.then_inc(soft, 1)
                dve.wait_ge(soft, 1)
                er = e[:, :, :, :].rearrange("p n b j -> p (n b) j")
                bc = mx[:, :].rearrange("p (n a) -> p n a", a=1).to_broadcast([128, NTB * B, WIN])
                nc.vector.tensor_reduce(mx[:, :], er, AX.X, ALU.max).then_inc(soft, 1)
                dve.wait_ge(soft, 2)
                nc.vector.tensor_tensor(er, er, bc, ALU.subtract).then_inc(soft, 1)
                dve.wait_ge(exp_ready, 1)
                nc.vector.tensor_reduce(mx[:, :], er, AX.X, ALU.add).then_inc(soft, 1)
                dve.wait_ge(soft, 4)
                nc.vector.reciprocal(mx[:, :], mx[:, :]).then_inc(soft, 1)
                dve.wait_ge(soft, 5)
                nc.vector.tensor_tensor(er, er, bc, ALU.mult).then_inc(soft, 1)
                dve.wait_ge(soft, 6)
                band = sb["cst"][:, C_BAND:C_BAND + 160].rearrange("p (r j) -> p r j", j=WIN)
                x1v = sb["x1"][:, :, :].rearrange("p (b n) f -> p b n f", b=B)
                for k in range(NTB + 2):
                    if k < NTB:
                        if k >= 2:
                            dve.wait_ge(at_done, k - 1)
                        for b in range(B):
                            m = nc.vector.tensor_tensor(am[k % 2][:, b, :].rearrange("p (r j) -> p r j", j=WIN),
                                                        e[:, k, b:b + 1, :].to_broadcast([128, 5, WIN]), band, ALU.mult)
                        m.then_inc(am_ready, 1)
                    if k >= 2:
                        n = k - 2
                        dve.wait_ge(v_done, n + 1)
                        nc.vector.tensor_tensor(x1v[:, :, n, :], ps[4 + n % 2][:, :].rearrange("p (b f) -> p b f", b=B),
                                                x1v[:, :, n, :], ALU.add).then_inc(x2_ready, 1)
                dve.wait_ge(x2_ready, NTB)
                for n in range(NT):
                    m = nc.vector.bn_stats(bst[:, n, :], sb["x1"][:, n, :])
                m.then_inc(st_ready, 1)
                dve.wait_ge(st_ready, 1)
                for n in range(NT):
                    m = nc.vector.bn_aggr(mv[:, n, :], bst[:, n, :])
                m.then_inc(mv_ready, 1)


def experts(nc, st, sb, inp, out):
    sem = lambda name: st.enter_context(nc.semaphore(name))
    NH = H // 128
    with ExitStack() as ctx:
        def buf(name, shape, dt=F32):
            return ctx.enter_context(nc.sbuf_tensor("f_" + name, shape, dt))

        def split(name, shape):
            return [buf(name + part, shape, BF16) for part in ("_hi", "_lo")]

        std, r1, v2, s2, r12 = (buf(n, [128, NT]) for n in ("std", "r1", "v2", "s2", "r12"))
        xn = buf("xn", [128, 4, 128])
        xnf = buf("xnf", [128, NT * 128])
        wr, br = buf("wr", [128, E]), buf("br", [128, E])
        lg, key, sel, ex, lg2 = (buf(n, [128, NT, E]) for n in ("lg", "key", "sel", "ex", "lg2"))
        m1, mk = buf("m1", [128, NT]), buf("mk", [128, NT])
        wt8 = buf("wt8", [E, NT * 128])
        b2 = buf("b2", [E, 128])
        NROW = 2 * E + E * NH
        rowp, colp = buf("rowp", [NROW, 128]), buf("colp", [128, NROW])
        lng, lnb, b1t = colp[:, 0:E], colp[:, E:2 * E], colp[:, 2 * E:NROW].rearrange("p (e h) -> p e h", h=NH)
        w1 = [buf(f"w1{i}", [128, H]) for i in range(2)]
        w1g = [buf(f"w1g{i}", [128, H]) for i in range(2)]
        w1s, w2s = [split(f"w1s{i}", [128, H]) for i in range(2)], [split(f"w2s{i}", [128, NH, 128]) for i in range(2)]
        xs = split("xs", [128, NT * 128])
        hs = [split(f"hs{i}", [128, NH, 512]) for i in range(2)]
        w2 = [buf(f"w2{i}", [128, NH, 128]) for i in range(2)]
        hb = [buf(f"hb{i}", [128, NH]) for i in range(2)]
        hh = [buf(f"hh{i}", [128, NH, 512]) for i in range(2)]
        PRODUCTS = ((0, 0), (0, 1), (1, 0))
        ps_h = [ctx.enter_context(nc.psum_tensor(f"fp_h{i}", [128, 512], F32)) for i in range(4)]
        ps_y = [ctx.enter_context(nc.psum_tensor(f"fp_y{i}", [128, 512], F32)) for i in range(2)]
        ps_r, ps_b = (ctx.enter_context(nc.psum_tensor("fp_" + n, [128, 512], F32)) for n in "rb")
        x_hi, x_lo, w_hi, w_lo, h_hi, h_lo = (sem("f_" + n) for n in ("xhi", "xlo", "whi", "wlo", "hhi", "hlo"))
        load, load_w, stored = sem("f_load"), [sem("f_lw0"), sem("f_lw1")], sem("f_out")
        nrm, sq1 = sem("f_nrm"), sem("f_sq")
        xn_ready, xn_turned, xnf_ready = sem("f_xn"), sem("f_turn"), sem("f_xnf")
        lg_done, rt, ex_ready = sem("f_lg"), sem("f_rt"), sem("f_ex")
        wt_done, wt_ready, bt_done, bt_used = sem("f_wt"), sem("f_wtr"), sem("f_bt"), sem("f_btu")
        w_ready, hb_done, hb_ready = sem("f_w"), sem("f_hbd"), sem("f_hb")
        h_done, h_ready, y_done, y_used = sem("f_h"), sem("f_hr"), sem("f_y"), sem("f_yu")
        col_done, col_ready = sem("f_cold"), sem("f_col")
        NCH = S * B // 512
        NN = E * NCH

        with nc.Block() as block:
            @block.sync
            def _(sp):
                sp.dma_start(wr[:, :], inp["L1_ffn_Wr"]).then_inc(load, 16)
                sp.dma_start(br[:, :], inp["L1_ffn_br"].partition_broadcast(128)).then_inc(load, 16)
                sp.dma_start(b2[:, :], inp["L1_ffn_b2"]).then_inc(load, 16)
                sp.dma_start(rowp[0:E, :], inp["L1_ffn_ln_g"]).then_inc(load, 16)
                sp.dma_start(rowp[E:2 * E, :], inp["L1_ffn_ln_b"]).then_inc(load, 16)
                sp.dma_start(rowp[2 * E:NROW, :], inp["L1_ffn_b1"].rearrange("e (h p) -> (e h) p", p=128)).then_inc(load, 16)
                for e in range(E):
                    if e >= 2:
                        sp.wait_ge(w_lo, 2 * (e - 1))
                        sp.wait_ge(hb_done, e - 1)
                    sp.dma_start(w1[e % 2][:, :], inp["L1_ffn_W1"][e]).then_inc(load_w[e % 2], 16)
                    sp.dma_start(w2[e % 2][:, :, :], inp["L1_ffn_W2"][e].rearrange("(h p) d -> p h d", p=128)).then_inc(load_w[e % 2], 16)
                ov = out.rearrange("b t c d -> (b t c) d").rearrange("(n p) d -> p n d", p=128)
                for n in range(NCH):
                    sp.wait_ge(y_used, 4 * (NN - NCH + n + 1))
                    sp.dma_start(ov[:, 4 * n:4 * n + 4, :], sb["x1"][:, 4 * n:4 * n + 4, :]).then_inc(stored, 16)
                sp.wait_ge(stored, 16 * NCH)

            @block.scalar
            def _(act):
                act.wait_ge(nrm, 1)
                nc.scalar.activation(std[:, :], std[:, :], ACT.Sqrt).then_inc(sq1, 1)
                act.wait_ge(nrm, 5)
                nc.scalar.activation(s2[:, :], v2[:, :], ACT.Sqrt).then_inc(sq1, 1)
                for g in range(NT // 4):
                    act.wait_ge(xn_turned, g + 1)
                    nc.scalar.copy(xnf[:, 512 * g:512 * g + 512], ps_y[g % 2][:, :]).then_inc(xnf_ready, 1)
                    act.wait_ge(xnf_ready, g + 1)
                    nc.scalar.copy(xs[0][:, 512 * g:512 * g + 512], xnf[:, 512 * g:512 * g + 512]).then_inc(x_hi, 1)
                act.wait_ge(rt, 12)
                nc.scalar.activation(ex[:, :, :], ex[:, :, :], ACT.Exp).then_inc(ex_ready, 1)
                for g in range(NT // 4):
                    act.wait_ge(wt_done, g + 1)
                    nc.scalar.copy(wt8[:, 512 * g:512 * g + 512], ps_y[g % 2][0:E, :]).then_inc(wt_ready, 1)
                for n in range(NN):
                    e = n // NCH
                    act.wait_ge(hb_ready, e + 1)
                    if n >= 2:
                        act.wait_ge(h_lo, 2 * (n - 1))
                    for h in range(NH):
                        act.wait_ge(h_done, NH * n + h + 1)
                        nc.scalar.activation(hh[n % 2][:, h, :], ps_h[h][:, :], ACT.Gelu, bias=hb[e % 2][:, h:h + 1]).then_inc(h_ready, 1)
                    if n >= 2:
                        act.wait_ge(y_done, n - 1)
                    for a in range(2):
                        act.wait_ge(h_ready, NH * n + 2 * a + 2)
                        nc.scalar.copy(hs[n % 2][0][:, 2 * a:2 * a + 2, :], hh[n % 2][:, 2 * a:2 * a + 2, :]).then_inc(h_hi, 1)

            @block.gpsimd
            def _(pool):
                for e in range(E):
                    pool.wait_ge(w_ready, e + 1)
                    pool.wait_ge(load_w[e % 2], 32 * (e // 2 + 1))
                    if e >= 2:
                        pool.wait_ge(y_done, NCH * (e - 1))
                    for i, (w, ws) in enumerate(((w1g, w1s), (w2, w2s))):
                        w, (hi, lo) = w[e % 2], ws[e % 2]
                        w, hi, lo = (x[(slice(None),) * (2 + i)] for x in (w, hi, lo))
                        nc.gpsimd.tensor_copy(hi, w).then_inc(w_hi, 1)
                        pool.wait_ge(w_hi, 2 * e + i + 1)
                        nc.gpsimd.tensor_tensor(lo, w, hi, ALU.subtract).then_inc(w_lo, 1)

            @block.tensor
            def _(pe):
                ident = sb["cst"][:, C_ID:C_ID + 128]
                pe.wait_ge(load, 96)
                nc.tensor.transpose(ps_b[:, 0:NROW], rowp[:, :], ident[0:NROW, 0:NROW]).then_inc(col_done, 1)
                for g in range(NT // 4):
                    if g >= 2:
                        pe.wait_ge(xnf_ready, g - 1)
                    for i in range(4):
                        pe.wait_ge(xn_ready, 4 * g + i + 1)
                        m = nc.tensor.transpose(ps_y[g % 2][:, 128 * i:128 * i + 128], xn[:, i, :], ident)
                        m.then_inc(sb["xn_used"], 1) if i < 3 else m.then_inc(xn_turned, 1)
                pe.wait_ge(xnf_ready, NT // 4)
                pe.wait_ge(load, 96)
                for n in range(NT):
                    m = nc.tensor.matmul(ps_r[:, E * n:E * n + E], xnf[:, 128 * n:128 * n + 128], wr[:, :], start=True, stop=True)
                m.then_inc(lg_done, 1)
                pe.wait_ge(rt, 16)
                for g in range(NT // 4):
                    if g >= 2:
                        pe.wait_ge(wt_ready, g - 1)
                    for i in range(4):
                        m = nc.tensor.transpose(ps_y[g % 2][0:E, 128 * i:128 * i + 128], sel[:, 4 * g + i, :], ident)
                    m.then_inc(wt_done, 1)
                for g in range(NT // 4):
                    pe.wait_ge(wt_ready, g + 1)
                    if g >= 1:
                        pe.wait_ge(bt_used, g)
                    for i in range(4):
                        n = 4 * g + i
                        m = nc.tensor.matmul(ps_b[:, 128 * i:128 * i + 128], wt8[:, 128 * n:128 * n + 128], b2[:, :], start=True, stop=True)
                    m.then_inc(bt_done, 1)
                pe.wait_ge(bt_used, NT // 4)
                for k in range(NN + 1):
                    if k < NN:
                        n, e = k, k // NCH
                        if n % NCH == 0:
                            pe.wait_ge(load_w[e % 2], 32 * (e // 2 + 1))
                            pe.wait_ge(col_ready, 1)
                            if e >= 1:
                                pe.wait_ge(hb_ready, e)
                            for h in range(NH):
                                m = nc.tensor.matmul(ps_r[:, h:h + 1], w1[e % 2][:, 128 * h:128 * h + 128], lnb[:, e:e + 1], start=True, stop=True)
                            m.then_inc(hb_done, 1)
                            pe.wait_ge(w_lo, 2 * e + 1)
                        if e == 0:
                            pe.wait_ge(x_lo, n + 1)
                        for h in range(NH):
                            if n >= 1:
                                pe.wait_ge(h_ready, NH * (n - 1) + h + 1)
                            for i, (a, c) in enumerate(PRODUCTS):
                                m = nc.tensor.matmul(ps_h[h][:, :], w1s[e % 2][a][:, 128 * h:128 * h + 128],
                                                     xs[c][:, 512 * (n % NCH):512 * (n % NCH) + 512], start=i == 0, stop=i == 2)
                            m.then_inc(h_done, 1)
                    if k >= 1:
                        n, e = k - 1, (k - 1) // NCH
                        pe.wait_ge(w_lo, 2 * e + 2)
                        pe.wait_ge(h_lo, 2 * (n + 1))
                        if n >= 2:
                            pe.wait_ge(y_used, 4 * (n - 1))
                        for i in range(4):
                            for h in range(NH):
                                for j, (a, c) in enumerate(PRODUCTS):
                                    m = nc.tensor.matmul(ps_y[n % 2][:, 128 * i:128 * i + 128], hs[n % 2][a][:, h, 128 * i:128 * i + 128],
                                                         w2s[e % 2][c][:, h, :], start=(h, j) == (0, 0), stop=(h, j) == (NH - 1, 2))
                        m.then_inc(y_done, 1)

            @block.vector
            def _(dve):
                mv = sb["mv"]
                nc.vector.tensor_scalar(std[:, :], mv[:, :, 1], 1e-5, None, ALU.add).then_inc(nrm, 1)
                dve.wait_ge(sq1, 1)
                nc.vector.reciprocal(r1[:, :], std[:, :]).then_inc(nrm, 1)
                dve.wait_ge(nrm, 2)
                nc.vector.tensor_tensor(v2[:, :], r1[:, :], r1[:, :], ALU.mult).then_inc(nrm, 1)
                dve.wait_ge(nrm, 3)
                nc.vector.tensor_tensor(v2[:, :], v2[:, :], mv[:, :, 1], ALU.mult).then_inc(nrm, 1)
                dve.wait_ge(nrm, 4)
                nc.vector.tensor_scalar(v2[:, :], v2[:, :], 1e-5, None, ALU.add).then_inc(nrm, 1)
                dve.wait_ge(sq1, 2)
                nc.vector.reciprocal(r12[:, :], s2[:, :]).then_inc(nrm, 1)
                dve.wait_ge(nrm, 6)
                nc.vector.tensor_tensor(r12[:, :], r12[:, :], r1[:, :], ALU.mult).then_inc(nrm, 1)
                dve.wait_ge(nrm, 7)
                for n in range(NT):
                    if n >= 4:
                        g, i = (n - 4) // 4, (n - 4) % 4
                        if i < 3:
                            dve.wait_ge(sb["xn_used"], 3 * g + i + 1)
                        else:
                            dve.wait_ge(xn_turned, g + 1)
                    nc.vector.tensor_scalar(xn[:, n % 4, :], sb["x1"][:, n, :], mv[:, n, 0:1], r12[:, n:n + 1],
                                            ALU.subtract, ALU.mult).then_inc(xn_ready, 1)
                for g in range(NT // 4):
                    dve.wait_ge(x_hi, g + 1)
                    nc.vector.tensor_tensor(xs[1][:, 512 * g:512 * g + 512], xnf[:, 512 * g:512 * g + 512],
                                            xs[0][:, 512 * g:512 * g + 512], ALU.subtract).then_inc(x_lo, 1)
                dve.wait_ge(col_done, 1)
                nc.vector.tensor_copy(colp[:, :], ps_b[:, 0:NROW]).then_inc(col_ready, 1)
                dve.wait_ge(col_ready, 1)
                step = [0]

                def link(i):
                    step[0] += 1
                    i.then_inc(rt, 1)
                    dve.wait_ge(rt, step[0])

                def per_tile(v):
                    return v.rearrange("p (n a) -> p n a", a=1).to_broadcast([128, NT, E])

                def per_expert(v):
                    return v.rearrange("p (a e) -> p a e", a=1).to_broadcast([128, NT, E])

                rank = per_expert(sb["cst"][:, C_RANK:C_RANK + E])
                dve.wait_ge(lg_done, 1)
                link(nc.vector.tensor_tensor(lg[:, :, :], ps_r[:, 0:NT * E].rearrange("p (n e) -> p n e", e=E), per_tile(s2[:, :]), ALU.mult))
                link(nc.vector.tensor_tensor(lg[:, :, :], lg[:, :, :], per_expert(br[:, :]), ALU.add))
                link(nc.vector.tensor_reduce(m1[:, :], lg[:, :, :], AX.X, ALU.max))
                link(nc.vector.tensor_tensor(key[:, :, :], lg[:, :, :], per_tile(m1[:, :]), ALU.is_ge))
                link(nc.vector.tensor_tensor(key[:, :, :], key[:, :, :], rank, ALU.mult))
                link(nc.vector.tensor_reduce(mk[:, :], key[:, :, :], AX.X, ALU.max))
                link(nc.vector.tensor_tensor(sel[:, :, :], key[:, :, :], per_tile(mk[:, :]), ALU.is_ge))
                link(nc.vector.scalar_tensor_tensor(out=lg2[:, :, :], in0=sel[:, :, :], scalar=-3.0e38, in1=lg[:, :, :],
                                                    op0=ALU.mult, op1=ALU.add))
                link(nc.vector.tensor_reduce(mk[:, :], lg2[:, :, :], AX.X, ALU.max))
                link(nc.vector.tensor_tensor(key[:, :, :], lg2[:, :, :], per_tile(mk[:, :]), ALU.is_ge))
                link(nc.vector.tensor_tensor(key[:, :, :], key[:, :, :], rank, ALU.mult))
                link(nc.vector.tensor_tensor(ex[:, :, :], lg[:, :, :], per_tile(m1[:, :]), ALU.subtract))
                link(nc.vector.tensor_reduce(mk[:, :], key[:, :, :], AX.X, ALU.max))
                link(nc.vector.tensor_tensor(key[:, :, :], key[:, :, :], per_tile(mk[:, :]), ALU.is_ge))
                link(nc.vector.tensor_tensor(sel[:, :, :], sel[:, :, :], key[:, :, :], ALU.add))
                dve.wait_ge(ex_ready, 1)
                step2 = [0]
                def link2(i):
                    step2[0] += 1
                    i.then_inc(sb["f_w2"], 1)
                    dve.wait_ge(sb["f_w2"], step2[0])
                link2(nc.vector.tensor_tensor(ex[:, :, :], ex[:, :, :], sel[:, :, :], ALU.mult))
                link2(nc.vector.tensor_reduce(m1[:, :], ex[:, :, :], AX.X, ALU.add))
                link2(nc.vector.reciprocal(m1[:, :], m1[:, :]))
                nc.vector.tensor_tensor(sel[:, :, :], ex[:, :, :], per_tile(m1[:, :]), ALU.mult).then_inc(rt, 1)
                dve.wait_ge(load, 96)
                for g in range(NT // 4):
                    dve.wait_ge(bt_done, g + 1)
                    x = sb["x1"][:, 4 * g:4 * g + 4, :].rearrange("p n f -> p (n f)")
                    nc.vector.tensor_tensor(x, ps_b[:, :], x, ALU.add).then_inc(bt_used, 1)

                def prepare_w(e):
                    if e >= 2:
                        dve.wait_ge(w_lo, 2 * (e - 1))
                    dve.wait_ge(load_w[e % 2], 32 * (e // 2 + 1))
                    nc.vector.tensor_scalar(w1g[e % 2][:, :], w1[e % 2][:, :], lng[:, e:e + 1], None, ALU.mult).then_inc(w_ready, 1)

                def prepare_b(e):
                    dve.wait_ge(hb_done, e + 1)
                    nc.vector.tensor_tensor(hb[e % 2][:, :], ps_r[:, 0:NH], b1t[:, e, :], ALU.add).then_inc(hb_ready, 1)

                prepare_w(0)
                for k in range(NN + 1):
                    if k % NCH == 0 and k < NN:
                        prepare_b(k // NCH)
                    if k < NN:
                        if k >= 2:
                            dve.wait_ge(y_done, k - 1)
                        for a in range(2):
                            dve.wait_ge(h_hi, 2 * k + a + 1)
                            nc.vector.tensor_tensor(hs[k % 2][1][:, 2 * a:2 * a + 2, :], hh[k % 2][:, 2 * a:2 * a + 2, :],
                                                    hs[k % 2][0][:, 2 * a:2 * a + 2, :], ALU.subtract).then_inc(h_lo, 1)
                    if k == 0:
                        continue
                    n = k - 1
                    e = n // NCH
                    if n % NCH == 1 and e + 1 < E:
                        prepare_w(e + 1)
                    dve.wait_ge(y_done, n + 1)
                    if n >= NCH:
                        dve.wait_ge(y_used, 4 * (n - NCH + 1))
                    for i in range(4):
                        j = 4 * (n % NCH) + i
                        nc.vector.scalar_tensor_tensor(out=sb["x1"][:, j, :], in0=ps_y[n % 2][:, 128 * i:128 * i + 128],
                                                       scalar=sel[:, j, e:e + 1], in1=sb["x1"][:, j, :],
                                                       op0=ALU.mult, op1=ALU.add).then_inc(y_used, 1)


def build(nc, inp, consts, out, stop=None, dbg=None):
    with ExitStack() as st:
        sb = {}

        def alloc(name, shape, dt=F32, stack=st):
            sb[name] = stack.enter_context(nc.sbuf_tensor("s_" + name, shape, dt))

        alloc("cst", [128, C_ALL])
        alloc("x1", [128, NT, 128])
        alloc("mv", [128, NT, 2])
        sb["load_xb"] = st.enter_context(nc.semaphore("load_xb"))
        mem = st.enter_context(ExitStack())
        alloc("qf", [128, B, T, C], stack=mem)
        for k in ("10", "20", "11", "21"):
            alloc("w" + k, [128, B, 256], stack=mem)
            alloc("first" + k, [128, 256], stack=mem)
        steps = mem.enter_context(ExitStack())
        alloc("kf", [128, T + 1, 128], stack=steps)
        alloc("vs", [128, T, 128], stack=steps)
        alloc("ktok", [128, T, 128], stack=steps)
        alloc("coef", [128, T, 9], stack=steps)
        prepare(nc, st, sb, inp, consts)
        if stop == 0:
            dump(nc, st, sb, dbg)
            return
        learn(nc, st, sb)
        if stop == 1:
            dump(nc, st, sb, dbg)
            return
        steps.close()
        read_out(nc, st, sb, inp)
        mem.close()
        if stop == 2:
            dump(nc, st, sb, dbg)
            return
        attend(nc, st, sb, inp)
        if stop == 3:
            dump(nc, st, sb, dbg)
            return
        sb["xn_used"] = st.enter_context(nc.semaphore("f_xnu"))
        sb["f_w2"] = st.enter_context(nc.semaphore("f_wsum"))
        experts(nc, st, sb, inp, out)


_INS = ['x', 'L0_conv_Wq', 'L0_conv_Wk', 'L0_conv_Wv', 'L0_conv_w_lr', 'L0_conv_w_forget', 'L0_conv_w_eta',
        'L0_conv_w1_0', 'L0_conv_w2_0', 'L0_conv_w1_1', 'L0_conv_w2_1', 'L1_attn_Wt', 'L1_attn_Wx', 'L1_attn_bh',
        'L1_attn_Wa', 'L1_attn_ba', 'L1_ffn_Wr', 'L1_ffn_br', 'L1_ffn_ln_g', 'L1_ffn_ln_b', 'L1_ffn_W1', 'L1_ffn_b1',
        'L1_ffn_W2', 'L1_ffn_b2']


def shape_constants():
    import numpy as np
    c = np.zeros((128, C_ALL), np.float32)
    p = np.arange(128)
    c[:, C_ID:C_ID + 128] = np.eye(128)
    c[:, C_MEAN:C_MEAN + 128] = (p[:, None] // C == p[None] // C) / C
    c[:, C_GRP:C_GRP + 128] = (p[:, None] // 4 == p[None] // 4) / 4
    w = np.arange(128 + WIN)
    c[:, C_BAND:C_BAND + 128 + WIN] = (w[None] >= p[:, None]) & (w[None] < p[:, None] + WIN)
    for n in range(S // 128):
        for j in range(WIN):
            key = 128 * n - WIN // 2 + p + (j - p) % WIN
            c[:, C_EDGE + WIN * n + j] = np.where((key < 0) | (key >= S), -10000.0, 0.0)
    c[:, C_RANK:C_RANK + E] = E - np.arange(E)
    for b in range(B):
        c[:, C_SEL + 128 * b:C_SEL + 128 * b + 128] = (p[:, None] // C == b) / C
    return c


def kernel(**inputs):
    import numpy as _np
    import concourse.bacc as _bacc
    from concourse import mybir as _mybir
    from concourse.bass_utils import run_bass_kernel_spmd as _run

    nc = _bacc.Bacc("TRN2", target_bir_lowering=False, num_devices=1)
    arrays, aps = {}, {}
    for name in _INS:
        a = _np.ascontiguousarray(inputs[name])
        arrays[f"in_{name}_dram"] = a
        aps[name] = nc.dram_tensor(f"in_{name}_dram", a.shape, _mybir.dt.from_np(a.dtype), kind="ExternalInput").ap()
    c = shape_constants()
    arrays["in_constants_dram"] = c
    consts = nc.dram_tensor("in_constants_dram", c.shape, _mybir.dt.float32, kind="ExternalInput").ap()
    out = nc.dram_tensor("out_0_dram", (B, T, C, D), _mybir.dt.float32, kind="ExternalOutput").ap()
    build(nc, aps, consts, out)
    r = _run(nc, [arrays], core_ids=[0])
    return r.results[0]["out_0_dram"]
```

```python
from contextlib import ExitStack

import concourse.bass as bass
from concourse import mybir

F32 = mybir.dt.float32
BF16 = mybir.dt.bfloat16
ALU = mybir.AluOpType
ACT = mybir.ActivationFunctionType
AX = mybir.AxisListType

B, T, C, D = 4, 32, 32, 128
S = T * C
NT = B * S // 128
DE = 256
NC_E = DE // 128
U = 32
WIN = 32
E = 8
H = 512
MAX_LR = 0.1
GELU_C = 0.7978845608028654
GELU_A = 0.044715
C_ID, C_MEAN, C_GRP, C_BAND, C_EDGE, C_RANK, C_SEL = 0, 128, 256, 384, 544, 800, 808
C_ALL = C_SEL + 512


PARAMS = ("21", "11", "10", "20")


def prepare(nc, st, sb, inp, consts):
    sem = lambda name: st.enter_context(nc.semaphore(name))
    NP = 3 * D + 3
    CH = 8
    NCK = T // CH
    with ExitStack() as ctx:
        xs = ctx.enter_context(nc.sbuf_tensor("xs", [128, T, 128], F32))
        xf = ctx.enter_context(nc.sbuf_tensor("xf", [128, T, B, C], F32))
        xg = ctx.enter_context(nc.sbuf_tensor("xg", [128, T, B, C], F32))
        proj = ctx.enter_context(nc.sbuf_tensor("proj", [128, T, NP], F32))
        wcat = ctx.enter_context(nc.sbuf_tensor("wcat", [128, NP], F32))
        bst = ctx.enter_context(nc.sbuf_tensor("bst", [128, B, 2, 6], F32))
        mv = ctx.enter_context(nc.sbuf_tensor("mv", [128, B, 2], F32))
        me = ctx.enter_context(nc.sbuf_tensor("me", [128, B, 2], F32))
        ge = ctx.enter_context(nc.sbuf_tensor("ge", [128, B, 2], F32))
        gvar = ctx.enter_context(nc.sbuf_tensor("gvar", [128, B], F32))
        gsd = ctx.enter_context(nc.sbuf_tensor("gsd", [128, B], F32))
        grs = ctx.enter_context(nc.sbuf_tensor("grs", [128, B], F32))
        gneg = ctx.enter_context(nc.sbuf_tensor("gneg", [128, B], F32))
        ss = ctx.enter_context(nc.sbuf_tensor("ss", [128, T, 2], F32))
        sn = ctx.enter_context(nc.sbuf_tensor("sn", [128, T, 2], F32))
        sig = ctx.enter_context(nc.sbuf_tensor("sig", [128, 3, T], F32))
        ps = [ctx.enter_context(nc.psum_tensor(f"pp{i}", [128, 512], F32)) for i in range(8)]

        load_x, load_c, load_w, load_p = sem("load_x"), sem("load_c"), sem("load_w"), sem("load_p")
        xt_done, xf_ready = sem("xt_done"), sem("xf_ready")
        gn_chain, gn_sum, gn_sqrt = sem("gn_chain"), sem("gn_sum"), sem("gn_sqrt")
        xg_ready, proj_done, proj_ready = sem("xg_ready"), sem("proj_done"), sem("proj_ready")
        sq_ready, nrm_chain, nrm_sqrt = sem("sq_ready"), sem("nrm_chain"), sem("nrm_sqrt")
        qk_normed, qk_turned, qk_ready = sem("qk_normed"), sem("qk_turned"), sem("qk_ready")
        sig_ready, gate_done = sem("sig_ready"), sem("gate_done")
        gn_step, q_copied, coef_ready = sem("gn_step"), sem("q_copied"), sem("coef_ready")

        def squares(c):
            return xs[:, 16 * (c % 2):16 * (c % 2) + 16, :].rearrange("p (t h) f -> p t (h f)", h=2)

        with nc.Block() as block:
            @block.sync
            def _(sp):
                xv = inp["x"].rearrange("b t c d -> b c t d")
                for b in range(B):
                    sp.dma_start(xs[32 * b:32 * b + 32, :, :], xv[b]).then_inc(load_x, 16)
                sp.dma_start(sb["cst"][:, :], consts).then_inc(load_c, 16)
                sp.dma_start(sb["x1"][:, :, :], inp["x"].rearrange("b t c d -> (b t c) d").rearrange("(n p) d -> p n d", p=128)).then_inc(sb["load_xb"], 16)

            @block.scalar
            def _(act):
                for a, k in ((0, "L0_conv_Wq"), (128, "L0_conv_Wk"), (256, "L0_conv_Wv")):
                    act.dma_start(wcat[:, a:a + 128], inp[k]).then_inc(load_w, 16)
                for i, k in enumerate(("L0_conv_w_lr", "L0_conv_w_forget", "L0_conv_w_eta")):
                    act.dma_start(wcat[:, 384 + i:385 + i], inp[k].rearrange("(d a) -> d a", a=1)).then_inc(load_w, 16)
                for k, src in (("10", "L0_conv_w1_0"), ("11", "L0_conv_w1_1")):
                    act.dma_start(sb["first" + k][:, :], inp[src]).then_inc(load_p, 16)
                for k, src in (("20", "L0_conv_w2_0"), ("21", "L0_conv_w2_1")):
                    act.dma_start(sb["first" + k][:, :].rearrange("p (h d) -> p h d", h=2),
                                  inp[src].rearrange("(h p) d -> p h d", p=128)).then_inc(load_p, 16)
                for g in range(T // 4):
                    act.wait_ge(xt_done, g + 1)
                    nc.scalar.copy(xf[:, 4 * g:4 * g + 4, :, :].rearrange("p t b c -> p (t b c)"), ps[g % 4][:, :]).then_inc(xf_ready, 1)
                act.wait_ge(gn_chain, 5)
                nc.scalar.activation(gsd[:, :], gvar[:, :], ACT.Sqrt).then_inc(gn_sqrt, 1)
                def norms(c):
                    act.wait_ge(nrm_chain, 3 * c + 1)
                    nc.scalar.activation(sn[:, CH * c:CH * c + CH, :], ss[:, CH * c:CH * c + CH, :], ACT.Sqrt).then_inc(nrm_sqrt, 1)

                def k_turned(g):
                    act.wait_ge(qk_turned, 2 * g + 2)
                    nc.scalar.copy(sb["kf"][:, 4 * g:4 * g + 4, :].rearrange("p t n -> p (t n)"), ps[6 + g % 2][:, :]).then_inc(qk_ready, 1)

                for t in range(T):
                    act.wait_ge(proj_done, t + 1)
                    nc.scalar.copy(proj[:, t, :], ps[t % 4][:, 0:NP]).then_inc(proj_ready, 1)
                    if t % CH == CH - 1:
                        c = t // CH
                        act.wait_ge(proj_ready, t + 1)
                        if c >= 2:
                            act.wait_ge(nrm_chain, 3 * (c - 2) + 1)
                        nc.scalar.activation(squares(c), proj[:, CH * c:CH * c + CH, 0:256], ACT.Square).then_inc(sq_ready, 1)
                    if t % CH == CH // 2 and t > CH:
                        norms(t // CH - 1)
                norms(NCK - 1)
                nc.scalar.activation(sig[:, :, :], proj[:, :, 384:387].rearrange("p t g -> p g t"), ACT.Sigmoid).then_inc(sig_ready, 1)
                for g in range(T // 4):
                    k_turned(g)
                act.wait_ge(load_p, 16 * 4)

            @block.tensor
            def _(pe):
                cst = sb["cst"]
                ident = cst[:, C_ID:C_ID + 128]
                pe.wait_ge(load_c, 16)
                pe.wait_ge(load_x, 64)
                for t in range(T):
                    if t % 4 == 0 and t >= 16:
                        pe.wait_ge(xf_ready, t // 4 - 3)
                    i = nc.tensor.transpose(ps[(t // 4) % 4][:, 128 * (t % 4):128 * (t % 4) + 128], xs[:, t, :], ident)
                    if t % 4 == 3:
                        i.then_inc(xt_done, 1)
                pe.wait_ge(gn_chain, 3)
                pe.wait_ge(xf_ready, T // 4)
                nc.tensor.matmul(ps[7][:, 0:2 * B], cst[:, C_GRP:C_GRP + 128],
                                 me[:, :, :].rearrange("p b s -> p (b s)"), start=True, stop=True).then_inc(gn_sum, 1)
                pe.wait_ge(xg_ready, B)
                pe.wait_ge(load_w, 16 * 6)
                for t in range(T):
                    if t >= 4:
                        pe.wait_ge(proj_ready, t - 3)
                    nc.tensor.matmul(ps[t % 4][:, 0:NP], xg[:, t, :, :].rearrange("p b c -> p (b c)"), wcat[:, :],
                                     start=True, stop=True).then_inc(proj_done, 1)
                pe.wait_ge(sig_ready, 1)
                for b in range(B):
                    nc.tensor.matmul(ps[3][:, 64 * b:64 * b + 64], cst[:, C_SEL + 128 * b:C_SEL + 128 * b + 128],
                                     sig[:, 1:3, :].rearrange("p g t -> p (g t)"), start=True, stop=True)
                nc.tensor.matmul(ps[3][:, 256:256 + T], cst[:, C_MEAN:C_MEAN + 128], sig[:, 0, :],
                                 start=True, stop=True).then_inc(gate_done, 1)
                for g in range(T // 4):
                    pe.wait_ge(qk_normed, 4 * g // CH + 1)
                    if g >= 2:
                        pe.wait_ge(qk_ready, g - 1)
                    for j in range(2):
                        if g >= 2:
                            pe.wait_ge(q_copied, g - 1)
                        for i in range(4):
                            t = 4 * g + i
                            src = proj[:, t, 0:128] if j == 0 else sb["ktok"][:, t, :]
                            m = nc.tensor.transpose(ps[4 + 2 * j + g % 2][:, 128 * i:128 * i + 128], src, ident)
                        m.then_inc(qk_turned, 1)

            @block.gpsimd
            def _(pool):
                pool.wait_ge(coef_ready, 1)
                nc.gpsimd.tensor_tensor(sb["vs"][:, T // 2:T, :], proj[:, T // 2:T, 256:384], sb["coef"][:, T // 2:T, 8:9].to_broadcast([128, T // 2, 128]), ALU.mult)

            @block.vector
            def _(dve):
                nc.vector.memset(sb["kf"][:, T, :], 0.0)
                dve.wait_ge(load_c, 16)
                dve.wait_ge(xf_ready, T // 4)
                for b in range(B):
                    for h in range(2):
                        i = nc.vector.bn_stats(bst[:, b, h, :], xf[:, 16 * h:16 * h + 16, b, :])
                i.then_inc(gn_chain, 1)
                dve.wait_ge(gn_chain, 1)
                for b in range(B):
                    i = nc.vector.bn_aggr(mv[:, b, :], bst[:, b, :, :].rearrange("p h s -> p (h s)"))
                i.then_inc(gn_chain, 1)
                dve.wait_ge(gn_chain, 2)
                nc.vector.tensor_copy(me[:, :, 0], mv[:, :, 0])
                for b in range(B):
                    i = nc.vector.scalar_tensor_tensor(out=me[:, b, 1:2], in0=mv[:, b, 0:1], scalar=mv[:, b, 0:1],
                                                       in1=mv[:, b, 1:2], op0=ALU.mult, op1=ALU.add)
                i.then_inc(gn_chain, 1)
                dve.wait_ge(gn_sum, 1)
                nc.vector.tensor_copy(ge[:, :, :].rearrange("p b s -> p (b s)"), ps[7][:, 0:2 * B]).then_inc(gn_chain, 1)
                dve.wait_ge(gn_chain, 4)
                for b in range(B):
                    i = nc.vector.tensor_scalar(gvar[:, b:b + 1], ge[:, b, 0:1], ge[:, b, 0:1], -1.0, ALU.mult, ALU.mult)
                i.then_inc(gn_step, 1)
                dve.wait_ge(gn_step, 1)
                nc.vector.scalar_tensor_tensor(out=gvar[:, :], in0=gvar[:, :], scalar=1e-5, in1=ge[:, :, 1],
                                               op0=ALU.add, op1=ALU.add).then_inc(gn_chain, 1)
                dve.wait_ge(gn_sqrt, 1)
                nc.vector.reciprocal(grs[:, :], gsd[:, :]).then_inc(gn_step, 1)
                dve.wait_ge(gn_step, 2)
                nc.vector.scalar_tensor_tensor(out=gneg[:, :], in0=ge[:, :, 0], scalar=-1.0, in1=grs[:, :],
                                               op0=ALU.mult, op1=ALU.mult).then_inc(gn_step, 1)
                dve.wait_ge(gn_step, 3)
                for b in range(B):
                    nc.vector.tensor_scalar(xg[:, :, b, :], xf[:, :, b, :], grs[:, b:b + 1], gneg[:, b:b + 1],
                                            ALU.mult, ALU.add).then_inc(xg_ready, 1)
                for c in range(NCK):
                    st_ = slice(CH * c, CH * c + CH)
                    dve.wait_ge(sq_ready, c + 1)
                    nc.vector.tensor_reduce(ss[:, st_, :], squares(c).rearrange("p t (j f) -> p t j f", j=2), AX.X, ALU.add).then_inc(nrm_chain, 1)
                    dve.wait_ge(nrm_sqrt, c + 1)
                    nc.vector.tensor_scalar(sn[:, st_, :], sn[:, st_, :], 1e-12, None, ALU.max).then_inc(nrm_chain, 1)
                    dve.wait_ge(nrm_chain, 3 * c + 2)
                    nc.vector.reciprocal(sn[:, st_, :], sn[:, st_, :]).then_inc(nrm_chain, 1)
                    dve.wait_ge(nrm_chain, 3 * c + 3)
                    nc.vector.tensor_tensor(proj[:, st_, 0:128], proj[:, st_, 0:128], sn[:, st_, 0:1].to_broadcast([128, CH, 128]), ALU.mult)
                    nc.vector.tensor_tensor(sb["ktok"][:, st_, :], proj[:, st_, 128:256], sn[:, st_, 1:2].to_broadcast([128, CH, 128]), ALU.mult).then_inc(qk_normed, 1)
                dve.wait_ge(gate_done, 1)
                gates = ps[3][:, 0:256].rearrange("p (b g t) -> p b g t", b=B, g=2)
                for b in range(B):
                    nc.vector.tensor_copy(sb["coef"][:, :, b], gates[:, b, 1, :])
                    nc.vector.tensor_scalar(sb["coef"][:, :, 4 + b], gates[:, b, 0, :], -1.0, 1.0, ALU.mult, ALU.add)
                nc.vector.tensor_scalar(sb["coef"][:, :, 8], ps[3][:, 256:256 + T], -MAX_LR * 2.0 / (C * D), None, ALU.mult).then_inc(coef_ready, 1)
                dve.wait_ge(coef_ready, 1)
                nc.vector.tensor_tensor(sb["vs"][:, 0:T // 2, :], proj[:, 0:T // 2, 256:384], sb["coef"][:, 0:T // 2, 8:9].to_broadcast([128, T // 2, 128]), ALU.mult)
                for g in range(T // 4):
                    dve.wait_ge(qk_turned, 2 * g + 1)
                    nc.vector.tensor_copy(sb["qf"][:, :, 4 * g:4 * g + 4, :].rearrange("p b t c -> p t b c"),
                                          ps[4 + g % 2][:, :].rearrange("p (t b c) -> p t b c", t=4, b=B)).then_inc(q_copied, 1)


def learn(nc, st, sb):
    sem = lambda name: st.enter_context(nc.semaphore(name))
    with ExitStack() as ctx:
        def buf(name, shape):
            return ctx.enter_context(nc.sbuf_tensor("l_" + name, shape, F32))

        W = {k: sb["w" + k] for k in PARAMS}
        M = {k: buf("m" + k, [128, B, 256]) for k in PARAMS}
        WT = {k: buf("wt" + k, [128, B, 256]) for k in ("21", "11", "20")}
        Q21 = buf("q21", [128, B, 256])
        eM, P = ({k: buf(n + k, [128, B, 256]) for k in ("10", "20", "11")} for n in ("em", "p"))
        kt = buf("kt", [128, 128])
        cf = buf("cf", [128, 9])
        km, h1m, dpm, dh1m = (buf(n, [128, B, 128]) for n in ("km", "h1m", "dpm", "dh1m"))
        g, g0c = [buf("g0", [128, 256]), buf("g1", [128, 256])], buf("g0c", [128, 256])
        h1, hv, dp, dh1 = (buf(n, [128, 128]) for n in ("h1", "hv", "dp", "dh1"))
        da = [buf("da0", [128, 256]), buf("da1", [128, 256])]
        gf, daf = [buf("gf0", [128, 256]), buf("gf1", [128, 256])], buf("daf", [128, 256])
        h1f, dpf, dh1f = (buf(n, [128, 128]) for n in ("h1f", "dpf", "dh1f"))
        ca, aq, u, th, tq, dd, gp = ([buf(f"{n}{l}", [128, 256]) for l in range(2)] for n in ("ca", "aq", "u", "th", "tq", "dd", "gp"))

        def bank(name, n=1):
            return ctx.enter_context(nc.psum_tensor("lp_" + name, [128, 512 * n], F32))

        ps_a, ps_b, ps_h, ps_t = bank("a"), bank("b"), bank("h"), bank("t")
        ps_g = [bank("g0", 2), bank("g1", 2)]

        first_turned, zeroed, table_loaded = sem("l_first"), sem("l_zeroed"), sem("l_table")
        mm_done = sem("l_mm")
        turned, gf_ready = sem("l_turned"), sem("l_f")
        chain = sem("l_chain")
        grad_done, mom_ready = sem("l_grad"), sem("l_mom")
        wt_done, wt_ready = sem("l_wt"), sem("l_wt_ready")
        w_ready = {k: sem("l_w" + k) for k in PARAMS}
        gelu_ready, pre_ready = sem("l_gelu"), sem("l_pre")
        u_ready, tanh_ready, slope_ready = ([sem(f"l_{n}{l}") for l in range(2)] for n in ("u", "tanh", "slope"))
        kt_in, cf_in = sem("l_kt_in"), sem("l_cf_in")
        km_ready, h1m_ready, dpm_ready, dh1m_ready, g0c_ready = (sem("l_" + n) for n in ("kmr", "h1mr", "dpmr", "dh1mr", "g0cr"))
        q_ready, em_ready, p_ready, q21_ready = sem("l_q"), sem("l_em"), sem("l_p"), sem("l_q21")
        A0, H1, A1, Y, DG1, DH1, DG0 = range(1, 8)
        TG0, TH1, TG1, TDP, TDA1, TDH1 = range(1, 7)
        G21, G10, G20, G11 = range(0, 8, 2)
        X20, X21, X11 = range(0, 6, 2)
        P10, P20, P11 = range(1, 4)
        K_H1, K_HV, K_DP, K_DA1, K_DH1, K_DA0 = range(1, 7)

        def rows(b):
            return slice(32 * b, 32 * b + 32)

        def half(h):
            return slice(2 * h, 2 * h + 2)

        def flat(x):
            return x.rearrange("p b n -> p (b n)")

        def grad_bank(n, h):
            return ps_g[n // 2 % 2][:, 512 * h:512 * h + 512]

        def wt_bank(k, h):
            return {"20": (ps_h, ps_b)[h], "21": ps_g[0][:, 512 * h:512 * h + 512], "11": ps_g[1][:, 512 * h:512 * h + 512]}[k][:, :]

        def step_of(t, k):
            return sb[k][:, bass.ds(t, 1), :].rearrange("p a n -> p (a n)")

        def rotated(engine, forward, backward):
            forward(-1, grads=False)
            with engine.Fori(0, T - 1) as t:
                backward(t)
                forward(t)
            backward(T - 1)
            forward(T - 1, steps=False)

        with nc.Block() as block:
            @block.gpsimd
            def _(pool):
                def per_batch(i):
                    return cf[:, i:i + 4].rearrange("p (b a) -> p b a", a=1).to_broadcast([128, B, 256])

                def eta_momentum(t, k, n):
                    pool.wait_ge(mom_ready, t * 8 + n + 2)
                    nc.gpsimd.tensor_tensor(eM[k][:, :, :], M[k][:, :, :], per_batch(0), ALU.mult).then_inc(em_ready, 1)

                def ahead(t, k, i):
                    pool.wait_ge(em_ready, t * 3 + i)
                    pool.wait_ge(q_ready, t * 3 + i)
                    nc.gpsimd.tensor_tensor(P[k][:, :, :], P[k][:, :, :], eM[k][:, :, :], ALU.add).then_inc(p_ready, 1)

                def forward(p, grads=True, steps=True):
                    if grads:
                        ahead(p, "11", P11)
                        pool.wait_ge(q21_ready, p + 1)
                        for h in range(2):
                            pool.wait_ge(mom_ready, p * 8 + 8 + G21 + h + 1)
                            nc.gpsimd.tensor_tensor(W["21"][:, half(h), :], Q21[:, half(h), :], M["21"][:, half(h), :], ALU.add).then_inc(w_ready["21"], 1)
                    if steps:
                        pool.wait_ge(mm_done, p * 7 + 7 + A0)
                        nc.gpsimd.tensor_copy(kt[:, :], step_of(p + 2, "kf")).then_inc(kt_in, 1)

                def backward(t):
                    pool.wait_ge(cf_in, t + 1)
                    eta_momentum(t, "10", G10)
                    eta_momentum(t, "20", G20)
                    eta_momentum(t, "11", G11)
                    pool.wait_ge(w_ready["21"], t * 2 + 2)
                    nc.gpsimd.tensor_tensor(Q21[:, :, :], W["21"][:, :, :], per_batch(4), ALU.mult).then_inc(q21_ready, 1)
                    ahead(t, "10", P10)
                    ahead(t, "20", P20)

                nc.gpsimd.tensor_copy(kt[:, :], sb["kf"][:, 0, :]).then_inc(kt_in, 1)
                for k in ("21", "10", "20", "11"):
                    for h in range(2):
                        nc.gpsimd.memset(M[k][:, half(h), :], 0.0).then_inc(mom_ready, 1)
                rotated(pool, forward, backward)

            @block.scalar
            def _(act):
                def hidden(t, l, p):
                    act.wait_ge(mm_done, t * 7 + (A0, A1)[l])
                    nc.scalar.activation(g[l][:, :], p[:, 0:256], ACT.Gelu_apprx_tanh).then_inc(gelu_ready, 1)

                def before_slope(t, l, p):
                    nc.scalar.mul(ca[l][:, :], p[:, 0:256], -1.5 * GELU_C).then_inc(pre_ready, 1)
                    nc.scalar.activation(aq[l][:, :], p[:, 0:256], ACT.Square, scale=GELU_A ** 0.5).then_inc(pre_ready, 1)

                def tanh(t, l):
                    act.wait_ge(u_ready[l], t * 2 + 1)
                    nc.scalar.activation(th[l][:, :], u[l][:, :], ACT.Tanh, scale=-1.0 / 1.5).then_inc(tanh_ready[l], 1)

                def tanh_squared(t, l):
                    act.wait_ge(tanh_ready[l], t * 2 + 1)
                    nc.scalar.activation(tq[l][:, :], th[l][:, :], ACT.Square).then_inc(tanh_ready[l], 1)

                def feature(t, n, dst, width):
                    act.wait_ge(turned, t * 6 + n)
                    nc.scalar.copy(dst[:, :], ps_t[:, 0:width]).then_inc(gf_ready, 1)

                def wt(t, n, k, h):
                    act.wait_ge(wt_done, t * 6 + n + h + 1)
                    nc.scalar.copy(flat(WT[k][:, half(h), :]), wt_bank(k, h)).then_inc(wt_ready, 1)

                def masked(dst, src, ready):
                    for b in range(B):
                        i = nc.scalar.copy(dst[rows(b), b, :], src[rows(b), :])
                    i.then_inc(ready, 1)

                def keep(t, k, batches=range(B)):
                    act.wait_ge(w_ready[k], t * 2 + 2)
                    for b in batches:
                        m = nc.scalar.mul(P[k][:, b, :], W[k][:, b, :], cf[:, 4 + b:5 + b])
                    if b == B - 1:
                        m.then_inc(q_ready, 1)

                def forward(p, grads=True, steps=True):
                    if not steps:
                        return
                    t = p + 1
                    if grads:
                        act.wait_ge(q21_ready, p + 1)
                        act.wait_ge(q_ready, p * 3 + 3)
                        act.wait_ge(mom_ready, p * 8 + 8 + G21 + 2)
                    nc.scalar.copy(cf[:, :], step_of(t, "coef")).then_inc(cf_in, 1)
                    hidden(t, 0, ps_a)
                    wt(t, X20, "20", 0)
                    feature(t, TG0, gf[0], 256)
                    wt(t, X20, "20", 1)
                    before_slope(t, 0, ps_a)
                    act.wait_ge(cf_in, t + 1)
                    keep(t, "10", (0, 1, 2))
                    feature(t, TH1, h1f, 128)
                    wt(t, X21, "21", 0)
                    wt(t, X21, "21", 1)

                def backward(t):
                    hidden(t, 1, ps_b)
                    before_slope(t, 1, ps_b)
                    feature(t, TG1, gf[1], 256)
                    tanh(t, 0)
                    tanh_squared(t, 0)
                    tanh(t, 1)
                    tanh_squared(t, 1)
                    wt(t, X11, "11", 0)
                    feature(t, TDP, dpf, 128)
                    masked(dpm, dp, dpm_ready)
                    wt(t, X11, "11", 1)
                    keep(t, "10", (3,))
                    feature(t, TDA1, daf, 256)
                    keep(t, "20", (0, 1, 2))
                    feature(t, TDH1, dh1f, 128)
                    for b in range(B):
                        i = nc.scalar.copy(km[rows(b), b, :], sb["ktok"][rows(b), bass.ds(t, 1), :].rearrange("p a n -> p (a n)"))
                    i.then_inc(km_ready, 1)
                    keep(t, "20", (3,))
                    masked(dh1m, dh1, dh1m_ready)
                    nc.scalar.copy(g0c[:, :], g[0][:, :]).then_inc(g0c_ready, 1)
                    keep(t, "11")

                nc.scalar.activation(g[0][:, :], sb["first10"][:, :], ACT.Gelu_apprx_tanh).then_inc(table_loaded, 1)
                act.wait_ge(table_loaded, 1)
                act.wait_ge(first_turned, 1)
                for k, p in (("20", ps_a), ("21", ps_t)):
                    for b in range(B):
                        i = nc.scalar.copy(W[k][:, b, :], p[:, 0:256])
                        if b % 2:
                            i.then_inc(w_ready[k], 1)
                act.wait_ge(zeroed, 4)
                rotated(act, forward, backward)

            @block.vector
            def _(dve):
                def momentum(t, k, n, b):
                    dve.wait_ge(grad_done, t * 8 + n + b // 2 + 1)
                    i = nc.vector.scalar_tensor_tensor(out=M[k][:, b, :], in0=M[k][:, b, :], scalar=cf[:, b:b + 1],
                                                       in1=grad_bank(n, b // 2)[:, 256 * (b % 2):256 * (b % 2) + 256],
                                                       op0=ALU.mult, op1=ALU.add)
                    if b % 2:
                        i.then_inc(mom_ready, 1)

                def update(t, k, n, i, h):
                    dve.wait_ge(p_ready, t * 3 + i)
                    dve.wait_ge(grad_done, t * 8 + n + h + 1)
                    nc.vector.tensor_tensor(flat(W[k][:, half(h), :]), flat(P[k][:, half(h), :]), grad_bank(n, h), ALU.add).then_inc(w_ready[k], 1)

                def momentum_after(t, k, n, h):
                    nc.vector.tensor_tensor(flat(M[k][:, half(h), :]), flat(eM[k][:, half(h), :]), grad_bank(n, h), ALU.add).then_inc(mom_ready, 1)

                def slope_in(t, l):
                    dve.wait_ge(pre_ready, t * 4 + 2 * l + 2)
                    nc.vector.scalar_tensor_tensor(out=u[l][:, :], in0=aq[l][:, :], scalar=1.0, in1=ca[l][:, :],
                                                   op0=ALU.add, op1=ALU.mult).then_inc(u_ready[l], 1)
                    nc.vector.scalar_tensor_tensor(out=dd[l][:, :], in0=aq[l][:, :], scalar=1.0 / 3.0, in1=ca[l][:, :],
                                                   op0=ALU.add, op1=ALU.mult).then_inc(u_ready[l], 1)

                def slope_out(t, l):
                    dve.wait_ge(tanh_ready[l], t * 2 + 2)
                    dve.wait_ge(u_ready[l], t * 2 + 2)
                    nc.vector.scalar_tensor_tensor(out=dd[l][:, :], in0=tq[l][:, :], scalar=-1.0, in1=dd[l][:, :],
                                                   op0=ALU.add, op1=ALU.mult).then_inc(slope_ready[l], 1)
                    dve.wait_ge(slope_ready[l], t * 2 + 1)
                    nc.vector.scalar_tensor_tensor(out=gp[l][:, :], in0=th[l][:, :], scalar=0.5, in1=dd[l][:, :],
                                                   op0=ALU.mult, op1=ALU.add).then_inc(slope_ready[l], 1)

                def slope_times(t, l, p, n):
                    dve.wait_ge(slope_ready[l], t * 2 + 2)
                    dve.wait_ge(mm_done, t * 7 + n)
                    nc.vector.scalar_tensor_tensor(out=da[l][:, :], in0=gp[l][:, :], scalar=0.5, in1=p[:, 0:256],
                                                   op0=ALU.add, op1=ALU.mult).then_inc(chain, 1)

                def forward(p, grads=True, steps=True):
                    t = p + 1
                    if grads:
                        update(p, "10", G10, P10, 0)
                        update(p, "10", G10, P10, 1)
                        update(p, "20", G20, P20, 0)
                        momentum_after(p, "10", G10, 0)
                        update(p, "20", G20, P20, 1)
                        momentum_after(p, "10", G10, 1)
                        momentum_after(p, "20", G20, 0)
                        momentum_after(p, "20", G20, 1)
                        update(p, "11", G11, P11, 0)
                    if steps:
                        dve.wait_ge(mm_done, t * 7 + H1)
                        nc.vector.tensor_tensor(h1[:, :], ps_h[:, 0:128], step_of(t, "ktok"), ALU.add).then_inc(chain, 1)
                    if grads:
                        update(p, "11", G11, P11, 1)
                    if steps:
                        dve.wait_ge(chain, t * 6 + K_H1)
                        dve.wait_ge(cf_in, t + 1)
                        nc.vector.scalar_tensor_tensor(out=hv[:, :], in0=h1[:, :], scalar=cf[:, 8:9], in1=step_of(t, "vs"),
                                                       op0=ALU.mult, op1=ALU.subtract).then_inc(chain, 1)
                    if grads:
                        momentum_after(p, "11", G11, 0)
                        momentum_after(p, "11", G11, 1)
                    if steps:
                        slope_in(t, 0)

                def backward(t):
                    slope_in(t, 1)
                    dve.wait_ge(mm_done, t * 7 + Y)
                    dve.wait_ge(chain, t * 6 + K_HV)
                    nc.vector.scalar_tensor_tensor(out=dp[:, :], in0=ps_h[:, 0:128], scalar=cf[:, 8:9], in1=hv[:, :],
                                                   op0=ALU.mult, op1=ALU.add).then_inc(chain, 1)
                    for b in range(B):
                        i = nc.vector.tensor_copy(h1m[rows(b), b, :], h1[rows(b), :])
                    i.then_inc(h1m_ready, 1)
                    slope_out(t, 1)
                    slope_times(t, 1, ps_a, DG1)
                    dve.wait_ge(mm_done, t * 7 + DH1)
                    dve.wait_ge(chain, t * 6 + K_DP)
                    nc.vector.tensor_tensor(dh1[:, :], ps_h[:, 0:128], dp[:, :], ALU.add).then_inc(chain, 1)
                    slope_out(t, 0)
                    momentum(t, "21", G21, 0)
                    momentum(t, "21", G21, 1)
                    slope_times(t, 0, ps_b, DG0)
                    momentum(t, "21", G21, 2)
                    momentum(t, "21", G21, 3)

                for m in (dpm, h1m, dh1m, km):
                    nc.vector.memset(m[:, :, :], 0.0).then_inc(zeroed, 1)
                for k in ("10", "11"):
                    for b in range(B):
                        i = nc.vector.tensor_copy(W[k][:, b, :], sb["first" + k][:, :])
                        if b % 2:
                            i.then_inc(w_ready[k], 1)
                dve.wait_ge(zeroed, 4)
                rotated(dve, forward, backward)

            @block.tensor
            def _(pe):
                ident = sb["cst"][:, C_ID:C_ID + 128]

                def up(p, x, w, w_wait=None):
                    for b in range(B):
                        if w_wait:
                            w_wait(b)
                        i = nc.tensor.matmul(p[rows(b), 0:256], x[:, rows(b)], w[:, b, :], start=True, stop=True)
                    i.then_inc(mm_done, 1)

                def down(p, x, w):
                    for h in range(2):
                        for b in range(B):
                            i = nc.tensor.matmul(p[rows(b), 0:128], x[:, 128 * h + 32 * b:128 * h + 32 * b + 32],
                                                 w[:, b, 128 * h:128 * h + 128], start=h == 0, stop=h == 1)
                    i.then_inc(mm_done, 1)

                def turn(x, width):
                    for h in range(width // 128):
                        i = nc.tensor.transpose(ps_t[:, 128 * h:128 * h + 128], x[:, 128 * h:128 * h + 128], ident)
                    i.then_inc(turned, 1)

                def turn_w(k, h):
                    for j in range(4):
                        i = nc.tensor.transpose(wt_bank(k, h)[:, 128 * j:128 * j + 128],
                                                W[k][:, 2 * h + j // 2, 128 * (j % 2):128 * (j % 2) + 128], ident)
                    i.then_inc(wt_done, 1)

                def grad(t, n, b, x, y):
                    i = nc.tensor.matmul(grad_bank(n, b // 2)[:, 256 * (b % 2):256 * (b % 2) + 256], x[:, b, :], y[:, :],
                                         start=True, stop=True)
                    if b % 2:
                        i.then_inc(grad_done, 1)

                def forward(p, grads=True, steps=True):
                    t = p + 1
                    if grads:
                        pe.wait_ge(km_ready, p + 1)
                        pe.wait_ge(chain, p * 6 + K_DA0)
                        for b in range(B):
                            grad(p, G10, b, km, da[0])
                        pe.wait_ge(dh1m_ready, p + 1)
                        pe.wait_ge(g0c_ready, p + 1)
                        pe.wait_ge(mom_ready, p * 8 + 8 + G21 + 2)
                        grad(p, G20, 0, dh1m, g0c)
                        grad(p, G20, 1, dh1m, g0c)
                        grad(p, G20, 2, dh1m, g0c)
                        grad(p, G20, 3, dh1m, g0c)
                    if steps:
                        pe.wait_ge(kt_in, p + 2)
                        up(ps_a, kt, W["10"], lambda b: pe.wait_ge(w_ready["10"], t * 2 + b // 2 + 1))
                        pe.wait_ge(w_ready["20"], t * 2 + 1)
                        turn_w("20", 0)
                        pe.wait_ge(gelu_ready, t * 2 + 1)
                        turn(g[0], 256)
                        pe.wait_ge(w_ready["20"], t * 2 + 2)
                        turn_w("20", 1)
                    if grads:
                        pe.wait_ge(h1m_ready, p + 1)
                        pe.wait_ge(mom_ready, p * 8 + 8 + G10 + 1)
                        grad(p, G11, 0, h1m, da[1])
                        grad(p, G11, 1, h1m, da[1])
                    if steps:
                        pe.wait_ge(wt_ready, t * 6 + X20 + 2)
                        pe.wait_ge(gf_ready, t * 6 + TG0)
                        down(ps_h, gf[0], WT["20"])
                    if grads:
                        pe.wait_ge(mom_ready, p * 8 + 8 + G10 + 2)
                        grad(p, G11, 2, h1m, da[1])
                        grad(p, G11, 3, h1m, da[1])
                    if steps:
                        pe.wait_ge(chain, t * 6 + K_H1)
                        turn(h1, 128)
                        pe.wait_ge(mom_ready, t * 8 + G20 + 2)
                        pe.wait_ge(w_ready["21"], t * 2 + 2)
                        turn_w("21", 0)
                        turn_w("21", 1)
                        pe.wait_ge(gf_ready, t * 6 + TH1)
                        up(ps_b, h1f, W["11"], lambda b: pe.wait_ge(w_ready["11"], t * 2 + b // 2 + 1))

                def backward(t):
                    pe.wait_ge(gelu_ready, t * 2 + 2)
                    turn(g[1], 256)
                    pe.wait_ge(mom_ready, t * 8 + G11 + 2)
                    turn_w("11", 0)
                    pe.wait_ge(wt_ready, t * 6 + X21 + 2)
                    pe.wait_ge(gf_ready, t * 6 + TG1)
                    down(ps_h, gf[1], WT["21"])
                    turn_w("11", 1)
                    pe.wait_ge(chain, t * 6 + K_DP)
                    turn(dp, 128)
                    pe.wait_ge(gf_ready, t * 6 + TDP)
                    up(ps_a, dpf, W["21"])
                    pe.wait_ge(chain, t * 6 + K_DA1)
                    turn(da[1], 256)
                    pe.wait_ge(dpm_ready, t + 1)
                    grad(t, G21, 0, dpm, g[1])
                    pe.wait_ge(wt_ready, t * 6 + X11 + 2)
                    pe.wait_ge(gf_ready, t * 6 + TDA1)
                    down(ps_h, daf, WT["11"])
                    grad(t, G21, 1, dpm, g[1])
                    pe.wait_ge(chain, t * 6 + K_DH1)
                    turn(dh1, 128)
                    grad(t, G21, 2, dpm, g[1])
                    pe.wait_ge(pre_ready, t * 4 + 4)
                    pe.wait_ge(gf_ready, t * 6 + TDH1)
                    up(ps_b, dh1f, W["20"])
                    grad(t, G21, 3, dpm, g[1])

                for k, p in (("20", ps_a), ("21", ps_t)):
                    for h in range(2):
                        i = nc.tensor.transpose(p[:, 128 * h:128 * h + 128], sb["first" + k][:, 128 * h:128 * h + 128], ident)
                i.then_inc(first_turned, 1)
                pe.wait_ge(w_ready["21"], 2)
                rotated(pe, forward, backward)


def read_out(nc, st, sb, inp):
    sem = lambda name: st.enter_context(nc.semaphore(name))
    with ExitStack() as ctx:
        def buf(name, shape):
            return ctx.enter_context(nc.sbuf_tensor("r_" + name, shape, F32))

        wf = {k: buf("wf" + k, [128, 256]) for k in PARAMS}
        g0, g1 = ([buf(f"g{l}{i}", [128, 1024]) for i in range(2)] for l in range(2))
        h1 = [buf(f"h1{i}", [128, 512]) for i in range(4)]
        z = [buf(f"z{i}", [128, 512]) for i in range(2)]
        bst = buf("bst", [128, NT, 6])
        ps_a0, ps_a1 = (ctx.enter_context(nc.psum_tensor("rp_a" + n, [128, 1024], F32)) for n in "01")
        ps_h, ps_z, ps_x = (ctx.enter_context(nc.psum_tensor("rp_" + n, [128, 512], F32)) for n in "hzx")
        wm = {k: buf("wm" + k, [128, 256]) for k in ("20", "21")}
        wm_turned, wt_copied = sem("r_wmt"), sem("r_wtc")
        wf_sum, wf_ready = sem("r_wfsum"), sem("r_wf")
        a0_done, h_done, a1_done, z_done, x_done = (sem("r_" + n) for n in ("a0", "h", "a1", "z", "x"))
        g0_ready, g1_ready, h_ready, z_ready = (sem("r_" + n) for n in ("g0r", "g1r", "hr", "zr"))
        x1_ready, st_ready, mv_ready = sem("r_x1"), sem("r_st"), sem("r_mv")
        N = B * S // 512
        order = ("10", "20", "11", "21")

        def q(n):
            return sb["qf"][:, n // 2, 16 * (n % 2):16 * (n % 2) + 16, :].rearrange("p t c -> p (t c)")

        with nc.Block() as block:
            @block.scalar
            def _(act):
                for k in range(N + 2):
                    if k < N:
                        act.wait_ge(a0_done, k + 1)
                        if k >= 2:
                            act.wait_ge(h_done, k - 1)
                        nc.scalar.activation(g0[k % 2][:, :], ps_a0[:, :], ACT.Gelu_apprx_tanh).then_inc(g0_ready, 1)
                    if k >= 2:
                        n = k - 2
                        act.wait_ge(a1_done, n + 1)
                        if n >= 2:
                            act.wait_ge(z_done, n - 1)
                        nc.scalar.activation(g1[n % 2][:, :], ps_a1[:, :], ACT.Gelu_apprx_tanh).then_inc(g1_ready, 1)

            @block.tensor
            def _(pe):
                ident = sb["cst"][:, C_ID:C_ID + 128]
                def turn_mean(i, k, p):
                    pe.wait_ge(wf_ready, i)
                    for h in range(2):
                        m = nc.tensor.transpose(p[:, 128 * h:128 * h + 128], wm[k][:, 128 * h:128 * h + 128], ident)
                    m.then_inc(wm_turned, 1)

                for k in range(N + 4):
                    if k < N:
                        pe.wait_ge(wf_ready, 1)
                        if k >= 1:
                            pe.wait_ge(g0_ready, k)
                        for h in range(2):
                            i = nc.tensor.matmul(ps_a0[:, 512 * h:512 * h + 512], wf["10"][:, 128 * h:128 * h + 128], q(k),
                                                 start=True, stop=True)
                        i.then_inc(a0_done, 1)
                    if k == 0:
                        turn_mean(2, "20", ps_z)
                    if k == 1:
                        turn_mean(4, "21", ps_x)
                    if 1 <= k <= N:
                        n = k - 1
                        pe.wait_ge(wt_copied, 1)
                        pe.wait_ge(g0_ready, n + 1)
                        if n >= 1:
                            pe.wait_ge(h_ready, n)
                        for h in range(2):
                            i = nc.tensor.matmul(ps_h[:, :], wf["20"][:, 128 * h:128 * h + 128], g0[n % 2][:, 512 * h:512 * h + 512],
                                                 start=h == 0, stop=h == 1)
                        i.then_inc(h_done, 1)
                    if 2 <= k <= N + 1:
                        n = k - 2
                        pe.wait_ge(wf_ready, 3)
                        pe.wait_ge(h_ready, n + 1)
                        if n >= 1:
                            pe.wait_ge(g1_ready, n)
                        for h in range(2):
                            i = nc.tensor.matmul(ps_a1[:, 512 * h:512 * h + 512], wf["11"][:, 128 * h:128 * h + 128], h1[n % 4][:, :],
                                                 start=True, stop=True)
                        i.then_inc(a1_done, 1)
                    if 3 <= k <= N + 2:
                        n = k - 3
                        pe.wait_ge(wt_copied, 2)
                        pe.wait_ge(g1_ready, n + 1)
                        if n >= 1:
                            pe.wait_ge(z_ready, n)
                        for h in range(2):
                            i = nc.tensor.matmul(ps_z[:, :], wf["21"][:, 128 * h:128 * h + 128], g1[n % 2][:, 512 * h:512 * h + 512],
                                                 start=h == 0, stop=h == 1)
                        i.then_inc(z_done, 1)
                    if 4 <= k:
                        n = k - 4
                        pe.wait_ge(z_ready, n + 1)
                        if n >= 1:
                            pe.wait_ge(x1_ready, n)
                        for i in range(4):
                            m = nc.tensor.transpose(ps_x[:, 128 * i:128 * i + 128], z[n % 2][:, 128 * i:128 * i + 128], ident)
                        m.then_inc(x_done, 1)

            @block.vector
            def _(dve):
                for i, k in enumerate(order):
                    w = wm.get(k, wf[k])
                    nc.vector.tensor_reduce(w[:, :], sb["w" + k][:, :, :].rearrange("p b n -> p n b"), AX.X, ALU.add).then_inc(wf_sum, 1)
                    dve.wait_ge(wf_sum, i + 1)
                    nc.vector.tensor_scalar(w[:, :], w[:, :], 1.0 / B, None, ALU.mult).then_inc(wf_ready, 1)
                    if k in wm:
                        dve.wait_ge(wm_turned, 1 if k == "20" else 2)
                        nc.vector.tensor_copy(wf[k][:, :], ps_z[:, 0:256] if k == "20" else ps_x[:, 0:256]).then_inc(wt_copied, 1)
                for k in range(1, N + 5):
                    if k <= N:
                        n = k - 1
                        dve.wait_ge(h_done, n + 1)
                        if n >= 4:
                            dve.wait_ge(a1_done, n - 3)
                            dve.wait_ge(z_ready, n - 3)
                        nc.vector.tensor_tensor(h1[n % 4][:, :], ps_h[:, :], q(n), ALU.add).then_inc(h_ready, 1)
                    if 3 <= k <= N + 2:
                        n = k - 3
                        dve.wait_ge(z_done, n + 1)
                        dve.wait_ge(h_ready, n + 1)
                        if n >= 2:
                            dve.wait_ge(x_done, n - 1)
                        nc.vector.tensor_tensor(z[n % 2][:, :], ps_z[:, :], h1[n % 4][:, :], ALU.add).then_inc(z_ready, 1)
                    if 4 <= k <= N + 3:
                        n = k - 4
                        dve.wait_ge(x_done, n + 1)
                        dve.wait_ge(sb["load_xb"], 16)
                        x1 = sb["x1"][:, 4 * n:4 * n + 4, :].rearrange("p t f -> p (t f)")
                        nc.vector.tensor_tensor(x1, ps_x[:, :], x1, ALU.add).then_inc(x1_ready, 1)
                    if 5 <= k:
                        n = k - 5
                        dve.wait_ge(x1_ready, n + 1)
                        for i in range(4):
                            m = nc.vector.bn_stats(bst[:, 4 * n + i, :], sb["x1"][:, 4 * n + i, :])
                        m.then_inc(st_ready, 1)
                        dve.wait_ge(st_ready, n + 1)
                        for i in range(4):
                            m = nc.vector.bn_aggr(sb["mv"][:, 4 * n + i, :], bst[:, 4 * n + i, :])
                        m.then_inc(mv_ready, 1)


def attend(nc, st, sb, inp):
    sem = lambda name: st.enter_context(nc.semaphore(name))
    HALF = WIN // 2
    QL, QN = WIN - 1, (WIN - 1) + S + WIN
    R = 8
    GR = WIN // 4
    SPAN = S + WIN
    NTB = S // 128
    with ExitStack() as ctx:
        def buf(name, shape):
            return ctx.enter_context(nc.sbuf_tensor("t_" + name, shape, F32))

        xl = buf("xl", [128, NT, 128])
        xlf = buf("xlf", [128, NT * 128])
        xsh = buf("xsh", [128, B, NTB + 1, 128])
        wt, wx = buf("wt", [128, U]), buf("wx", [128, U])
        wa, bh, ba = buf("wa", [128, B]), buf("bh", [128, 1]), buf("ba", [128, 1])
        qp, kp = buf("qp", [128, QN]), buf("kp", [128, SPAN])
        hs = [buf(f"h{i}", [128, SPAN]) for i in range(R)]
        wag = buf("wag", [128, GR, 32])
        es = buf("es", [128, S])
        e = buf("e", [128, NTB, B, WIN])
        mx = buf("mx", [128, NTB * B])
        am = [buf(f"am{i}", [128, B, 160]) for i in range(2)]
        at1 = [buf(f"at1{i}", [128, 512]) for i in range(2)]
        at2 = [buf(f"at2{i}", [32, 512]) for i in range(2)]
        std, rstd = buf("std", [128, NT]), buf("rstd", [128, NT])
        bst = buf("bst", [128, NT, 6])
        ps = [ctx.enter_context(nc.psum_tensor(f"tp{i}", [128, 512], F32)) for i in range(6)]
        ps_e = ctx.enter_context(nc.psum_tensor("tp_e", [128, 1024], F32))

        load, load_wa, shifted = sem("t_load"), sem("t_loadwa"), sem("t_shift")
        cleared, wa_clear, wag_ready = sem("t_cleared"), sem("t_waclear"), sem("t_wag")
        es_ready, et_done = sem("t_es"), sem("t_et")
        ve, std_ready, rstd_ready, xl_ready = sem("t_ve"), sem("t_std"), sem("t_rstd"), sem("t_xl")
        xl_turned, xlf_ready = sem("t_turn"), sem("t_xlf")
        qk_done, qk_ready = sem("t_qk"), sem("t_qkr")
        sum_ready = [sem("t_sumv"), sem("t_sump")]
        tanh_ready, e_done = sem("t_tanh"), sem("t_edone")
        soft, exp_ready = sem("t_soft"), sem("t_exp")
        am_ready, at_done, at_ready, v_done = sem("t_am"), sem("t_at"), sem("t_atr"), sem("t_v")
        x2_ready, st_ready, mv_ready = sem("t_x2"), sem("t_st"), sem("t_mv")

        places = [GR * (i % 4) + i // 4 for i in range(WIN)]
        order = [(p + HALF) % WIN for p in places]

        def starts(j):
            s0 = j if j < HALF else j - WIN
            return s0, s0 - (HALF - 1)

        def on_pool(i):
            return i % 3 == 2

        def nth(i):
            return sum(on_pool(k) == on_pool(i) for k in range(i + 1))

        def add(ns, eng, i):
            if i >= R:
                eng.wait_ge(e_done, (i - R) // 4 + 1)
            s0, t0 = starts(order[i])
            nc_out = hs[i % R][:, :].rearrange("p (g i) -> p g i", i=WIN)
            qv = qp[:, QL + t0:QL + t0 + SPAN].rearrange("p (g i) -> p g i", i=WIN)
            k0 = HALF + s0
            kv = kp[:, k0:k0 + SPAN - WIN + 1:WIN].rearrange("p (g a) -> p g a", a=1).to_broadcast([128, SPAN // WIN, WIN])
            ns.tensor_tensor(nc_out, qv, kv, ALU.add).then_inc(sum_ready[on_pool(i)], 1)

        with nc.Block() as block:
            @block.sync
            def _(sp):
                sp.dma_start(wt[:, :], inp["L1_attn_Wt"]).then_inc(load, 16)
                sp.dma_start(wx[:, :], inp["L1_attn_Wx"]).then_inc(load, 16)
                for b in range(B):
                    sp.dma_start(bh[32 * b:32 * b + 32, :], inp["L1_attn_bh"].rearrange("(u a) -> u a", a=1)).then_inc(load, 16)
                sp.dma_start(ba[:, :], inp["L1_attn_ba"].partition_broadcast(128)).then_inc(load, 16)
                sp.wait_ge(wa_clear, 1)
                for b in range(B):
                    sp.dma_start(wa[32 * b:32 * b + 32, b:b + 1], inp["L1_attn_Wa"]).then_inc(load_wa, 16)
                sp.wait_ge(cleared, 2)
                for b in range(B):
                    sp.wait_ge(xl_ready, 8 * b + 8)
                    sp.dma_start(xsh[HALF:128, b, 0:NTB, :], xl[0:128 - HALF, 8 * b:8 * b + 8, :]).then_inc(shifted, 16)
                    sp.dma_start(xsh[0:HALF, b, 1:NTB + 1, :], xl[128 - HALF:128, 8 * b:8 * b + 8, :]).then_inc(shifted, 16)

            @block.gpsimd
            def _(pool):
                nc.gpsimd.memset(wa[:, :], 0.0).then_inc(wa_clear, 1)
                nc.gpsimd.memset(wag[:, :, :], 0.0).then_inc(wa_clear, 1)
                nc.gpsimd.memset(xsh[:, :, 0, :], 0.0).then_inc(cleared, 1)
                nc.gpsimd.memset(xsh[:, :, NTB, :], 0.0).then_inc(cleared, 1)
                nc.gpsimd.memset(qp[:, :], 0.0).then_inc(cleared, 1)
                nc.gpsimd.memset(kp[:, :], 0.0).then_inc(cleared, 1)
                pool.wait_ge(load_wa, 16 * B)
                pool.wait_ge(wa_clear, 2)
                for r in range(GR):
                    m = nc.gpsimd.tensor_copy(wag[:, r, B * r:B * r + B], wa[:, :])
                m.then_inc(wag_ready, 1)
                pool.wait_ge(qk_ready, 2)
                for i in range(WIN):
                    if on_pool(i):
                        add(nc.gpsimd, pool, i)

            @block.scalar
            def _(act):
                act.wait_ge(ve, 1)
                nc.scalar.activation(std[:, :], std[:, :], ACT.Sqrt).then_inc(std_ready, 1)
                for g in range(NT // 4):
                    act.wait_ge(xl_turned, g + 1)
                    nc.scalar.copy(xlf[:, 512 * g:512 * g + 512], ps[g % 2][:, :]).then_inc(xlf_ready, 1)
                act.wait_ge(cleared, 4)
                act.wait_ge(load, 16 * 7)
                for h in range(2):
                    act.wait_ge(qk_done, 2 * h + 1)
                    nc.scalar.activation(qp[:, QL + 512 * h:QL + 512 * h + 512], ps[2 + h][:, :], ACT.Identity, bias=bh[:, 0:1])
                    act.wait_ge(qk_done, 2 * h + 2)
                    nc.scalar.copy(kp[:, HALF + 512 * h:HALF + 512 * h + 512], ps[4 + h][:, :]).then_inc(qk_ready, 1)
                for i in range(WIN):
                    act.wait_ge(sum_ready[on_pool(i)], nth(i))
                    t0 = -starts(order[i])[1]
                    nc.scalar.activation(hs[i % R][:, t0:t0 + S], hs[i % R][:, t0:t0 + S], ACT.Tanh).then_inc(tanh_ready, 1)
                act.wait_ge(e_done, GR)
                for h in range(2):
                    nc.scalar.copy(es[:, 512 * h:512 * h + 512], ps_e[:, 512 * h:512 * h + 512]).then_inc(es_ready, 1)
                act.wait_ge(soft, 3)
                nc.scalar.activation(e[:, :, :, :], e[:, :, :, :], ACT.Exp).then_inc(exp_ready, 1)
                for n in range(NTB):
                    act.wait_ge(at_done, n + 1)
                    if n >= 2:
                        act.wait_ge(v_done, n - 1)
                    nc.scalar.copy(at1[n % 2][:, :], ps[n % 2][:, :])
                    nc.scalar.copy(at2[n % 2][:, :], ps[2 + n % 2][0:32, :]).then_inc(at_ready, 1)

            @block.tensor
            def _(pe):
                ident = sb["cst"][:, C_ID:C_ID + 128]
                for g in range(NT // 4):
                    pe.wait_ge(xl_ready, 4 * g + 4)
                    if g >= 2:
                        pe.wait_ge(xlf_ready, g - 1)
                    for i in range(4):
                        m = nc.tensor.transpose(ps[g % 2][:, 128 * i:128 * i + 128], xl[:, 4 * g + i, :], ident)
                    m.then_inc(xl_turned, 1)
                pe.wait_ge(load, 16 * 7)
                pe.wait_ge(xlf_ready, NT // 4)
                for h in range(2):
                    for w, o in ((wt, 2), (wx, 4)):
                        for b in range(B):
                            m = nc.tensor.matmul(ps[o + h][32 * b:32 * b + 32, :], w[:, :], xlf[:, 1024 * b + 512 * h:1024 * b + 512 * h + 512],
                                                 start=True, stop=True)
                        m.then_inc(qk_done, 1)
                pe.wait_ge(wag_ready, 1)
                for r in range(GR):
                    pe.wait_ge(tanh_ready, 4 * r + 4)
                    for h in range(2):
                        for g in range(4):
                            i = 4 * r + g
                            t0 = -starts(order[i])[1] + 512 * h
                            m = nc.tensor.matmul(ps_e[32 * g:32 * g + 32, 512 * h:512 * h + 512], wag[:, r, :],
                                                 hs[i % R][:, t0:t0 + 512], start=r == 0, stop=r == GR - 1)
                    m.then_inc(e_done, 1)
                pe.wait_ge(es_ready, 2)
                for n in range(NTB):
                    m = nc.tensor.transpose(ps_e[:, 128 * n:128 * n + 128], es[:, 128 * n:128 * n + 128], ident)
                m.then_inc(et_done, 1)
                pe.wait_ge(shifted, 16 * 2 * B)
                pe.wait_ge(qk_ready, 2)
                for k in range(NTB + 1):
                    if k < NTB:
                        n = k
                        pe.wait_ge(am_ready, n + 1)
                        if n >= 2:
                            pe.wait_ge(at_ready, n - 1)
                        for b in range(B):
                            nc.tensor.transpose(ps[n % 2][:, 128 * b:128 * b + 128], am[n % 2][:, b, 0:128], ident)
                        for b in range(B):
                            m = nc.tensor.transpose(ps[2 + n % 2][0:32, 128 * b:128 * b + 128], am[n % 2][:, b, 128:160], ident)
                        m.then_inc(at_done, 1)
                    if k >= 1:
                        n = k - 1
                        pe.wait_ge(at_ready, n + 1)
                        if n >= 2:
                            pe.wait_ge(x2_ready, n - 1)
                        for b in range(B):
                            nc.tensor.matmul(ps[4 + n % 2][:, 128 * b:128 * b + 128], at1[n % 2][:, 128 * b:128 * b + 128],
                                             xsh[:, b, n, :], start=True, stop=False)
                            m = nc.tensor.matmul(ps[4 + n % 2][:, 128 * b:128 * b + 128], at2[n % 2][:, 128 * b:128 * b + 128],
                                                 xsh[0:32, b, n + 1, :], start=False, stop=True)
                        m.then_inc(v_done, 1)

            @block.vector
            def _(dve):
                mv = sb["mv"]
                nc.vector.tensor_scalar(std[:, :], mv[:, :, 1], 1e-5, None, ALU.add).then_inc(ve, 1)
                dve.wait_ge(std_ready, 1)
                nc.vector.reciprocal(rstd[:, :], std[:, :]).then_inc(rstd_ready, 1)
                dve.wait_ge(rstd_ready, 1)
                for n in range(NT):
                    nc.vector.tensor_scalar(xl[:, n, :], sb["x1"][:, n, :], mv[:, n, 0:1], rstd[:, n:n + 1],
                                            ALU.subtract, ALU.mult).then_inc(xl_ready, 1)
                dve.wait_ge(qk_ready, 2)
                for i in range(WIN):
                    if not on_pool(i):
                        add(nc.vector, dve, i)
                dve.wait_ge(et_done, 1)
                edge = sb["cst"][:, C_EDGE:C_EDGE + NTB * WIN].rearrange("p (n j) -> p n j", j=WIN)
                pe_ = ps_e[:, :].rearrange("p (n j b) -> p n b j", n=NTB, b=B)
                for b in range(B):
                    m = nc.vector.scalar_tensor_tensor(out=e[:, :, b, :], in0=pe_[:, :, b, :], scalar=ba[:, 0:1], in1=edge,
                                                       op0=ALU.add, op1=ALU.add)
                m.then_inc(soft, 1)
                dve.wait_ge(soft, 1)
                er = e[:, :, :, :].rearrange("p n b j -> p (n b) j")
                bc = mx[:, :].rearrange("p (n a) -> p n a", a=1).to_broadcast([128, NTB * B, WIN])
                nc.vector.tensor_reduce(mx[:, :], er, AX.X, ALU.max).then_inc(soft, 1)
                dve.wait_ge(soft, 2)
                nc.vector.tensor_tensor(er, er, bc, ALU.subtract).then_inc(soft, 1)
                dve.wait_ge(exp_ready, 1)
                nc.vector.tensor_reduce(mx[:, :], er, AX.X, ALU.add).then_inc(soft, 1)
                dve.wait_ge(soft, 4)
                nc.vector.reciprocal(mx[:, :], mx[:, :]).then_inc(soft, 1)
                dve.wait_ge(soft, 5)
                nc.vector.tensor_tensor(er, er, bc, ALU.mult).then_inc(soft, 1)
                dve.wait_ge(soft, 6)
                band = sb["cst"][:, C_BAND:C_BAND + 160].rearrange("p (r j) -> p r j", j=WIN)
                x1v = sb["x1"][:, :, :].rearrange("p (b n) f -> p b n f", b=B)
                for k in range(NTB + 3):
                    if k < NTB:
                        if k >= 2:
                            dve.wait_ge(at_done, k - 1)
                        for b in range(B):
                            m = nc.vector.tensor_tensor(am[k % 2][:, b, :].rearrange("p (r j) -> p r j", j=WIN),
                                                        e[:, k, b:b + 1, :].to_broadcast([128, 5, WIN]), band, ALU.mult)
                        m.then_inc(am_ready, 1)
                    if 2 <= k < NTB + 2:
                        n = k - 2
                        dve.wait_ge(v_done, n + 1)
                        nc.vector.tensor_tensor(x1v[:, :, n, :], ps[4 + n % 2][:, :].rearrange("p (b f) -> p b f", b=B),
                                                x1v[:, :, n, :], ALU.add).then_inc(x2_ready, 1)
                    if k >= 3:
                        n = k - 3
                        dve.wait_ge(x2_ready, n + 1)
                        for b in range(B):
                            m = nc.vector.bn_stats(bst[:, NTB * b + n, :], sb["x1"][:, NTB * b + n, :])
                        m.then_inc(st_ready, 1)
                        dve.wait_ge(st_ready, n + 1)
                        for b in range(B):
                            m = nc.vector.bn_aggr(mv[:, NTB * b + n, :], bst[:, NTB * b + n, :])
                        m.then_inc(mv_ready, 1)
                dve.wait_ge(mv_ready, NTB)


def experts(nc, st, sb, inp, out):
    sem = lambda name: st.enter_context(nc.semaphore(name))
    NH = H // 128
    with ExitStack() as ctx:
        def buf(name, shape, dt=F32):
            return ctx.enter_context(nc.sbuf_tensor("f_" + name, shape, dt))

        def split(name, shape):
            return [buf(name + part, shape, BF16) for part in ("_hi", "_lo")]

        std, r1, v2, s2, r12 = (buf(n, [128, NT]) for n in ("std", "r1", "v2", "s2", "r12"))
        xn = buf("xn", [128, 8, 128])
        xnf = buf("xnf", [128, NT * 128])
        wr, br = buf("wr", [128, E]), buf("br", [128, E])
        lg, key, sel, ex, lg2 = (buf(n, [128, NT, E]) for n in ("lg", "key", "sel", "ex", "lg2"))
        m1, mk = buf("m1", [128, NT]), buf("mk", [128, NT])
        wt8 = buf("wt8", [E, NT * 128])
        b2 = buf("b2", [E, 128])
        NROW = 2 * E + E * NH
        HB = NT * E
        rowp, colp = buf("rowp", [NROW, 128]), buf("colp", [128, NROW])
        lng, lnb, b1t = colp[:, 0:E], colp[:, E:2 * E], colp[:, 2 * E:NROW].rearrange("p (e h) -> p e h", h=NH)
        w1 = [buf(f"w1{i}", [128, H]) for i in range(2)]
        w1g = [buf(f"w1g{i}", [128, H]) for i in range(2)]
        w1s, w2s = [split(f"w1s{i}", [128, H]) for i in range(2)], [split(f"w2s{i}", [128, NH, 128]) for i in range(2)]
        xs = split("xs", [128, NT * 128])
        hs = [split(f"hs{i}", [128, NH, 512]) for i in range(2)]
        w2 = [buf(f"w2{i}", [128, NH, 128]) for i in range(2)]
        hb = [buf(f"hb{i}", [128, NH]) for i in range(2)]
        hh = [buf(f"hh{i}", [128, NH, 512]) for i in range(2)]
        PRODUCTS = ((0, 0), (0, 1), (1, 0))
        ps_h = [ctx.enter_context(nc.psum_tensor(f"fp_h{i}", [128, 512], F32)) for i in range(4)]
        ps_y = [ctx.enter_context(nc.psum_tensor(f"fp_y{i}", [128, 512], F32)) for i in range(2)]
        ps_r, ps_b = (ctx.enter_context(nc.psum_tensor("fp_" + n, [128, 512], F32)) for n in "rb")
        x_hi, x_lo, w_hi, w_lo, h_hi, h_lo = (sem("f_" + n) for n in ("xhi", "xlo", "whi", "wlo", "hhi", "hlo"))
        load, load_w, stored = sem("f_load"), [sem("f_lw0"), sem("f_lw1")], sem("f_out")
        nrm, sq1 = sem("f_nrm"), sem("f_sq")
        xn_ready, xn_turned, xnf_ready = sem("f_xn"), sem("f_turn"), sem("f_xnf")
        lg_done, rt, ex_ready = sem("f_lg"), sem("f_rt"), sem("f_ex")
        shares = sem("f_shares")
        wt_done, wt_ready, bt_done, bt_used = sem("f_wt"), sem("f_wtr"), sem("f_bt"), sem("f_btu")
        w_ready, hb_done, hb_ready = sem("f_w"), sem("f_hbd"), sem("f_hb")
        h_done, h_ready, y_done, y_used = sem("f_h"), sem("f_hr"), sem("f_y"), sem("f_yu")
        h_lo_first = sem("f_hlo0")
        col_done, col_ready = sem("f_cold"), sem("f_col")
        NCH = S * B // 512
        NN = E * NCH

        def split_done(engine, n):
            if n == 0:
                engine.wait_ge(h_lo_first, 2)
            else:
                engine.wait_ge(h_lo, 2 * n)

        with nc.Block() as block:
            @block.sync
            def _(sp):
                sp.dma_start(wr[:, :], inp["L1_ffn_Wr"]).then_inc(load, 16)
                sp.dma_start(br[:, :], inp["L1_ffn_br"].partition_broadcast(128)).then_inc(load, 16)
                sp.dma_start(b2[:, :], inp["L1_ffn_b2"]).then_inc(load, 16)
                sp.dma_start(rowp[0:E, :], inp["L1_ffn_ln_g"]).then_inc(load, 16)
                sp.dma_start(rowp[E:2 * E, :], inp["L1_ffn_ln_b"]).then_inc(load, 16)
                sp.dma_start(rowp[2 * E:NROW, :], inp["L1_ffn_b1"].rearrange("e (h p) -> (e h) p", p=128)).then_inc(load, 16)
                for e in range(E):
                    if e >= 2:
                        sp.wait_ge(w_lo, 2 * (e - 1))
                        sp.wait_ge(hb_done, e - 1)
                    sp.dma_start(w1[e % 2][:, :], inp["L1_ffn_W1"][e]).then_inc(load_w[e % 2], 16)
                    sp.dma_start(w2[e % 2][:, :, :], inp["L1_ffn_W2"][e].rearrange("(h p) d -> p h d", p=128)).then_inc(load_w[e % 2], 16)
                ov = out.rearrange("b t c d -> (b t c) d").rearrange("(n p) d -> p n d", p=128)
                for n in range(NCH):
                    sp.wait_ge(y_used, 4 * (NN - NCH + n + 1))
                    sp.dma_start(ov[:, 4 * n:4 * n + 4, :], sb["x1"][:, 4 * n:4 * n + 4, :]).then_inc(stored, 16)
                sp.wait_ge(stored, 16 * NCH)

            @block.scalar
            def _(act):
                act.wait_ge(nrm, 1)
                nc.scalar.activation(std[:, :], std[:, :], ACT.Sqrt).then_inc(sq1, 1)
                act.wait_ge(nrm, 5)
                nc.scalar.activation(s2[:, :], v2[:, :], ACT.Sqrt).then_inc(sq1, 1)
                for g in range(NT // 4):
                    act.wait_ge(xn_turned, g + 1)
                    nc.scalar.copy(xnf[:, 512 * g:512 * g + 512], ps_y[g % 2][:, :]).then_inc(xnf_ready, 1)
                    act.wait_ge(xnf_ready, g + 1)
                    nc.scalar.copy(xs[0][:, 512 * g:512 * g + 512], xnf[:, 512 * g:512 * g + 512]).then_inc(x_hi, 1)
                for n in range(NN):
                    e = n // NCH
                    act.wait_ge(hb_ready, e + 1)
                    if n >= 2:
                        split_done(act, n - 2)
                    for h in range(NH):
                        act.wait_ge(h_done, NH * n + h + 1)
                        nc.scalar.activation(hh[n % 2][:, h, :], ps_h[h][:, :], ACT.Gelu, bias=hb[e % 2][:, h:h + 1]).then_inc(h_ready, 1)
                    if n >= 2:
                        act.wait_ge(y_done, n - 1)
                    for a in range(2):
                        act.wait_ge(h_ready, NH * n + 2 * a + 2)
                        nc.scalar.copy(hs[n % 2][0][:, 2 * a:2 * a + 2, :], hh[n % 2][:, 2 * a:2 * a + 2, :]).then_inc(h_hi, 1)
                    if n == 0:
                        act.wait_ge(rt, 12)
                        nc.scalar.activation(ex[:, :, :], ex[:, :, :], ACT.Exp).then_inc(ex_ready, 1)
                    if 1 <= n <= NT // 4:
                        g = n - 1
                        act.wait_ge(wt_done, g + 1)
                        nc.scalar.copy(wt8[:, 512 * g:512 * g + 512], ps_r[0:E, :]).then_inc(wt_ready, 1)

            @block.gpsimd
            def _(pool):
                for e in range(E):
                    pool.wait_ge(w_ready, e + 1)
                    pool.wait_ge(load_w[e % 2], 32 * (e // 2 + 1))
                    if e >= 2:
                        pool.wait_ge(y_done, NCH * (e - 1))
                    for i, (w, ws) in enumerate(((w1g, w1s), (w2, w2s))):
                        w, (hi, lo) = w[e % 2], ws[e % 2]
                        w, hi, lo = (x[(slice(None),) * (2 + i)] for x in (w, hi, lo))
                        nc.gpsimd.tensor_copy(hi, w).then_inc(w_hi, 1)
                        pool.wait_ge(w_hi, 2 * e + i + 1)
                        nc.gpsimd.tensor_tensor(lo, w, hi, ALU.subtract).then_inc(w_lo, 1)
                    if e == 0:
                        for a in range(2):
                            pool.wait_ge(h_hi, a + 1)
                            nc.gpsimd.tensor_tensor(hs[0][1][:, 2 * a:2 * a + 2, :], hh[0][:, 2 * a:2 * a + 2, :],
                                                    hs[0][0][:, 2 * a:2 * a + 2, :], ALU.subtract).then_inc(h_lo_first, 1)

            @block.tensor
            def _(pe):
                ident = sb["cst"][:, C_ID:C_ID + 128]
                pe.wait_ge(load, 96)
                nc.tensor.transpose(ps_b[:, 0:NROW], rowp[:, :], ident[0:NROW, 0:NROW]).then_inc(col_done, 1)
                for g in range(NT // 4 + 1):
                    if g < NT // 4:
                        if g >= 2:
                            pe.wait_ge(xnf_ready, g - 1)
                        for i in range(4):
                            pe.wait_ge(xn_ready, 4 * g + i + 1)
                            m = nc.tensor.transpose(ps_y[g % 2][:, 128 * i:128 * i + 128], xn[:, 4 * (g % 2) + i, :], ident)
                        m.then_inc(xn_turned, 1)
                    if g >= 1:
                        pe.wait_ge(xnf_ready, g)
                        for n in range(4 * g - 4, 4 * g):
                            m = nc.tensor.matmul(ps_r[:, E * n:E * n + E], xnf[:, 128 * n:128 * n + 128], wr[:, :], start=True, stop=True)
                m.then_inc(lg_done, 1)

                def hidden_bias(e):
                    pe.wait_ge(load_w[e % 2], 32 * (e // 2 + 1))
                    pe.wait_ge(col_ready, 1)
                    for h in range(NH):
                        m = nc.tensor.matmul(ps_r[:, HB + h:HB + h + 1], w1[e % 2][:, 128 * h:128 * h + 128], lnb[:, e:e + 1], start=True, stop=True)
                    m.then_inc(hb_done, 1)

                def turn_weights(g):
                    pe.wait_ge(rt, 16)
                    if g >= 1:
                        pe.wait_ge(wt_ready, g)
                    for i in range(4):
                        m = nc.tensor.transpose(ps_r[0:E, 128 * i:128 * i + 128], sel[:, 4 * g + i, :], ident)
                    m.then_inc(wt_done, 1)

                def output_bias(g):
                    pe.wait_ge(wt_ready, g + 1)
                    if g >= 1:
                        pe.wait_ge(bt_used, g)
                    for i in range(4):
                        n = 4 * g + i
                        m = nc.tensor.matmul(ps_b[:, 128 * i:128 * i + 128], wt8[:, 128 * n:128 * n + 128], b2[:, :], start=True, stop=True)
                    m.then_inc(bt_done, 1)

                hidden_bias(0)
                for k in range(NN + 1):
                    if k < NN:
                        n, e = k, k // NCH
                        if n % NCH == 0 and e >= 1:
                            pe.wait_ge(hb_ready, e)
                            pe.wait_ge(wt_ready, min(NT // 4, NCH * e - 1))
                            hidden_bias(e)
                        pe.wait_ge(w_lo, 2 * e + 1)
                        if e == 0:
                            pe.wait_ge(x_lo, n + 1)
                        for h in range(NH):
                            if n >= 1:
                                pe.wait_ge(h_ready, NH * (n - 1) + h + 1)
                            for i, (a, c) in enumerate(PRODUCTS):
                                m = nc.tensor.matmul(ps_h[h][:, :], w1s[e % 2][a][:, 128 * h:128 * h + 128],
                                                     xs[c][:, 512 * (n % NCH):512 * (n % NCH) + 512], start=i == 0, stop=i == 2)
                            m.then_inc(h_done, 1)
                    if k >= 1:
                        n, e = k - 1, (k - 1) // NCH
                        pe.wait_ge(w_lo, 2 * e + 2)
                        split_done(pe, n)
                        if n >= 2:
                            pe.wait_ge(y_used, 4 * (n - 1))
                        for i in range(4):
                            for h in range(NH):
                                for j, (a, c) in enumerate(PRODUCTS):
                                    m = nc.tensor.matmul(ps_y[n % 2][:, 128 * i:128 * i + 128], hs[n % 2][a][:, h, 128 * i:128 * i + 128],
                                                         w2s[e % 2][c][:, h, :], start=(h, j) == (0, 0), stop=(h, j) == (NH - 1, 2))
                        m.then_inc(y_done, 1)
                    if 2 <= k < NT // 4 + 2:
                        output_bias(k - 2)
                    if 1 <= k <= NT // 4:
                        pe.wait_ge(hb_ready, k // NCH + 1)
                        turn_weights(k - 1)

            @block.vector
            def _(dve):
                mv = sb["mv"]

                def prepare_w(e):
                    if e >= 2:
                        dve.wait_ge(w_lo, 2 * (e - 1))
                    dve.wait_ge(load_w[e % 2], 32 * (e // 2 + 1))
                    nc.vector.tensor_scalar(w1g[e % 2][:, :], w1[e % 2][:, :], lng[:, e:e + 1], None, ALU.mult).then_inc(w_ready, 1)

                def prepare_b(e):
                    dve.wait_ge(hb_done, e + 1)
                    nc.vector.tensor_tensor(hb[e % 2][:, :], ps_r[:, HB:HB + NH], b1t[:, e, :], ALU.add).then_inc(hb_ready, 1)

                nc.vector.tensor_scalar(std[:, :], mv[:, :, 1], 1e-5, None, ALU.add).then_inc(nrm, 1)
                dve.wait_ge(sq1, 1)
                nc.vector.reciprocal(r1[:, :], std[:, :]).then_inc(nrm, 1)
                dve.wait_ge(nrm, 2)
                nc.vector.tensor_tensor(v2[:, :], r1[:, :], r1[:, :], ALU.mult).then_inc(nrm, 1)
                dve.wait_ge(nrm, 3)
                nc.vector.tensor_tensor(v2[:, :], v2[:, :], mv[:, :, 1], ALU.mult).then_inc(nrm, 1)
                dve.wait_ge(nrm, 4)
                nc.vector.tensor_scalar(v2[:, :], v2[:, :], 1e-5, None, ALU.add).then_inc(nrm, 1)
                dve.wait_ge(sq1, 2)
                nc.vector.reciprocal(r12[:, :], s2[:, :]).then_inc(nrm, 1)
                dve.wait_ge(nrm, 6)
                nc.vector.tensor_tensor(r12[:, :], r12[:, :], r1[:, :], ALU.mult).then_inc(nrm, 1)
                dve.wait_ge(nrm, 7)
                for n in range(NT):
                    if n >= 8 and n % 4 == 0:
                        dve.wait_ge(xn_turned, (n - 8) // 4 + 1)
                    nc.vector.tensor_scalar(xn[:, n % 8, :], sb["x1"][:, n, :], mv[:, n, 0:1], r12[:, n:n + 1],
                                            ALU.subtract, ALU.mult).then_inc(xn_ready, 1)
                dve.wait_ge(col_done, 1)
                nc.vector.tensor_copy(colp[:, :], ps_b[:, 0:NROW]).then_inc(col_ready, 1)
                dve.wait_ge(col_ready, 1)
                prepare_w(0)
                for g in range(NT // 4):
                    dve.wait_ge(x_hi, g + 1)
                    nc.vector.tensor_tensor(xs[1][:, 512 * g:512 * g + 512], xnf[:, 512 * g:512 * g + 512],
                                            xs[0][:, 512 * g:512 * g + 512], ALU.subtract).then_inc(x_lo, 1)
                prepare_b(0)
                step = [0]

                def link(i):
                    step[0] += 1
                    i.then_inc(rt, 1)
                    dve.wait_ge(rt, step[0])

                def per_tile(v):
                    return v.rearrange("p (n a) -> p n a", a=1).to_broadcast([128, NT, E])

                def per_expert(v):
                    return v.rearrange("p (a e) -> p a e", a=1).to_broadcast([128, NT, E])

                rank = per_expert(sb["cst"][:, C_RANK:C_RANK + E])
                dve.wait_ge(lg_done, 1)
                link(nc.vector.tensor_tensor(lg[:, :, :], ps_r[:, 0:NT * E].rearrange("p (n e) -> p n e", e=E), per_tile(s2[:, :]), ALU.mult))
                link(nc.vector.tensor_tensor(lg[:, :, :], lg[:, :, :], per_expert(br[:, :]), ALU.add))
                link(nc.vector.tensor_reduce(m1[:, :], lg[:, :, :], AX.X, ALU.max))
                link(nc.vector.tensor_tensor(key[:, :, :], lg[:, :, :], per_tile(m1[:, :]), ALU.is_ge))
                link(nc.vector.tensor_tensor(key[:, :, :], key[:, :, :], rank, ALU.mult))
                link(nc.vector.tensor_reduce(mk[:, :], key[:, :, :], AX.X, ALU.max))
                link(nc.vector.tensor_tensor(sel[:, :, :], key[:, :, :], per_tile(mk[:, :]), ALU.is_ge))
                link(nc.vector.scalar_tensor_tensor(out=lg2[:, :, :], in0=sel[:, :, :], scalar=-3.0e38, in1=lg[:, :, :],
                                                    op0=ALU.mult, op1=ALU.add))
                link(nc.vector.tensor_reduce(mk[:, :], lg2[:, :, :], AX.X, ALU.max))
                link(nc.vector.tensor_tensor(key[:, :, :], lg2[:, :, :], per_tile(mk[:, :]), ALU.is_ge))
                link(nc.vector.tensor_tensor(key[:, :, :], key[:, :, :], rank, ALU.mult))
                link(nc.vector.tensor_tensor(ex[:, :, :], lg[:, :, :], per_tile(m1[:, :]), ALU.subtract))
                link(nc.vector.tensor_reduce(mk[:, :], key[:, :, :], AX.X, ALU.max))
                link(nc.vector.tensor_tensor(key[:, :, :], key[:, :, :], per_tile(mk[:, :]), ALU.is_ge))
                link(nc.vector.tensor_tensor(sel[:, :, :], sel[:, :, :], key[:, :, :], ALU.add))
                dve.wait_ge(ex_ready, 1)
                nc.vector.tensor_tensor(ex[:, :, :], ex[:, :, :], sel[:, :, :], ALU.mult).then_inc(shares, 1)
                dve.wait_ge(shares, 1)
                nc.vector.tensor_reduce(m1[:, :], ex[:, :, :], AX.X, ALU.add).then_inc(shares, 1)
                dve.wait_ge(shares, 2)
                nc.vector.reciprocal(m1[:, :], m1[:, :]).then_inc(shares, 1)
                dve.wait_ge(shares, 3)
                nc.vector.tensor_tensor(sel[:, :, :], ex[:, :, :], per_tile(m1[:, :]), ALU.mult).then_inc(rt, 1)
                dve.wait_ge(rt, 16)

                for k in range(NN + 1):
                    if k % NCH == 0 and 0 < k < NN:
                        prepare_b(k // NCH)
                    if 3 <= k < NT // 4 + 3:
                        g = k - 3
                        dve.wait_ge(bt_done, g + 1)
                        dve.wait_ge(y_used, 4 * g + 4)
                        x = sb["x1"][:, 4 * g:4 * g + 4, :].rearrange("p n f -> p (n f)")
                        nc.vector.tensor_tensor(x, ps_b[:, :], x, ALU.add).then_inc(bt_used, 1)
                    if 0 < k < NN:
                        if k >= 2:
                            dve.wait_ge(y_done, k - 1)
                        for a in range(2):
                            dve.wait_ge(h_hi, 2 * k + a + 1)
                            nc.vector.tensor_tensor(hs[k % 2][1][:, 2 * a:2 * a + 2, :], hh[k % 2][:, 2 * a:2 * a + 2, :],
                                                    hs[k % 2][0][:, 2 * a:2 * a + 2, :], ALU.subtract).then_inc(h_lo, 1)
                    if k == 0:
                        continue
                    n = k - 1
                    e = n // NCH
                    if n % NCH == 1 and e + 1 < E:
                        prepare_w(e + 1)
                    if NCH <= n < 2 * NCH:
                        dve.wait_ge(bt_used, n - NCH + 1)
                    dve.wait_ge(y_done, n + 1)
                    if n >= NCH:
                        dve.wait_ge(y_used, 4 * (n - NCH + 1))
                    for i in range(4):
                        j = 4 * (n % NCH) + i
                        nc.vector.scalar_tensor_tensor(out=sb["x1"][:, j, :], in0=ps_y[n % 2][:, 128 * i:128 * i + 128],
                                                       scalar=sel[:, j, e:e + 1], in1=sb["x1"][:, j, :],
                                                       op0=ALU.mult, op1=ALU.add).then_inc(y_used, 1)


def build(nc, inp, consts, out):
    with ExitStack() as st:
        sb = {}

        def alloc(name, shape, dt=F32, stack=st):
            sb[name] = stack.enter_context(nc.sbuf_tensor("s_" + name, shape, dt))

        alloc("cst", [128, C_ALL])
        alloc("x1", [128, NT, 128])
        alloc("mv", [128, NT, 2])
        sb["load_xb"] = st.enter_context(nc.semaphore("load_xb"))
        mem = st.enter_context(ExitStack())
        alloc("qf", [128, B, T, C], stack=mem)
        for k in ("10", "20", "11", "21"):
            alloc("w" + k, [128, B, 256], stack=mem)
            alloc("first" + k, [128, 256], stack=mem)
        steps = mem.enter_context(ExitStack())
        alloc("kf", [128, T + 1, 128], stack=steps)
        alloc("vs", [128, T, 128], stack=steps)
        alloc("ktok", [128, T, 128], stack=steps)
        alloc("coef", [128, T, 9], stack=steps)
        prepare(nc, st, sb, inp, consts)
        learn(nc, st, sb)
        steps.close()
        read_out(nc, st, sb, inp)
        mem.close()
        attend(nc, st, sb, inp)
        experts(nc, st, sb, inp, out)


_INS = ['x', 'L0_conv_Wq', 'L0_conv_Wk', 'L0_conv_Wv', 'L0_conv_w_lr', 'L0_conv_w_forget', 'L0_conv_w_eta',
        'L0_conv_w1_0', 'L0_conv_w2_0', 'L0_conv_w1_1', 'L0_conv_w2_1', 'L1_attn_Wt', 'L1_attn_Wx', 'L1_attn_bh',
        'L1_attn_Wa', 'L1_attn_ba', 'L1_ffn_Wr', 'L1_ffn_br', 'L1_ffn_ln_g', 'L1_ffn_ln_b', 'L1_ffn_W1', 'L1_ffn_b1',
        'L1_ffn_W2', 'L1_ffn_b2']


def shape_constants():
    import numpy as np
    c = np.zeros((128, C_ALL), np.float32)
    p = np.arange(128)
    c[:, C_ID:C_ID + 128] = np.eye(128)
    c[:, C_MEAN:C_MEAN + 128] = (p[:, None] // C == p[None] // C) / C
    c[:, C_GRP:C_GRP + 128] = (p[:, None] // 4 == p[None] // 4) / 4
    w = np.arange(128 + WIN)
    c[:, C_BAND:C_BAND + 128 + WIN] = (w[None] >= p[:, None]) & (w[None] < p[:, None] + WIN)
    for n in range(S // 128):
        for j in range(WIN):
            key = 128 * n - WIN // 2 + p + (j - p) % WIN
            c[:, C_EDGE + WIN * n + j] = np.where((key < 0) | (key >= S), -10000.0, 0.0)
    c[:, C_RANK:C_RANK + E] = E - np.arange(E)
    for b in range(B):
        c[:, C_SEL + 128 * b:C_SEL + 128 * b + 128] = (p[:, None] // C == b) / C
    return c


def kernel(**inputs):
    import numpy as _np
    import concourse.bacc as _bacc
    from concourse import mybir as _mybir
    from concourse.bass_utils import run_bass_kernel_spmd as _run

    nc = _bacc.Bacc("TRN2", target_bir_lowering=False, num_devices=1)
    arrays, aps = {}, {}
    for name in _INS:
        a = _np.ascontiguousarray(inputs[name])
        arrays[f"in_{name}_dram"] = a
        aps[name] = nc.dram_tensor(f"in_{name}_dram", a.shape, _mybir.dt.from_np(a.dtype), kind="ExternalInput").ap()
    c = shape_constants()
    arrays["in_constants_dram"] = c
    consts = nc.dram_tensor("in_constants_dram", c.shape, _mybir.dt.float32, kind="ExternalInput").ap()
    out = nc.dram_tensor("out_0_dram", (B, T, C, D), _mybir.dt.float32, kind="ExternalOutput").ap()
    build(nc, aps, consts, out)
    r = _run(nc, [arrays], core_ids=[0])
    return r.results[0]["out_0_dram"]
```
